# Optimizing a Trainium2 kernel written in Bass

```python
import numpy as np
import jax
import jax.numpy as jnp

def _softmax(x, axis=-1):
    return jax.nn.softmax(x, axis=axis)

def _gelu(x):
    return jax.nn.gelu(x, approximate=True)

def _silu(x):
    return jax.nn.silu(x)

def _sigmoid(x):
    return jax.nn.sigmoid(x)

def _layernorm(x, axis=-1, eps=1e-05):
    m = jnp.mean(x, axis=axis, keepdims=True)
    v = jnp.var(x, axis=axis, keepdims=True)
    return (x - m) / jnp.sqrt(v + eps)

def _scatter_add(tgt, idx, src, axis=0):
    return tgt.at[idx].add(src)

def _segment_sum(src, seg, n):
    return jax.ops.segment_sum(src, seg, n)
kernel_name = 'mk_recurrent_d1_jaxref_r4_c8fdad'

def setup_inputs(seed: int=0):
    np.random.seed(seed)
    _w = jnp.asarray

    def _L0_attn_setup():
        import jax, jax.numpy as jnp
        import numpy as np
        N_HEADS = 16
        ROPE_BASE = 10000.0

        def _rope(x):
            B, L, H, Dh = x.shape
            half = Dh // 2
            inv_freq = 1.0 / ROPE_BASE ** (jnp.arange(0, half, dtype=jnp.float32) / half)
            ang = jnp.arange(L, dtype=jnp.float32)[:, None] * inv_freq[None, :]
            cos = jnp.concatenate([jnp.cos(ang), jnp.cos(ang)], axis=-1).astype(x.dtype)
            sin = jnp.concatenate([jnp.sin(ang), jnp.sin(ang)], axis=-1).astype(x.dtype)
            cos = cos[None, :, None, :]
            sin = sin[None, :, None, :]
            x1, x2 = (x[..., :half], x[..., half:])
            rot = jnp.concatenate([-x2, x1], axis=-1)
            return x * cos + rot * sin
        key = jax.random.key(seed)
        k1, k2, k3 = jax.random.split(key, 3)
        B, L, D = (2, 512, 256)
        x = jax.random.normal(k1, (B, L, D), dtype=jnp.float32)
        w_qkv = jax.random.normal(k2, (3 * D, D), dtype=jnp.float32) * D ** (-0.5)
        w_out = jax.random.normal(k3, (D, D), dtype=jnp.float32) * D ** (-0.5)
        return {'x': x, 'w_qkv': w_qkv, 'w_out': w_out}
    _L0_attn_in = _L0_attn_setup()

    def _L0_ffn_setup():
        import jax, jax.numpy as jnp
        import numpy as np
        DIM = 256
        DEPTH = 2
        HEADS = 8
        DIM_HEAD = 64
        WINDOW = 128
        INNER = HEADS * DIM_HEAD
        HID = int(DIM * 4 * 2 / 3)
        B, N = (2, 2048)
        QK_SCALE = 8.0

        def shift_token(t):
            t1, t2 = jnp.split(t, 2, axis=-1)
            t2 = jnp.pad(t2, ((0, 0), (1, 0), (0, 0)))[:, :-1]
            return jnp.concatenate([t1, t2], axis=-1)

        def l2norm(t):
            return t / jnp.clip(jnp.linalg.norm(t, axis=-1, keepdims=True), 1e-12)

        def rotate_half(x):
            x1, x2 = jnp.split(x, 2, axis=-1)
            return jnp.concatenate([-x2, x1], axis=-1)

        def rotary_xpos(q, k):
            n = q.shape[-2]
            half_idx = jnp.arange(0, DIM_HEAD, 2, dtype=jnp.float32)
            inv_freq = 1.0 / 10000.0 ** (half_idx / DIM_HEAD)
            t = jnp.arange(n, dtype=jnp.float32)
            freqs = t[:, None] * inv_freq[None, :]
            freqs = jnp.concatenate([freqs, freqs], axis=-1)
            base = (half_idx + 0.4 * DIM_HEAD) / (1.4 * DIM_HEAD)
            power = (t - n // 2) / float(WINDOW // 2)
            scale = base[None, :] ** power[:, None]
            scale = jnp.concatenate([scale, scale], axis=-1)
            cos, sin = (jnp.cos(freqs), jnp.sin(freqs))
            q = q * cos * scale + rotate_half(q) * sin * scale
            k = k * cos / scale + rotate_half(k) * sin / scale
            return (q, k)

        def local_attention(q, k, v):
            b, h, n, d = q.shape
            w = n // WINDOW
            bq = q.reshape(b, h, w, WINDOW, d) * QK_SCALE
            bk = k.reshape(b, h, w, WINDOW, d)
            bv = v.reshape(b, h, w, WINDOW, d)

            def look_around(t):
                p = jnp.pad(t, ((0, 0), (0, 0), (1, 0), (0, 0), (0, 0)))
                return jnp.concatenate([p[:, :, :w], p[:, :, 1:]], axis=3)
            bk, bv = (look_around(bk), look_around(bv))
            bt = jnp.arange(n).reshape(w, WINDOW)
            btp = jnp.pad(bt, ((1, 0), (0, 0)), constant_values=-1)
            btk = jnp.concatenate([btp[:w], btp[1:]], axis=1)
            sim = jnp.einsum('bhwid,bhwjd->bhwij', bq, bk)
            i = bt[:, :, None]
            j = btk[:, None, :]
            mask = (i < j) | (i > j + WINDOW) | (j == -1)
            sim = jnp.where(mask, -jnp.finfo(sim.dtype).max, sim)
            attn = jax.nn.softmax(sim, axis=-1)
            out = jnp.einsum('bhwij,bhwjd->bhwid', attn, bv)
            return out.reshape(b, h, n, d)

        def _layer(x, wqkv, qs, ksc, wo, lg, lb, w1, b1, w2, b2):
            b, n, _ = x.shape
            h = shift_token(x)
            qkv = h @ wqkv
            q, k, v = jnp.split(qkv, 3, axis=-1)
            to_heads = lambda t: t.reshape(b, n, HEADS, DIM_HEAD).transpose(0, 2, 1, 3)
            q, k, v = (to_heads(q), to_heads(k), to_heads(v))
            q = l2norm(q) * qs
            k = l2norm(k) * ksc
            q, k = rotary_xpos(q, k)
            o = local_attention(q, k, v)
            o = o.transpose(0, 2, 1, 3).reshape(b, n, INNER)
            x = x + o @ wo
            h = shift_token(x)
            mu = h.mean(-1, keepdims=True)
            var = h.var(-1, keepdims=True)
            h = (h - mu) / jnp.sqrt(var + 1e-05) * lg + lb
            h = h @ w1 + b1
            a, g = jnp.split(h, 2, axis=-1)
            h = a * jax.nn.gelu(g, approximate=False)
            x = x + h @ w2 + b2
            return x
        key = jax.random.key(seed)
        ks = jax.random.split(key, 6)
        return {'x': jax.random.normal(ks[0], (B, N, DIM), jnp.float32), 'wqkv': jax.random.normal(ks[1], (DEPTH, DIM, 3 * INNER), jnp.float32) * 0.02, 'q_scale': jnp.ones((DEPTH, DIM_HEAD), jnp.float32), 'k_scale': jnp.ones((DEPTH, DIM_HEAD), jnp.float32), 'wo': jax.random.normal(ks[2], (DEPTH, INNER, DIM), jnp.float32) * 0.02, 'ln_g': jnp.ones((DEPTH, DIM), jnp.float32), 'ln_b': jnp.zeros((DEPTH, DIM), jnp.float32), 'w1': jax.random.normal(ks[3], (DEPTH, DIM, 2 * HID), jnp.float32) * 0.02, 'b1': jnp.zeros((DEPTH, 2 * HID), jnp.float32), 'w2': jax.random.normal(ks[4], (DEPTH, HID, DIM), jnp.float32) * 0.02, 'b2': jnp.zeros((DEPTH, DIM), jnp.float32)}
    _L0_ffn_in = _L0_ffn_setup()
    _d = {'L0_attn_x': _L0_attn_in['x'], 'L0_attn_w_qkv': _L0_attn_in['w_qkv'], 'L0_attn_w_out': _L0_attn_in['w_out'], 'L0_ffn_wqkv': _L0_ffn_in['wqkv'], 'L0_ffn_q_scale': _L0_ffn_in['q_scale'], 'L0_ffn_k_scale': _L0_ffn_in['k_scale'], 'L0_ffn_wo': _L0_ffn_in['wo'], 'L0_ffn_ln_g': _L0_ffn_in['ln_g'], 'L0_ffn_ln_b': _L0_ffn_in['ln_b'], 'L0_ffn_w1': _L0_ffn_in['w1'], 'L0_ffn_b1': _L0_ffn_in['b1'], 'L0_ffn_w2': _L0_ffn_in['w2'], 'L0_ffn_b2': _L0_ffn_in['b2']}
    _x0 = _d['L0_attn_x']
    _d['L0_attn_x'] = jax.random.normal(jax.random.fold_in(jax.random.key(seed), 1), (4, 1024, 256), dtype=_x0.dtype)
    del _x0
    return _d

def reference(L0_attn_x, L0_attn_w_qkv, L0_attn_w_out, L0_ffn_wqkv, L0_ffn_q_scale, L0_ffn_k_scale, L0_ffn_wo, L0_ffn_ln_g, L0_ffn_ln_b, L0_ffn_w1, L0_ffn_b1, L0_ffn_w2, L0_ffn_b2):

    def _L0_attn_ref(x, w_qkv, w_out):
        import jax, jax.numpy as jnp
        import numpy as np
        N_HEADS = 16
        ROPE_BASE = 10000.0

        def _rope(x):
            B, L, H, Dh = x.shape
            half = Dh // 2
            inv_freq = 1.0 / ROPE_BASE ** (jnp.arange(0, half, dtype=jnp.float32) / half)
            ang = jnp.arange(L, dtype=jnp.float32)[:, None] * inv_freq[None, :]
            cos = jnp.concatenate([jnp.cos(ang), jnp.cos(ang)], axis=-1).astype(x.dtype)
            sin = jnp.concatenate([jnp.sin(ang), jnp.sin(ang)], axis=-1).astype(x.dtype)
            cos = cos[None, :, None, :]
            sin = sin[None, :, None, :]
            x1, x2 = (x[..., :half], x[..., half:])
            rot = jnp.concatenate([-x2, x1], axis=-1)
            return x * cos + rot * sin
        B, L, D = x.shape
        H = N_HEADS
        Dh = D // H
        qkv = jnp.einsum('bld,ed->ble', x, w_qkv)
        q, k, v = jnp.split(qkv, 3, axis=-1)
        q = q.reshape(B, L, H, Dh)
        k = k.reshape(B, L, H, Dh)
        v = v.reshape(B, L, H, Dh)
        q = _rope(q)
        k = _rope(k)
        scale = 1.0 / jnp.sqrt(jnp.asarray(Dh, dtype=x.dtype))
        scores = jnp.einsum('blhd,bmhd->bhlm', q, k) * scale
        attn = jax.nn.softmax(scores, axis=-1)
        out = jnp.einsum('bhlm,bmhd->blhd', attn, v).reshape(B, L, D)
        return jnp.einsum('bld,ed->ble', out, w_out)

    def _L0_ffn_ref(x, wqkv, q_scale, k_scale, wo, ln_g, ln_b, w1, b1, w2, b2):
        import jax, jax.numpy as jnp
        import numpy as np
        DIM = 256
        DEPTH = 2
        HEADS = 8
        DIM_HEAD = 64
        WINDOW = 128
        INNER = HEADS * DIM_HEAD
        HID = int(DIM * 4 * 2 / 3)
        B, N = (2, 2048)
        QK_SCALE = 8.0

        def shift_token(t):
            t1, t2 = jnp.split(t, 2, axis=-1)
            t2 = jnp.pad(t2, ((0, 0), (1, 0), (0, 0)))[:, :-1]
            return jnp.concatenate([t1, t2], axis=-1)

        def l2norm(t):
            return t / jnp.clip(jnp.linalg.norm(t, axis=-1, keepdims=True), 1e-12)

        def rotate_half(x):
            x1, x2 = jnp.split(x, 2, axis=-1)
            return jnp.concatenate([-x2, x1], axis=-1)

        def rotary_xpos(q, k):
            n = q.shape[-2]
            half_idx = jnp.arange(0, DIM_HEAD, 2, dtype=jnp.float32)
            inv_freq = 1.0 / 10000.0 ** (half_idx / DIM_HEAD)
            t = jnp.arange(n, dtype=jnp.float32)
            freqs = t[:, None] * inv_freq[None, :]
            freqs = jnp.concatenate([freqs, freqs], axis=-1)
            base = (half_idx + 0.4 * DIM_HEAD) / (1.4 * DIM_HEAD)
            power = (t - n // 2) / float(WINDOW // 2)
            scale = base[None, :] ** power[:, None]
            scale = jnp.concatenate([scale, scale], axis=-1)
            cos, sin = (jnp.cos(freqs), jnp.sin(freqs))
            q = q * cos * scale + rotate_half(q) * sin * scale
            k = k * cos / scale + rotate_half(k) * sin / scale
            return (q, k)

        def local_attention(q, k, v):
            b, h, n, d = q.shape
            w = n // WINDOW
            bq = q.reshape(b, h, w, WINDOW, d) * QK_SCALE
            bk = k.reshape(b, h, w, WINDOW, d)
            bv = v.reshape(b, h, w, WINDOW, d)

            def look_around(t):
                p = jnp.pad(t, ((0, 0), (0, 0), (1, 0), (0, 0), (0, 0)))
                return jnp.concatenate([p[:, :, :w], p[:, :, 1:]], axis=3)
            bk, bv = (look_around(bk), look_around(bv))
            bt = jnp.arange(n).reshape(w, WINDOW)
            btp = jnp.pad(bt, ((1, 0), (0, 0)), constant_values=-1)
            btk = jnp.concatenate([btp[:w], btp[1:]], axis=1)
            sim = jnp.einsum('bhwid,bhwjd->bhwij', bq, bk)
            i = bt[:, :, None]
            j = btk[:, None, :]
            mask = (i < j) | (i > j + WINDOW) | (j == -1)
            sim = jnp.where(mask, -jnp.finfo(sim.dtype).max, sim)
            attn = jax.nn.softmax(sim, axis=-1)
            out = jnp.einsum('bhwij,bhwjd->bhwid', attn, bv)
            return out.reshape(b, h, n, d)

        def _layer(x, wqkv, qs, ksc, wo, lg, lb, w1, b1, w2, b2):
            b, n, _ = x.shape
            h = shift_token(x)
            qkv = h @ wqkv
            q, k, v = jnp.split(qkv, 3, axis=-1)
            to_heads = lambda t: t.reshape(b, n, HEADS, DIM_HEAD).transpose(0, 2, 1, 3)
            q, k, v = (to_heads(q), to_heads(k), to_heads(v))
            q = l2norm(q) * qs
            k = l2norm(k) * ksc
            q, k = rotary_xpos(q, k)
            o = local_attention(q, k, v)
            o = o.transpose(0, 2, 1, 3).reshape(b, n, INNER)
            x = x + o @ wo
            h = shift_token(x)
            mu = h.mean(-1, keepdims=True)
            var = h.var(-1, keepdims=True)
            h = (h - mu) / jnp.sqrt(var + 1e-05) * lg + lb
            h = h @ w1 + b1
            a, g = jnp.split(h, 2, axis=-1)
            h = a * jax.nn.gelu(g, approximate=False)
            x = x + h @ w2 + b2
            return x
        for l in range(DEPTH):
            x = _layer(x, wqkv[l], q_scale[l], k_scale[l], wo[l], ln_g[l], ln_b[l], w1[l], b1[l], w2[l], b2[l])
        return x
    x = L0_attn_x
    xn = _layernorm(x, axis=-1)
    s = _L0_attn_ref(xn, L0_attn_w_qkv, L0_attn_w_out)
    g = _silu(_L0_ffn_ref(xn, L0_ffn_wqkv, L0_ffn_q_scale, L0_ffn_k_scale, L0_ffn_wo, L0_ffn_ln_g, L0_ffn_ln_b, L0_ffn_w1, L0_ffn_b1, L0_ffn_w2, L0_ffn_b2))
    x = x + s * g
    return x

_drawn_inputs = setup_inputs


def setup_inputs(seed=0):
    import zlib

    import numpy as np

    out = dict(_drawn_inputs(seed))
    spreads = {'L0_ffn_q_scale': (1.0, 0.6),
     'L0_ffn_k_scale': (1.0, 0.6),
     'L0_ffn_ln_g': (1.0, 0.6),
     'L0_ffn_ln_b': (0.0, 0.8),
     'L0_ffn_b1': (0.0, 0.8),
     'L0_ffn_b2': (0.0, 1.361)}
    factors = {'L0_ffn_wqkv': 8.0, 'L0_ffn_wo': 8.0, 'L0_ffn_w1': 7.016, 'L0_ffn_w2': 7.05}
    for name, (base, spread) in spreads.items():
        noise = np.random.default_rng([zlib.crc32(name.encode()), seed]).standard_normal(out[name].shape)
        drawn = base * np.exp(spread * noise) if base else spread * noise
        out[name] = jnp.asarray(drawn.astype(out[name].dtype))
    for name, factor in factors.items():
        out[name] = (out[name] * factor).astype(out[name].dtype)
    return out
```

```python
from contextlib import ExitStack

import numpy as np
import concourse.bass as bass
from concourse import mybir

F32 = mybir.dt.float32
F32R = mybir.dt.float32r
ALU = mybir.AluOpType
ACT = mybir.ActivationFunctionType
AX_X = mybir.AxisListType.X

P = 128
B, L, D = 4, 1024, 256
KD = D // P
TILES = L // P
G_HEADS, G_DIM = 16, 16
UNITS = B * G_HEADS // 2
SPLIT = 4 * G_DIM
CH = 512
EPS = 1e-5
STORES = 4 * KD + KD


def flat(ap):
    return ap.rearrange("o p n -> (o p) n")


def apart(eng, passed):
    eng.sem_inc(passed, 1)


def prepare_tokens(nc, x, wqkv_t, rope, ident_in, xnt, qs_dram, ks_dram, v_dram):
    with ExitStack() as ctx:
        sb = lambda n, s, d=F32: ctx.enter_context(nc.sbuf_tensor(n, s, d))
        ps = lambda n, s: ctx.enter_context(nc.psum_tensor(n, s, F32))
        sem = lambda n: ctx.enter_context(nc.semaphore(n))

        ident = sb("a_ident", [P, P])
        wqkv = sb("a_wqkv", [P, KD, 3 * D])
        table = sb("a_rope", [P, TILES, 2, G_DIM])
        x_in = sb("x_in", [P, 2, 4, D])
        stats = sb("stats", [P, 2, 4, 6])
        moments = sb("moments", [P, 2, 4, 2])
        half = sb("half", [P, 4])
        rstd = sb("rstd", [P, 2, 4])
        xn = sb("xn", [P, 2, 4, D])
        xs = sb("xs", [P, 2, KD, CH])
        roped = sb("roped", [P, 2, 2 * D])
        turned = sb("turned", [P, 2, 2 * D])
        qkr = sb("qkr", [P, 2, 2 * D])
        split = sb("split", [P, 2, 4, 2, CH], F32R)
        v_sb = sb("v_sb", [P, 2, 4, D])

        ps_x = [ps(f"ps_x{k}", [P, CH]) for k in range(KD)]
        ps_qk = [ps(f"ps_qk{k}", [P, CH]) for k in range(2)]
        ps_v = [ps(f"ps_v{k}", [P, CH]) for k in range(2)]
        ps_t = [ps(f"ps_t{k}", [P, CH]) for k in range(2)]

        dve_passed, pool_passed = sem("a_dve_passed"), sem("a_pool_passed")
        consts_in = sem("consts_in")
        x_loaded = [sem(f"x_loaded{c}") for c in range(2)]
        half_set = sem("half_set")
        stats_done = sem("stats_done")
        moments_done = sem("moments_done")
        eps_added = sem("eps_added")
        rstd_done = sem("rstd_done")
        xn_done = sem("xn_done")
        x_turned = sem("x_turned")
        xs_done = sem("xs_done")
        xnt_done = sem("xnt_done")
        qk_mm = sem("qk_mm")
        v_mm = sem("v_mm")
        v_copied = sem("v_copied")
        rope_cos = sem("rope_cos")
        rope_sin = sem("rope_sin")
        rope_sum = sem("rope_sum")
        qk_turned = sem("qk_turned")
        high_done = sem("high_done")
        low_done = sem("low_done")
        stored = [sem(f"stored{c}") for c in range(2)]

        with nc.Block() as block:

            @block.sync
            def _(sp):
                sp.dma_start(ident[:, :], ident_in).then_inc(consts_in, 16)
                sp.dma_start(wqkv[:, :, :], wqkv_t.rearrange("(k p) n -> p k n", p=P)).then_inc(consts_in, 16)
                sp.dma_start(table[:, :, :, :], rope.rearrange("(t p) s n -> p t s n", p=P)).then_inc(consts_in, 16)

                def load(i, c):
                    src = x[bass.ds(i, 1), c * CH:(c + 1) * CH, :].rearrange("o (t p) n -> p (o t) n", p=P)
                    sp.dma_start(x_in[:, c, :, :], src).then_inc(x_loaded[c], 16)

                def store(i, c):
                    sp.wait_ge(low_done, 8 * i + 4 * c + 4)
                    for part, dram in ((0, qs_dram), (1, ks_dram)):
                        for f in range(KD):
                            for s in range(2):
                                dst = dram[bass.ds(2 * i + f, 1), :, s, :, c * CH:(c + 1) * CH].rearrange("o h d n -> (o h) d n")
                                sp.dma_start(dst, split[:, c, 2 * part + f, s, :].bitcast(F32)).then_inc(stored[c], 16)
                    sp.wait_ge(v_copied, 8 * i + 4 * c + 4)
                    for f in range(KD):
                        dst = v_dram[bass.ds(2 * i + f, 1), c * 4:c * 4 + 4, :, :].rearrange("o t p n -> p (o t) n")
                        sp.dma_start(dst, v_sb[:, c, :, f * P:(f + 1) * P]).then_inc(stored[c], 16)

                load(0, 0)
                load(0, 1)
                with sp.Fori(0, B - 1) as i:
                    for c in range(2):
                        sp.wait_ge(xn_done, 8 * i + 4 * c + 4)
                        load(i + 1, c)
                    for c in range(2):
                        store(i, c)
                for c in range(2):
                    store(B - 1, c)
                for c in range(2):
                    sp.wait_ge(stored[c], B * STORES * 16)

            @block.gpsimd
            def _(pool):
                nc.gpsimd.memset(half[:, :], -0.5).then_inc(half_set, 1)
                nc.gpsimd.memset(xnt[:, :, :, 0:1], 0.0).then_inc(half_set, 1)
                pool.wait_ge(half_set, 2)

                def inverse_deviation(i, c):
                    pool.wait_ge(moments_done, 8 * i + 4 * c + 4)
                    apart(pool, pool_passed)
                    nc.gpsimd.tensor_scalar(rstd[:, c, :], moments[:, c, :, 1], EPS, None, ALU.add).then_inc(eps_added, 1)
                    pool.wait_ge(eps_added, 2 * i + c + 1)
                    nc.gpsimd.tensor_tensor(rstd[:, c, :], rstd[:, c, :], half[:, :], ALU.pow).then_inc(rstd_done, 1)

                def body(i, last):
                    for c in range(2):
                        pool.wait_ge(xs_done, 4 * i + 2 * c + 2)
                        apart(pool, pool_passed)
                        for k in range(KD):
                            nc.gpsimd.tensor_copy(xnt[:, k, bass.ds(2 * i + c, 1), 1:].rearrange("p o n -> p (o n)"),
                                                  xs[:, c, k, :]).then_inc(xnt_done, 1)
                        if c == 0:
                            nc.gpsimd.tensor_copy(xnt[:, :, bass.ds(2 * i + 1, 1), 0:1].rearrange("p k o n -> p k (o n)"),
                                                  xs[:, 0, :, CH - 1:]).then_inc(xnt_done, 1)
                        for t in range(4 * c, 4 * c + 4):
                            pool.wait_ge(rope_sin, 8 * i + t + 1)
                            if t >= 2:
                                pool.wait_ge(qk_turned, 8 * i + t - 1)
                            elif not isinstance(i, int) or i:
                                pool.wait_ge(qk_turned, 8 * i + t - 1)
                            nc.gpsimd.tensor_tensor(qkr[:, t % 2, :], roped[:, t % 2, :], turned[:, t % 2, :],
                                                    ALU.add).then_inc(rope_sum, 1)
                            if not last and t in (1, 4):
                                inverse_deviation(i + 1, t // 4)

                inverse_deviation(0, 0)
                inverse_deviation(0, 1)
                body(0, False)
                with pool.Fori(1, B - 1) as i:
                    body(i, False)
                body(B - 1, True)

            @block.vector
            def _(dve):
                def normalise(i, c):
                    dve.wait_ge(x_loaded[c], 16 * i + 16)
                    for t in range(4):
                        nc.vector.bn_stats(stats[:, c, t, :], x_in[:, c, t, :]).then_inc(stats_done, 1)
                    dve.wait_ge(stats_done, 8 * i + 4 * c + 4)
                    apart(dve, dve_passed)
                    for t in range(4):
                        nc.vector.bn_aggr(moments[:, c, t, :], stats[:, c, t, :]).then_inc(moments_done, 1)

                def scale(i, c, before):
                    dve.wait_ge(rstd_done, 2 * i + c + 1)
                    if before:
                        dve.wait_ge(x_turned, 4 * i + 2 * c - 2)
                    for t in range(4):
                        nc.vector.tensor_scalar(xn[:, c, t, :], x_in[:, c, t, :], moments[:, c, t, 0:1],
                                                rstd[:, c, t:t + 1], ALU.subtract, ALU.mult).then_inc(xn_done, 1)

                def rotate(i, t, first):
                    dve.wait_ge(qk_mm, 8 * i + t + 1)
                    if t >= 2 or not first:
                        dve.wait_ge(rope_sum, 8 * i + t - 1)
                    src = ps_qk[t % 2][:, :].rearrange("p (h n) -> p h n", n=G_DIM)
                    cos = table[:, t, 0, :].rearrange("p (o n) -> p o n", o=1).broadcast_to([P, 2 * G_HEADS, G_DIM])
                    sin = table[:, t, 1, :].rearrange("p (o n) -> p o n", o=1)
                    a = roped[:, t % 2, :].rearrange("p (h n) -> p h n", n=G_DIM)
                    r = turned[:, t % 2, :].rearrange("p (h n) -> p h n", n=G_DIM)
                    hd = G_DIM // 2
                    nc.vector.tensor_tensor(a, src, cos, ALU.mult)
                    nc.vector.tensor_tensor(r[:, :, 0:hd], src[:, :, hd:], sin[:, :, 0:hd].broadcast_to([P, 2 * G_HEADS, hd]), ALU.mult)
                    nc.vector.tensor_tensor(r[:, :, hd:], src[:, :, 0:hd], sin[:, :, hd:].broadcast_to([P, 2 * G_HEADS, hd]),
                                            ALU.mult).then_inc(rope_sin, 1)

                def low(i, t):
                    dve.wait_ge(high_done, 8 * i + t + 1)
                    c, s = t // 4, slice((t % 4) * P, (t % 4 + 1) * P)
                    nc.vector.tensor_tensor(split[:, c, :, 1, s], ps_t[t % 2][:, :].rearrange("p (f n) -> p f n", f=4),
                                            split[:, c, :, 0, s], ALU.subtract).then_inc(low_done, 1)

                def body(i, first, last):
                    for t in range(TILES):
                        rotate(i, t, first)
                        if t:
                            low(i, t - 1)
                        if not last and t in (1, 4):
                            normalise(i + 1, t // 4)
                        if not last and t in (3, 6):
                            scale(i + 1, t // 4, True)
                    low(i, TILES - 1)

                dve.wait_ge(consts_in, 48)
                normalise(0, 0)
                normalise(0, 1)
                scale(0, 0, False)
                scale(0, 1, False)
                body(0, True, False)
                with dve.Fori(1, B - 1) as i:
                    body(i, False, False)
                body(B - 1, False, True)

            @block.scalar
            def _(act):
                def take_x(i, c, first):
                    if not first:
                        act.wait_ge(xnt_done, 5 * i + 2 * c - 2)
                        act.wait_ge(v_mm, 8 * i + 4 * c - 4)
                    act.wait_ge(x_turned, 2 * (2 * i + c) + 2)
                    for k in range(KD):
                        nc.scalar.copy(xs[:, c, k, :], ps_x[k][:, :]).then_inc(xs_done, 1)

                def body(i, first):
                    take_x(i, 0, first)
                    for t in range(TILES):
                        c = t // 4
                        if t % 4 == 0 and not first:
                            act.wait_ge(stored[c], 16 * STORES * i)
                        act.wait_ge(v_mm, 8 * i + t + 1)
                        nc.scalar.copy(v_sb[:, c, t % 4, :], ps_v[t % 2][:, 0:D]).then_inc(v_copied, 1)
                        if t == 2:
                            take_x(i, 1, first)
                        act.wait_ge(qk_turned, 8 * i + t + 1)
                        nc.scalar.copy(split[:, c, :, 0, (t % 4) * P:(t % 4 + 1) * P],
                                       ps_t[t % 2][:, :].rearrange("p (f n) -> p f n", f=4)).then_inc(high_done, 1)

                body(0, True)
                with act.Fori(1, B) as i:
                    body(i, False)

            @block.tensor
            def _(pe):
                def turn_x(i, c, first):
                    pe.wait_ge(xn_done, 8 * i + 4 * c + 4)
                    if c or not first:
                        pe.wait_ge(xs_done, 4 * i + 2 * c)
                    for k in range(KD):
                        for t in range(4):
                            mm = nc.tensor.transpose(ps_x[k][:, t * P:(t + 1) * P], xn[:, c, t, k * P:(k + 1) * P], ident[:, :])
                        mm.then_inc(x_turned, 1)

                def project(i, t, first):
                    c, s = t // 4, slice((t % 4) * P, (t % 4 + 1) * P)
                    if t % 4 == 0:
                        pe.wait_ge(xs_done, 4 * i + 2 * c + 2)
                    if t >= 2 or not first:
                        pe.wait_ge(rope_sin, 8 * i + t - 1)
                        pe.wait_ge(v_copied, 8 * i + t - 1)
                    for k in range(KD):
                        mm = nc.tensor.matmul(ps_qk[t % 2][:, :], xs[:, c, k, s], wqkv[:, k, 0:2 * D], start=(k == 0), stop=(k == KD - 1))
                    mm.then_inc(qk_mm, 1)
                    for k in range(KD):
                        mm = nc.tensor.matmul(ps_v[t % 2][:, 0:D], xs[:, c, k, s], wqkv[:, k, 2 * D:], start=(k == 0), stop=(k == KD - 1))
                    mm.then_inc(v_mm, 1)

                def turn_qk(i, t, first):
                    pe.wait_ge(rope_sum, 8 * i + t + 1)
                    if t >= 2 or not first:
                        pe.wait_ge(low_done, 8 * i + t - 1)
                    for f in range(4):
                        mm = nc.tensor.transpose(ps_t[t % 2][:, f * P:(f + 1) * P], qkr[:, t % 2, f * P:(f + 1) * P], ident[:, :])
                    mm.then_inc(qk_turned, 1)

                def body(i, first):
                    turn_x(i, 0, first)
                    for t in range(TILES):
                        project(i, t, first)
                        if t == 2:
                            turn_x(i, 1, first)
                        if t:
                            turn_qk(i, t - 1, first)
                    turn_qk(i, TILES - 1, first)

                pe.wait_ge(consts_in, 48)
                body(0, True)
                with pe.Fori(1, B) as i:
                    body(i, False)


def global_attention(nc, ident_in, qs_dram, ks_dram, v_dram, o_dram):
    with ExitStack() as ctx:
        sb = lambda n, s, d=F32: ctx.enter_context(nc.sbuf_tensor(n, s, d))
        ps = lambda n, s: ctx.enter_context(nc.psum_tensor(n, s, F32))
        sem = lambda n: ctx.enter_context(nc.semaphore(n))

        NB = 4
        ROWS = SPLIT + 2
        PADDED = 96
        ident = sb("g_ident", [P, P])
        q_st = [[sb(f"q_st{u}{j}", [PADDED, L], F32R) for j in range(2)] for u in range(NB)]
        k_st = [[sb(f"k_st{u}{j}", [PADDED, L], F32R) for j in range(2)] for u in range(NB)]
        v_in = sb("v_in", [P, TILES, P])
        v_st = sb("v_st", [P, TILES, 2 * NB, 2 * G_DIM])
        probs = sb("probs", [P, 4, 2, L])
        maxima = sb("maxima", [P, 2, 2, TILES, 2])
        neg_max = sb("neg_max", [P, 2, TILES])
        neg_hl = sb("neg_hl", [P, 2, 2, TILES], F32R)
        max_rows = sb("max_rows", [4 * TILES, P])
        o_sb = sb("o_sb", [P, 2, CH])

        ps_st = [ps(f"ps_st{j}", [P, L]) for j in range(2)]
        ps_m = [ps(f"ps_m{k}", [P, CH]) for k in range(3)]
        ps_o = ps("ps_o", [P, CH])

        pool_passed = sem("g_pool_passed")
        ident_loaded = sem("g_ident_loaded")
        ones_set = sem("ones_set")
        qk_in = [sem(f"qk_in{u}") for u in range(NB)]
        v_loaded = sem("v_loaded")
        v_placed = sem("v_placed")
        rows_zeroed = sem("rows_zeroed")
        m_ready = sem("m_ready")
        m_used = sem("m_used")
        max_found = sem("max_found")
        neg_high = sem("neg_high")
        neg_done = sem("neg_done")
        rows_out = sem("rows_out")
        rows_in = [sem(f"rows_in{u}") for u in range(NB)]
        st_ready = sem("st_ready")
        exp_done = sem("exp_done")
        pv_done = sem("pv_done")
        o_copied = sem("o_copied")
        o_stored = [sem(f"o_stored{c}") for c in range(2)]

        HALF = 2 * TILES
        USES = 2 * HALF + 1
        LEAD = USES + HALF
        ITERS = UNITS // NB

        def bank(base, k):
            start = base % 3 if isinstance(base, int) else LEAD % 3
            return ps_m[(start + k) % 3]


        with nc.Block() as block:

            @block.sync
            def _(sp):
                def load(i, u):
                    for j in range(2):
                        head = 2 * u + j
                        src = qs_dram[bass.ds(i, 1), head, :, :, :].rearrange("o s d n -> (o s d) n")
                        sp.dma_start(q_st[u][j][0:SPLIT, :].bitcast(F32),
                                     src.unsqueeze(0).broadcast_to([2, 2 * G_DIM, L])).then_inc(qk_in[u], 16)
                        for s in range(2):
                            src = ks_dram[bass.ds(i, 1), head, s, :, :].rearrange("o d n -> (o d) n")
                            sp.dma_start(k_st[u][j][2 * s * G_DIM:2 * (s + 1) * G_DIM, :].bitcast(F32),
                                         src.unsqueeze(0).broadcast_to([2, G_DIM, L])).then_inc(qk_in[u], 16)

                def load_v(i):
                    sp.dma_start(v_in[:, :, :], v_dram[bass.ds(i, 1), :, :, :].rearrange("o t p n -> p (o t) n")).then_inc(v_loaded, 16)

                def place_rows(i, u):
                    sp.wait_ge(rows_out, NB * i + u + 1)
                    for j in range(2):
                        sp.dma_start(q_st[u][j][SPLIT:ROWS, :].bitcast(F32),
                                     max_rows[j * 2 * TILES:(j + 1) * 2 * TILES, :]).then_inc(rows_in[u], 16)

                def store_o(i, u):
                    sp.wait_ge(o_copied, NB * i + u + 1)
                    dst = o_dram[bass.ds(NB * i + u, 1), :, :].rearrange("o p n -> (o p) n")
                    sp.dma_start(dst, o_sb[:, u % 2, :]).then_inc(o_stored[u % 2], 16)

                def body(i, first, last):
                    for u in range(NB):
                        if u:
                            store_o(i, u - 1)
                        elif not first:
                            store_o(i - 1, NB - 1)
                        if u < NB - 1:
                            place_rows(i, u + 1)
                        elif not last:
                            place_rows(i + 1, 0)
                        if not last:
                            if u == 0:
                                sp.wait_ge(v_placed, i + 1)
                                load_v(i + 1)
                            sp.wait_ge(st_ready, 2 * TILES * (NB * i + u) + 2 * TILES)
                            load(i + 1, u)
                    if last:
                        store_o(i, NB - 1)

                sp.dma_start(ident[:, :], ident_in).then_inc(ident_loaded, 16)
                for u in range(NB):
                    load(0, u)
                load_v(0)
                place_rows(0, 0)
                body(0, True, False)
                with sp.Fori(1, ITERS - 1) as i:
                    body(i, False, False)
                body(ITERS - 1, False, True)
                for c in range(2):
                    sp.wait_ge(o_stored[c], UNITS // 2 * 16)

            @block.gpsimd
            def _(pool):
                for u in range(NB):
                    for j in range(2):
                        nc.gpsimd.memset(k_st[u][j][SPLIT:PADDED, :].bitcast(F32), 1.0).then_inc(ones_set, 1)
                pool.wait_ge(ones_set, 2 * NB)
                for cols in (slice(0, 1), slice(1 + G_DIM, 2 * G_DIM)):
                    nc.gpsimd.memset(v_st[:, :, :, cols], 1.0).then_inc(ones_set, 1)

                def zero_rows(u, end):
                    for j in range(2):
                        nc.gpsimd.memset(q_st[u][j][SPLIT:end, :].bitcast(F32), 0.0).then_inc(rows_zeroed, 1)

                def place_v(i):
                    pool.wait_ge(v_loaded, 16 * i + 16)
                    pool.wait_ge(rows_zeroed, 2 * NB * (i + 1))
                    apart(pool, pool_passed)
                    nc.gpsimd.tensor_copy(v_st[:, :, :, 1:1 + G_DIM], v_in[:, :, :].rearrange("p t (e n) -> p t e n", n=G_DIM)).then_inc(v_placed, 1)

                def body(i, last):
                    pool.wait_ge(v_placed, i + 1)
                    for u in range(NB):
                        pool.wait_ge(st_ready, 2 * TILES * (NB * i + u) + 2 * TILES)
                        apart(pool, pool_passed)
                        zero_rows(u, ROWS)
                    pool.wait_ge(pv_done, TILES * NB * (i + 1))
                    place_v(i + 1)

                pool.wait_ge(ones_set, 2 * NB + 2)
                for u in range(NB):
                    zero_rows(u, PADDED)
                place_v(0)
                with pool.Fori(0, ITERS - 1) as i:
                    body(i, False)

            @block.tensor
            def _(pe):
                def maxima_scores(base, k, i, u, qt, j):
                    for h in range(2):
                        use = k + h
                        if isinstance(base, int):
                            if base + use >= 3:
                                pe.wait_ge(m_used, base + use - 2)
                        else:
                            pe.wait_ge(m_used, base + use - 2)
                        nc.tensor.matmul(bank(base, use)[:, :], q_st[u][j][:, qt * P:(qt + 1) * P],
                                         k_st[u][j][:, h * CH:(h + 1) * CH], start=True, stop=True).then_inc(m_ready, 1)

                def half_maxima(base, k, i, u, half, step):
                    if half == 0 and step == 0:
                        pe.wait_ge(qk_in[u], 96 * i + 96)
                        pe.wait_ge(rows_zeroed, 2 * (NB * i + u) + 2)
                    for j in range(2):
                        maxima_scores(base, k + 4 * step + 2 * j, i, u, 4 * half + step, j)

                def turn_maxima(base, k, i, u):
                    pe.wait_ge(neg_done, NB * i + u + 1)
                    pe.wait_ge(m_used, base + k - 2)
                    nc.tensor.transpose(bank(base, k)[0:4 * TILES, 0:P], neg_hl[:, :, :, :].rearrange("p a b c -> p (a b c)").bitcast(F32),
                                        ident[:, :]).then_inc(m_ready, 1)

                def scores(n, kt, u, j):
                    g = 2 * TILES * n + 2 * kt + j
                    if not isinstance(n, int) or g >= 2:
                        pe.wait_ge(exp_done, g - 1)
                    for h in range(2):
                        mm = nc.tensor.matmul(ps_st[j][:, h * CH:(h + 1) * CH], k_st[u][j][:, kt * P:(kt + 1) * P],
                                              q_st[u][j][:, h * CH:(h + 1) * CH], start=True, stop=True)
                    mm.then_inc(st_ready, 1)

                def product(n, kt, u):
                    pe.wait_ge(exp_done, 2 * TILES * n + 2 * kt + 2)
                    if kt == 0 and (not isinstance(n, int) or n):
                        pe.wait_ge(o_copied, n)
                    for j in range(2):
                        for h in range(2):
                            r = 32 * (2 * j + h)
                            mm = nc.tensor.matmul(ps_o[r:r + 32, :], v_st[:, kt, 2 * u + j, :],
                                                  probs[:, kt % 4, j, h * CH:(h + 1) * CH], start=(kt == 0), stop=(kt == TILES - 1))
                    mm.then_inc(pv_done, 1)

                def body(i, first, last):
                    for u in range(NB):
                        n = NB * i + u
                        base = LEAD + USES * n
                        i1, u1 = (i, u + 1) if u + 1 < NB else (i + 1, 0)
                        i2, u2 = (i, u + 2) if u + 2 < NB else (i + 1, u + 2 - NB)
                        more1, more2 = not last or u + 1 < NB, not last or u + 2 < NB
                        pe.wait_ge(rows_in[u], 32 * i + 32)
                        for kt in range(TILES):
                            for j in range(2):
                                scores(n, kt, u, j)
                            if kt < 4 and more1:
                                half_maxima(base, 0, i1, u1, 1, kt)
                            if kt == 4 and more1:
                                turn_maxima(base, HALF, i1, u1)
                            if kt >= 4 and more2:
                                half_maxima(base, HALF + 1, i2, u2, 0, kt - 4)
                            if kt:
                                product(n, kt - 1, u)
                            elif u:
                                product(n - 1, TILES - 1, u - 1)
                            elif not first:
                                product(n - 1, TILES - 1, NB - 1)
                            if kt == 0 and u == 0:
                                pe.wait_ge(v_placed, i + 1)
                        if last and u == NB - 1:
                            product(n, TILES - 1, u)

                pe.wait_ge(ident_loaded, 16)
                pe.wait_ge(ones_set, 2 * NB + 2)
                for half in range(2):
                    for step in range(4):
                        half_maxima(0, HALF * half, 0, 0, half, step)
                turn_maxima(0, 2 * HALF, 0, 0)
                for step in range(4):
                    half_maxima(0, USES, 0, 1, 0, step)
                body(0, True, False)
                with pe.Fori(1, ITERS - 1) as i:
                    body(i, False, False)
                body(ITERS - 1, False, True)

            @block.vector
            def _(dve):
                def half_maxima(base, k, n, half):
                    for step in range(4):
                        for j in range(2):
                            for h in range(2):
                                use = k + 4 * step + 2 * j + h
                                dve.wait_ge(m_ready, base + use + 1)
                                nc.vector.tensor_reduce(maxima[:, n, j, 4 * half + step, h:h + 1], bank(base, use)[:, :],
                                                        AX_X, ALU.max).then_inc(m_used, 1)

                def negate(base, k, count, par):
                    dve.wait_ge(m_used, base + k)
                    nc.vector.tensor_reduce(neg_max[:, :, :], maxima[:, par, :, :, :], AX_X, ALU.max, negate=True).then_inc(max_found, 1)
                    dve.wait_ge(max_found, count)
                    nc.vector.tensor_copy(neg_hl[:, :, 0, :], neg_max[:, :, :]).then_inc(neg_high, 1)
                    dve.wait_ge(neg_high, count)
                    nc.vector.tensor_tensor(neg_hl[:, :, 1, :], neg_max[:, :, :], neg_hl[:, :, 0, :], ALU.subtract).then_inc(neg_done, 1)

                def rows(base, k, i, u, first):
                    dve.wait_ge(m_ready, base + k + 1)
                    if u:
                        dve.wait_ge(rows_in[u - 1], 32 * i + 32)
                    elif not first:
                        dve.wait_ge(rows_in[NB - 1], 32 * i)
                    nc.vector.tensor_copy(max_rows[:, :], bank(base, k)[0:4 * TILES, 0:P]).then_inc(m_used, 1)
                    dve.wait_ge(m_used, base + k + 1)
                    dve.sem_inc(rows_out, 1)

                def body(i, first, last):
                    for u in range(NB):
                        n = NB * i + u
                        base = LEAD + USES * n
                        i1, u1 = (i, u + 1) if u + 1 < NB else (i + 1, 0)
                        if not last or u + 1 < NB:
                            half_maxima(base, 0, (u + 1) % 2, 1)
                            negate(base, HALF, n + 2, (u + 1) % 2)
                        if not last or u + 1 < NB:
                            rows(base, HALF, i1, u1, False)
                        if not last or u + 2 < NB:
                            half_maxima(base, HALF + 1, u % 2, 0)

                half_maxima(0, 0, 0, 0)
                half_maxima(0, HALF, 0, 1)
                negate(0, 2 * HALF, 1, 0)
                rows(0, 2 * HALF, 0, 0, True)
                half_maxima(0, USES, 1, 0)
                body(0, True, False)
                with dve.Fori(1, ITERS - 1) as i:
                    body(i, False, False)
                body(ITERS - 1, False, True)

            @block.scalar
            def _(act):
                def copy_o(n, i, u):
                    act.wait_ge(pv_done, TILES * (n + 1))
                    if not isinstance(i, int) or 2 * i + u // 2:
                        act.wait_ge(o_stored[u % 2], 16 * (2 * i + u // 2))
                    nc.scalar.copy(o_sb[:, u % 2, :], ps_o[:, :]).then_inc(o_copied, 1)

                def body(i, first, last):
                    for u in range(NB):
                        n = NB * i + u
                        for kt in range(TILES):
                            for j in range(2):
                                act.wait_ge(st_ready, 2 * TILES * n + 2 * kt + j + 1)
                                if not isinstance(n, int) or TILES * n + kt >= 4:
                                    act.wait_ge(pv_done, TILES * n + kt - 3)
                                nc.scalar.activation(probs[:, kt % 4, j, :], ps_st[j][:, :], ACT.Exp,
                                                     scale=float(G_DIM) ** -0.5).then_inc(exp_done, 1)
                            if kt == 0:
                                if u:
                                    copy_o(n - 1, i, u - 1)
                                elif not first:
                                    copy_o(n - 1, i - 1, NB - 1)
                    if last:
                        copy_o(NB * i + NB - 1, i, NB - 1)

                body(0, True, False)
                with act.Fori(1, ITERS - 1) as i:
                    body(i, False, False)
                body(ITERS - 1, False, True)


DEPTH = 2
HEADS, HDIM = 8, 64
INNER = HEADS * HDIM
HID = int(D * 4 * 2 / 3)
CHUNKS = B * L // CH
WPC = CH // P
WINDOWS = CHUNKS * WPC
FT = HID // P
TAIL = HID - FT * P
TAIL_AT = 64
LAST = DEPTH * CHUNKS
QK_SCALE = 8.0
MASKED = -3.0e38


class Weights:

    def __init__(self, ctx, nc):
        sb = lambda n, s: ctx.enter_context(nc.sbuf_tensor(n, s, F32))
        per = lambda n, s: [sb(f"{n}{l}", s) for l in range(DEPTH)]
        self.wqkv = per("wqkv_l", [P, KD, 3 * INNER])
        self.wo = per("wo_l", [P, INNER // P, D])
        self.w1 = per("w1_l", [P, KD, (2 * FT + 1) * P])
        self.w2 = per("w2_l", [P, FT + 1, D])
        self.tables = per("tables_l", [P, TILES, 4, HDIM])
        self.lnp = per("lnp_l", [P, 2, KD])
        self.b1 = per("b1_l", [P, 2, FT + 1])
        self.b2 = per("b2_l", [P, KD])
        self.mask = sb("l_mask", [P, 4, P])
        self.ident = sb("l_ident", [P, P])
        self.mean_w = sb("mean_w", [P, P])
        self.parity = sb("parity", [P, 2])


def load_weights(nc, wt, wqkv, q_scale, k_scale, wo, ln_g, ln_b, w1, b1, w2, b2, xpos, mask_in, ident_in):
    with ExitStack() as ctx:
        sb = lambda n, s: ctx.enter_context(nc.sbuf_tensor(n, s, F32))
        sem = lambda n: ctx.enter_context(nc.semaphore(n))
        base = sb("xpos_in", [P, TILES, 4, HDIM])
        scales = sb("scales_in", [P, DEPTH, 2, HDIM])
        zeroed = sem("w_zeroed")
        loaded = sem("w_loaded")
        scaled = sem("w_scaled")
        LOADS = 6 + DEPTH * 19
        with nc.Block() as block:

            @block.vector
            def _(dve):
                for l in range(DEPTH):
                    nc.vector.memset(wt.w1[l][:, :, 2 * FT * P:], 0.0).then_inc(zeroed, 1)
                    nc.vector.memset(wt.w2[l][:, FT, :], 0.0).then_inc(zeroed, 1)
                    nc.vector.memset(wt.b1[l][:, :, FT:], 0.0).then_inc(zeroed, 1)
                nc.vector.memset(wt.mean_w[:, :], 1.0 / D).then_inc(zeroed, 1)
                nc.vector.memset(wt.parity[:, 0:1], 0.0).then_inc(zeroed, 1)
                nc.vector.memset(wt.parity[:, 1:2], 1.0).then_inc(zeroed, 1)
                dve.wait_ge(loaded, LOADS * 16)
                hd = HDIM // 2
                for l in range(DEPTH):
                    for s in range(2):
                        sc = scales[:, l, s, :].rearrange("p (o n) -> p o n", o=1)
                        for t in range(2):
                            out, src = wt.tables[l][:, :, 2 * s + t, :], base[:, :, 2 * s + t, :]
                            if t == 0:
                                nc.vector.tensor_tensor(out, src, sc.broadcast_to([P, TILES, HDIM]), ALU.mult).then_inc(scaled, 1)
                            else:
                                for a in range(2):
                                    o, i = slice(a * hd, (a + 1) * hd), slice((1 - a) * hd, (2 - a) * hd)
                                    nc.vector.tensor_tensor(out[:, :, o], src[:, :, o], sc[:, :, i].broadcast_to([P, TILES, hd]),
                                                            ALU.mult).then_inc(scaled, 1)

            @block.sync
            def _(sp):
                sp.wait_ge(zeroed, 3 * DEPTH + 3)
                n = [0]

                def get(dst, src):
                    sp.dma_start(dst, src).then_inc(loaded, 16)
                    n[0] += 1

                get(wt.ident[:, :], ident_in)
                get(wt.mask[:, 0:2, :], mask_in[0:2].rearrange("s p n -> p s n"))
                get(wt.mask[:, 3, :], mask_in[2])
                get(base[:, :, :, :], xpos.rearrange("(t p) s n -> p t s n", p=P))
                get(scales[:, :, 0, :], q_scale.unsqueeze(0).broadcast_to([P, DEPTH, HDIM]))
                get(scales[:, :, 1, :], k_scale.unsqueeze(0).broadcast_to([P, DEPTH, HDIM]))
                for l in range(DEPTH):
                    get(wt.wqkv[l][:, :, :], wqkv[l].rearrange("(k p) n -> p k n", p=P))
                    get(wt.wo[l][:, :, :], wo[l].rearrange("(k p) n -> p k n", p=P))
                    for k in range(KD):
                        rows = w1[l, k * P:(k + 1) * P, :]
                        get(wt.w1[l][:, k, 0:FT * P], rows[:, HID:HID + FT * P])
                        get(wt.w1[l][:, k, FT * P:2 * FT * P], rows[:, 0:FT * P])
                        get(wt.w1[l][:, k, 2 * FT * P:2 * FT * P + TAIL], rows[:, HID + FT * P:])
                        get(wt.w1[l][:, k, 2 * FT * P + TAIL_AT:2 * FT * P + TAIL_AT + TAIL], rows[:, FT * P:HID])
                    get(wt.w2[l][:, 0:FT, :], w2[l, 0:FT * P, :].rearrange("(k p) n -> p k n", p=P))
                    get(wt.w2[l][TAIL_AT:TAIL_AT + TAIL, FT, :], w2[l, FT * P:, :])
                    with nc.allow_non_contiguous_dma(reason="a bias has one element for a partition"):
                        get(wt.b1[l][:, 0, 0:FT], b1[l, 0:FT * P].rearrange("(k p) -> p k", p=P))
                        get(wt.b1[l][:, 1, 0:FT], b1[l, HID:HID + FT * P].rearrange("(k p) -> p k", p=P))
                        get(wt.b1[l][TAIL_AT:TAIL_AT + TAIL, 0, FT:FT + 1], b1[l, FT * P:HID].rearrange("(p o) -> p o", o=1))
                        get(wt.b1[l][0:TAIL, 1, FT:FT + 1], b1[l, HID + FT * P:].rearrange("(p o) -> p o", o=1))
                        get(wt.b2[l][:, :], b2[l].rearrange("(k p) -> p k", p=P))
                        get(wt.lnp[l][:, 0, :], ln_g[l].rearrange("(k p) -> p k", p=P))
                        get(wt.lnp[l][:, 1, :], ln_b[l].rearrange("(k p) -> p k", p=P))
                assert n[0] == LOADS, n
                sp.wait_ge(loaded, n[0] * 16)


def local_layers(nc, wt, xnt):
    with ExitStack() as ctx:
        sb = lambda n, s: ctx.enter_context(nc.sbuf_tensor(n, s, F32))
        ps = lambda n: ctx.enter_context(nc.psum_tensor(n, [P, CH], F32))
        sem = lambda n: ctx.enter_context(nc.semaphore(n))

        h = sb("h", [P, KD, CH])
        v_ring = sb("v_ring", [P, WPC, INNER])
        k_ring = sb("k_ring", [P, HEADS // 2, WPC * P])
        q_pad = [sb(f"q_pad{j}", [P, HEADS // 2, P]) for j in range(2)]
        rope_a = sb("rope_a", [P, 2, INNER])
        rope_b = sb("rope_b", [P, 2, INNER])
        qk_n = sb("qk_n", [P, 2, INNER])
        sumsq = sb("sumsq", [P, 2 * HEADS])
        clipped = sb("clipped", [P, 2 * HEADS])
        halves = sb("halves", [P, 2 * HEADS])
        inv_norm = sb("inv_norm", [P, 2 * HEADS])
        probs = sb("l_probs", [P, HEADS, 2 * P])
        neg_max = sb("l_neg_max", [P, HEADS])
        total = sb("l_total", [P, HEADS])
        inv_total = sb("l_inv_total", [P, HEADS])
        p_turned = sb("p_turned", [P, 2, 2, 2, P])
        o_ring = sb("o_ring", [P, 2, HEADS // 2, CH])
        mid = sb("mid", [P, KD, 1 + CH])
        centred = sb("centred", [P, KD, CH])
        dev = sb("dev", [P, CH])
        gate = sb("gate", [P, 2, CH])
        hidden = sb("hidden", [P, FT + 1, CH])
        eps_col = sb("eps_col", [P, 1])

        ps_q, ps_k, ps_v, ps_o = ps("ps_q"), ps("ps_k"), ps("ps_v"), ps("l_ps_o")
        ring = [ps(f"ring{b}") for b in range(2)]
        ffn = [ps(f"ffn{b}") for b in range(2)]

        dve_passed, pool_passed = sem("l_dve_passed"), sem("l_pool_passed")
        cleared = sem("cleared")
        mask_picked = sem("mask_picked")
        h_ready = sem("h_ready")
        q_mm, k_mm, v_mm = sem("q_mm"), sem("k_mm"), sem("l_v_mm")
        squared = sem("squared")
        v_out = sem("v_out")
        cos_done = sem("cos_done")
        sums_done = sem("sums_done")
        roped = sem("l_roped")
        clip_done = sem("clip_done")
        inv_done = sem("inv_done")
        added = sem("added")
        qk_ready = sem("qk_ready")
        ring_ready = [sem(f"ring_ready{b}") for b in range(2)]
        ring_taken = [sem(f"ring_taken{b}") for b in range(2)]
        exp_done = sem("l_exp_done")
        inv_total_done = sem("inv_total_done")
        p_ready = sem("p_ready")
        pv_mm = sem("pv_mm")
        o_out = sem("o_out")
        ffn_ready = [sem(f"ffn_ready{b}") for b in range(2)]
        ffn_taken = [sem(f"ffn_taken{b}") for b in range(2)]
        carried = sem("carried")
        sq_dev = sem("sq_dev")
        ln_done = sem("ln_done")
        dev_done = sem("dev_done")
        scaled = sem("l_scaled")
        normed = sem("normed")
        tail_gated = sem("tail_gated")
        x_out = sem("x_out")

        PT, TQ, TK, SC = 0, 4, 5, 6

        def ring_use(W, r):
            return 5 * W - 7 + r // 2

        USES = (9, 8)
        WO, MEAN, GATE, W2 = 0, 1, 2, 7
        TAILS = 7

        def plan(body):
            yield 0, 0, None
            yield 1, 0, None
            yield 2, 0, 0
            yield (3, CHUNKS), 0, 0
            yield (CHUNKS, CHUNKS + 2), 1, 0
            yield (CHUNKS + 2, LAST), 1, 1
            yield LAST, None, 1
            yield LAST + 1, None, 1

        def run(eng, body):
            for g, la, lf in plan(body):
                if isinstance(g, int):
                    body(g, la, lf)
                else:
                    with eng.Fori(*g) as i:
                        body(i, la, lf)

        def parts(g, w):
            if not isinstance(g, int):
                return True, True, True
            W = WPC * g + w
            n = WPC * LAST
            return W < n, 1 <= W <= n, 2 <= W <= n + 1

        CLEARED = 8
        with nc.Block() as block:

            @block.gpsimd
            def _(pool):
                nc.gpsimd.memset(halves[:, :], -0.5).then_inc(cleared, 1)
                nc.gpsimd.memset(v_ring[:, WPC - 1, :], 0.0).then_inc(cleared, 1)
                nc.gpsimd.memset(k_ring[:, :, (WPC - 1) * P:], 0.0).then_inc(cleared, 1)
                for j in range(2):
                    nc.gpsimd.memset(q_pad[j][:, :, :], 0.0).then_inc(cleared, 1)
                nc.gpsimd.memset(mid[:, :, :], 0.0).then_inc(cleared, 1)
                nc.gpsimd.memset(hidden[:, FT, :], 0.0).then_inc(cleared, 1)
                nc.gpsimd.memset(eps_col[:, :], EPS).then_inc(cleared, 1)
                pool.wait_ge(cleared, CLEARED)

                def body(g, la, lf):
                    for w in range(WPC):
                        W = WPC * g + w
                        if not parts(g, w)[0]:
                            continue
                        pool.wait_ge(sums_done, W + 1)
                        apart(pool, pool_passed)
                        nc.gpsimd.tensor_scalar(clipped[:, :], sumsq[:, :], 1e-24, None, ALU.max).then_inc(clip_done, 1)
                        pool.wait_ge(clip_done, W + 1)
                        nc.gpsimd.tensor_tensor(inv_norm[:, :], clipped[:, :], halves[:, :], ALU.pow).then_inc(inv_done, 1)
                        pool.wait_ge(roped, W + 1)
                        nc.gpsimd.tensor_tensor(rope_a[:, :, :], rope_a[:, :, :], rope_b[:, :, :], ALU.add).then_inc(added, 1)
                        pool.wait_ge(inv_done, W + 1)
                        pool.wait_ge(added, W + 1)
                        if not isinstance(g, int) or W:
                            pool.wait_ge(ring_ready[TK % 2], ring_use(W, TK) + 1)
                        nc.gpsimd.tensor_tensor(qk_n[:, :, :].rearrange("p s (h n) -> p (s h) n", n=HDIM),
                                                rope_a[:, :, :].rearrange("p s (h n) -> p (s h) n", n=HDIM),
                                                inv_norm[:, :].unsqueeze(2).broadcast_to([P, 2 * HEADS, HDIM]),
                                                ALU.mult).then_inc(qk_ready, 1)

                run(pool, body)

            @block.tensor
            def _(pe):
                def project(g, w, la):
                    W = WPC * g + w
                    if w == 0:
                        pe.wait_ge(h_ready, g + 1)
                    for n, (bank, done, free) in enumerate(((ps_q, q_mm, roped), (ps_k, k_mm, roped), (ps_v, v_mm, v_out))):
                        if not isinstance(g, int) or W:
                            pe.wait_ge(free, W)
                        for k in range(KD):
                            mm = nc.tensor.matmul(bank[:, :], h[:, k, w * P:(w + 1) * P], wt.wqkv[la][:, k, n * INNER:(n + 1) * INNER],
                                                  start=(k == 0), stop=(k == KD - 1))
                        mm.then_inc(done, 1)

                def ring_wait(W, r):
                    if not isinstance(W, int) or ring_use(W, r) > 0:
                        pe.wait_ge(ring_taken[r % 2], ring_use(W, r))

                def turn_probs(W, p):
                    pe.wait_ge(p_ready, 4 * (W - 2) + p + 1)
                    ring_wait(W, PT + p)
                    for j in range(2):
                        for s in range(2):
                            mm = nc.tensor.transpose(ring[(PT + p) % 2][:, (2 * j + s) * P:(2 * j + s + 1) * P],
                                                     probs[:, 2 * p + j, s * P:(s + 1) * P], wt.ident[:, :])
                    mm.then_inc(ring_ready[(PT + p) % 2], 1)

                def values(W, w, p):
                    ws = (w - 2) % WPC
                    pe.wait_ge(ring_taken[(PT + p) % 2], ring_use(W, PT + p) + 1)
                    if p == 0 and (not isinstance(W, int) or W > 2):
                        pe.wait_ge(o_out, W - 2)
                    for s, slot in enumerate(((ws - 1) % WPC, ws)):
                        for j in range(2):
                            head = 2 * p + j
                            mm = nc.tensor.matmul(ps_o[j * HDIM:(j + 1) * HDIM, p * P:(p + 1) * P],
                                                  v_ring[:, slot, head * HDIM:(head + 1) * HDIM], p_turned[:, p % 2, j, s, :],
                                                  start=(s == 0), stop=(s == 1))
                    if p == HEADS // 2 - 1:
                        mm.then_inc(pv_mm, 1)

                def turn_qk(W):
                    pe.wait_ge(qk_ready, W)
                    for s, r in ((0, TQ), (1, TK)):
                        ring_wait(W, r)
                        for p in range(HEADS // 2):
                            mm = nc.tensor.transpose(ring[r % 2][:, p * P:(p + 1) * P], qk_n[:, s, p * P:(p + 1) * P], wt.ident[:, :])
                        mm.then_inc(ring_ready[r % 2], 1)

                def scores(W, w):
                    ws = (w - 1) % WPC
                    pe.wait_ge(ring_taken[TQ % 2], ring_use(W, TQ) + 1)
                    pe.wait_ge(ring_taken[TK % 2], ring_use(W, TK) + 1)
                    for p in range(HEADS // 2):
                        r = SC + p
                        ring_wait(W, r)
                        for j in range(2):
                            out = ring[r % 2][:, 2 * j * P:(2 * j + 2) * P]
                            if ws:
                                mm = nc.tensor.matmul(out, q_pad[j][:, p, :], k_ring[:, p, (ws - 1) * P:(ws + 1) * P], start=True, stop=True)
                            else:
                                nc.tensor.matmul(out[:, 0:P], q_pad[j][:, p, :], k_ring[:, p, (WPC - 1) * P:], start=True, stop=True)
                                mm = nc.tensor.matmul(out[:, P:], q_pad[j][:, p, :], k_ring[:, p, 0:P], start=True, stop=True)
                        mm.then_inc(ring_ready[r % 2], 1)

                def ffn_fill(g, bank, use, operands):
                    if not isinstance(g, int) or (g - 2) * USES[bank] + use > 0:
                        pe.wait_ge(ffn_taken[bank], (g - 2) * USES[bank] + use)
                    for n, (a, b) in enumerate(operands):
                        mm = nc.tensor.matmul(ffn[bank][:, :], a, b, start=(n == 0), stop=(n == len(operands) - 1))
                    mm.then_inc(ffn_ready[bank], 1)

                def output_product(g, lf):
                    pe.wait_ge(o_out, WPC * (g - 1))
                    for m in range(KD):
                        ffn_fill(g, m, WO, [(wt.wo[lf][:, p, m * P:(m + 1) * P], o_ring[:, bass.ds(g % 2, 1), p, :].rearrange("p o n -> p (o n)"))
                                            for p in range(HEADS // 2)])

                def shifted(src):
                    return src[:, 0, 1:], src[:, 1, 0:CH]

                def mean(g):
                    for m in range(KD):
                        pe.wait_ge(ffn_taken[m], (g - 2) * USES[m] + WO + 1)
                    ffn_fill(g, 0, MEAN, [(wt.mean_w[:, :], x) for x in shifted(mid)])

                def variance(g):
                    pe.wait_ge(sq_dev, g - 1)
                    ffn_fill(g, 1, MEAN, [(wt.mean_w[:, :], hidden[:, k, :]) for k in range(KD)])

                def hidden_tile(g, lf, f):
                    if f == 0:
                        pe.wait_ge(normed, g - 1)
                    for bank in range(2):
                        c = (bank * FT + f) * P
                        ffn_fill(g, bank, GATE + f, [(wt.w1[lf][:, k, c:c + P], centred[:, k, :]) for k in range(KD)])

                def tails(g, lf):
                    ffn_fill(g, 0, TAILS, [(wt.w1[lf][:, k, 2 * FT * P:], centred[:, k, :]) for k in range(KD)])

                def down(g, lf, m):
                    pe.wait_ge(ffn_taken[1], (g - 2) * USES[1] + GATE + FT)
                    pe.wait_ge(ffn_taken[0], (g - 2) * USES[0] + TAILS + 1)
                    ffn_fill(g, 1 - m, W2 + m, [(wt.w2[lf][:, f, m * P:(m + 1) * P], hidden[:, f, :]) for f in range(FT + 1)])

                def body(g, la, lf):
                    for w in range(WPC):
                        W = WPC * g + w
                        new, mid_, old = parts(g, w)
                        if new:
                            project(g, w, la)
                        if old:
                            turn_probs(W, 0)
                            turn_probs(W, 1)
                            values(W, w, 0)
                            turn_probs(W, 2)
                            values(W, w, 1)
                            turn_probs(W, 3)
                            values(W, w, 2)
                            values(W, w, 3)
                        if lf is not None:
                            if w == 0:
                                output_product(g, lf)
                            elif w < 3:
                                hidden_tile(g, lf, 2 * w - 2)
                            else:
                                tails(g, lf)
                        if mid_:
                            turn_qk(W)
                        if lf is not None:
                            if w == 0:
                                mean(g)
                            elif w < 3:
                                hidden_tile(g, lf, 2 * w - 1)
                                if w == 2:
                                    hidden_tile(g, lf, 4)
                            else:
                                down(g, lf, 0)
                        if mid_:
                            scores(W, w)
                        if lf is not None:
                            if w == 0:
                                variance(g)
                            elif w == 3:
                                down(g, lf, 1)

                pe.wait_ge(cleared, CLEARED)
                run(pe, body)

            @block.scalar
            def _(act):
                def head_squares(W):
                    for s, (bank, mm) in enumerate(((ps_q, q_mm), (ps_k, k_mm))):
                        act.wait_ge(mm, W + 1)
                        if not isinstance(W, int) or W:
                            act.wait_ge(added, W)
                        nc.scalar.activation(rope_b[:, s, :], bank[:, :], ACT.Square).then_inc(squared, 1)

                def take_v(W, w):
                    act.wait_ge(v_mm, W + 1)
                    nc.scalar.copy(v_ring[:, w, :], ps_v[:, :]).then_inc(v_out, 1)

                def take_probs(W, p):
                    r = PT + p
                    act.wait_ge(ring_ready[r % 2], ring_use(W, r) + 1)
                    nc.scalar.copy(p_turned[:, p % 2, :, :, :].rearrange("p j s n -> p (j s n)"), ring[r % 2][:, :]).then_inc(ring_taken[r % 2], 1)

                def take_o(g, w):
                    act.wait_ge(pv_mm, WPC * g + w - 1)
                    chunk, ws = (g, w - 2) if w >= 2 else (g - 1, w + 2)
                    nc.scalar.copy(o_ring[:, bass.ds(chunk % 2, 1), :, ws * P:(ws + 1) * P].rearrange("p o h n -> p (o h) n"),
                                   ps_o[:, :].rearrange("p (h n) -> p h n", n=P)).then_inc(o_out, 1)

                def take_qk(W, w):
                    ws = (w - 1) % WPC
                    act.wait_ge(ring_ready[TQ % 2], ring_use(W, TQ) + 1)
                    nc.scalar.copy(q_pad[0][0:HDIM, :, :], ring[TQ % 2][0:HDIM, :].rearrange("p (h n) -> p h n", n=P))
                    nc.scalar.copy(q_pad[1][HDIM:, :, :], ring[TQ % 2][HDIM:, :].rearrange("p (h n) -> p h n", n=P)).then_inc(ring_taken[TQ % 2], 1)
                    act.wait_ge(ring_ready[TK % 2], ring_use(W, TK) + 1)
                    nc.scalar.copy(k_ring[:, :, ws * P:(ws + 1) * P], ring[TK % 2][:, :].rearrange("p (h n) -> p h n", n=P)).then_inc(ring_taken[TK % 2], 1)

                def exponentials(W):
                    for head in range(HEADS):
                        if head % 2 == 0:
                            r = SC + head // 2
                            act.wait_ge(ring_taken[r % 2], ring_use(W, r) + 1)
                        nc.scalar.activation(probs[:, head, :], probs[:, head, :], ACT.Exp, bias=neg_max[:, head:head + 1], scale=-1.0,
                                             accum_out=total[:, head:head + 1]).then_inc(exp_done, 1)

                def square_deviations(g):
                    act.wait_ge(ffn_taken[0], (g - 2) * USES[0] + MEAN + 1)
                    for k in range(KD):
                        ins = nc.scalar.activation(hidden[:, k, :], centred[:, k, :], ACT.Square)
                    ins.then_inc(sq_dev, 1)

                def inverse_deviation(g):
                    act.wait_ge(ffn_ready[1], (g - 2) * USES[1] + MEAN + 1)
                    nc.scalar.activation(dev[:, :], ffn[1][:, :], ACT.Ln, bias=eps_col[:, :]).then_inc(ffn_taken[1], 1)
                    act.wait_ge(ffn_taken[1], (g - 2) * USES[1] + MEAN + 1)
                    nc.scalar.activation(dev[:, :], dev[:, :], ACT.Exp, scale=-0.5).then_inc(dev_done, 1)

                def gate_tile(g, lf, f):
                    act.wait_ge(ffn_ready[0], (g - 2) * USES[0] + GATE + f + 1)
                    if f < FT:
                        nc.scalar.activation(gate[:, f % 2, :], ffn[0][:, :], ACT.Gelu, bias=wt.b1[lf][:, 1, f:f + 1]).then_inc(ffn_taken[0], 1)
                    else:
                        nc.scalar.activation(gate[TAIL_AT:TAIL_AT + TAIL, f % 2, :], ffn[0][0:TAIL, :], ACT.Gelu,
                                             bias=wt.b1[lf][0:TAIL, 1, f:f + 1]).then_inc(tail_gated, 1)

                def body(g, la, lf):
                    for w in range(WPC):
                        W = WPC * g + w
                        new, mid_, old = parts(g, w)
                        if new:
                            head_squares(W)
                            take_v(W, w)
                        if old:
                            for p in range(HEADS // 2):
                                take_probs(W, p)
                            take_o(g, w)
                        if lf is not None:
                            if w in (1, 2):
                                gate_tile(g, lf, 2 * w - 2)
                            elif w == 3:
                                gate_tile(g, lf, FT)
                        if mid_:
                            take_qk(W, w)
                        if lf is not None:
                            if w == 0:
                                square_deviations(g)
                            elif w < 3:
                                gate_tile(g, lf, 2 * w - 1)
                                if w == 2:
                                    gate_tile(g, lf, 4)
                        if mid_:
                            exponentials(W)
                        if lf is not None and w == 0:
                            inverse_deviation(g)

                act.wait_ge(cleared, CLEARED)
                run(act, body)

            @block.vector
            def _(dve):
                def take_h(g, n):
                    if not isinstance(g, int) or g:
                        dve.wait_ge(v_mm, WPC * g)
                    src = lambda k, s: xnt[:, k, bass.ds(n, 1), s].rearrange("p o n -> p (o n)")
                    nc.vector.tensor_copy(h[:, 0, :], src(0, slice(1, 1 + CH)))
                    nc.vector.tensor_copy(h[:, 1, :], src(1, slice(0, CH))).then_inc(h_ready, 1)

                def rotate(g, w, la):
                    W = WPC * g + w
                    tab = wt.tables[la][:, bass.ds((g % 2) * WPC + w, 1), :, :].rearrange("p o s n -> p (o s) n")
                    if not isinstance(W, int) or W:
                        dve.wait_ge(qk_ready, W)
                    view = lambda x: x.rearrange("p (h n) -> p h n", n=HDIM)
                    for s, bank in enumerate((ps_q, ps_k)):
                        dve.wait_ge(squared, 2 * W + s + 1)
                        nc.vector.tensor_tensor(view(rope_a[:, s, :]), view(bank[:, :]), tab[:, 2 * s:2 * s + 1, :].broadcast_to([P, HEADS, HDIM]),
                                                ALU.mult).then_inc(cos_done, 1)
                    if not isinstance(W, int) or W:
                        dve.wait_ge(clip_done, W)
                    nc.vector.tensor_reduce(sumsq[:, :], rope_b[:, :, :].rearrange("p s (h n) -> p (s h) n", n=HDIM), AX_X, ALU.add).then_inc(sums_done, 1)
                    dve.wait_ge(sums_done, W + 1)
                    for s, bank in enumerate((ps_q, ps_k)):
                        halves_ = lambda x: x.rearrange("p (h a n) -> p h a n", a=2, n=HDIM // 2)
                        sin = tab[:, 2 * s + 1, :].rearrange("p (a n) -> p a n", a=2).unsqueeze(1).broadcast_to([P, HEADS, 2, HDIM // 2])
                        ins = nc.vector.tensor_tensor(halves_(rope_b[:, s, :]), halves_(bank[:, :])[:, :, ::-1, :], sin, ALU.mult)
                    ins.then_inc(roped, 1)

                def mask_and_max(g, w):
                    W = WPC * g + w
                    mask = wt.mask[:, 1::2, :]
                    if w == 1:
                        dve.wait_ge(mask_picked, g + 1)
                        mask = wt.mask[:, 2:4, :]
                    pair = lambda x: x.rearrange("p (s n) -> p s n", s=2)
                    for head in range(HEADS):
                        r = SC + head // 2
                        if head % 2 == 0:
                            dve.wait_ge(ring_ready[r % 2], ring_use(W, r) + 1)
                            apart(dve, dve_passed)
                        src = ring[r % 2][:, (head % 2) * 2 * P:(head % 2 + 1) * 2 * P]
                        ins = nc.vector.tensor_tensor_reduce(pair(probs[:, head, :]), pair(src), mask, -1.0, 3.4e38, ALU.add, ALU.min, neg_max[:, head:head + 1])
                        if head % 2:
                            ins.then_inc(ring_taken[r % 2], 1)

                def normalise(W):
                    dve.wait_ge(exp_done, HEADS * W)
                    nc.vector.reciprocal(inv_total[:, :], total[:, :]).then_inc(inv_total_done, 1)
                    dve.wait_ge(inv_total_done, W)
                    for p in range(HEADS // 2):
                        for j in range(2):
                            head = 2 * p + j
                            ins = nc.vector.tensor_scalar(probs[:, head, :], probs[:, head, :], inv_total[:, head:head + 1], None, ALU.mult)
                        ins.then_inc(p_ready, 1)

                def x_chunk(n, k, s):
                    return xnt[:, k, bass.ds(n, 1), s].rearrange("p o n -> p (o n)")

                def add_attention(g, n):
                    nc.vector.tensor_scalar(mid[:, :, 0:1], mid[:, :, CH:CH + 1], wt.parity[:, bass.ds(g % 2, 1)], None, ALU.mult).then_inc(carried, 1)
                    dve.wait_ge(carried, g - 1)
                    for m in range(KD):
                        dve.wait_ge(ffn_ready[m], (g - 2) * USES[m] + WO + 1)
                        ins = nc.vector.tensor_tensor(mid[:, m, 1:], ffn[m][:, :], x_chunk(n, m, slice(1, 1 + CH)), ALU.add)
                        ins.then_inc(ffn_taken[m], 1)

                def centre(g):
                    dve.wait_ge(ffn_ready[0], (g - 2) * USES[0] + MEAN + 1)
                    nc.vector.scalar_tensor_tensor(out=centred[:, 0, :], in0=ffn[0][:, :], scalar=-1.0, in1=mid[:, 0, 1:], op0=ALU.mult, op1=ALU.add)
                    nc.vector.scalar_tensor_tensor(out=centred[:, 1, :], in0=ffn[0][:, :], scalar=-1.0, in1=mid[:, 1, 0:CH], op0=ALU.mult,
                                                   op1=ALU.add).then_inc(ffn_taken[0], 1)

                def scale(g, lf):
                    dve.wait_ge(dev_done, g - 1)
                    dve.wait_ge(sq_dev, g - 1)
                    for k in range(KD):
                        nc.vector.tensor_tensor(centred[:, k, :], centred[:, k, :], dev[:, :], ALU.mult).then_inc(scaled, 1)
                    dve.wait_ge(scaled, 2 * (g - 1))
                    for k in range(KD):
                        ins = nc.vector.tensor_scalar(centred[:, k, :], centred[:, k, :], wt.lnp[lf][:, 0, k:k + 1], wt.lnp[lf][:, 1, k:k + 1],
                                                      ALU.mult, ALU.add)
                    ins.then_inc(normed, 1)

                def hidden_tile(g, lf, f):
                    if f < FT:
                        dve.wait_ge(ffn_taken[0], (g - 2) * USES[0] + GATE + f + 1)
                    else:
                        dve.wait_ge(tail_gated, g - 1)
                    rows, bank, use = (slice(0, P), 1, GATE + f) if f < FT else (slice(TAIL_AT, TAIL_AT + TAIL), 0, TAILS)
                    dve.wait_ge(ffn_ready[bank], (g - 2) * USES[bank] + use + 1)
                    nc.vector.scalar_tensor_tensor(out=hidden[rows, f, :], in0=ffn[bank][rows, :], scalar=wt.b1[lf][rows, 0, f:f + 1],
                                                   in1=gate[rows, f % 2, :], op0=ALU.add, op1=ALU.mult).then_inc(ffn_taken[bank], 1)

                def add_ffn(g, lf, n, m):
                    dve.wait_ge(ffn_ready[1 - m], (g - 2) * USES[1 - m] + W2 + m + 1)
                    nc.vector.scalar_tensor_tensor(out=x_chunk(n, m, slice(1, 1 + CH)), in0=ffn[1 - m][:, :], scalar=wt.b2[lf][:, m:m + 1],
                                                   in1=mid[:, m, 1:], op0=ALU.add, op1=ALU.add).then_inc(ffn_taken[1 - m], 1)

                def carry(g, n):
                    for m in range(KD):
                        dve.wait_ge(ffn_taken[1 - m], (g - 2) * USES[1 - m] + W2 + m + 1)
                    nc.vector.tensor_scalar(xnt[:, :, bass.ds((n + 1) % CHUNKS, 1), 0:1].rearrange("p k o n -> p k (o n)"),
                                            xnt[:, :, bass.ds(n, 1), CH:CH + 1].rearrange("p k o n -> p k (o n)"),
                                            wt.parity[:, bass.ds((g + 1) % 2, 1)], None, ALU.mult).then_inc(x_out, 1)

                def body(g, la, lf):
                    n = g - 2 - CHUNKS * lf if lf is not None else None
                    for w in range(WPC):
                        W = WPC * g + w
                        new, mid_, old = parts(g, w)
                        if w == 0 and (not isinstance(g, int) or g < LAST):
                            nc.vector.tensor_copy(wt.mask[:, 2:3, :], wt.mask[:, bass.ds(g % 2, 1), :]).then_inc(mask_picked, 1)
                        if new:
                            rotate(g, w, la)
                        if lf is not None:
                            if w == 0:
                                add_attention(g, n)
                                centre(g)
                            elif w < 3:
                                hidden_tile(g, lf, 2 * w - 2)
                                hidden_tile(g, lf, 2 * w - 1)
                                if w == 2:
                                    hidden_tile(g, lf, 4)
                            else:
                                hidden_tile(g, lf, FT)
                        if mid_:
                            mask_and_max(g, w)
                            normalise(W)
                        if lf is not None:
                            if w == 0:
                                scale(g, lf)
                            elif w == 3:
                                add_ffn(g, lf, n, 0)
                                add_ffn(g, lf, n, 1)
                                carry(g, n)
                        if w == WPC - 1 and new and not (isinstance(g, int) and g + 1 == LAST):
                            take_next(g, la, lf)

                def take_next(g, la, lf):
                    if lf is not None:
                        dve.wait_ge(x_out, g - 1)
                    take_h(g + 1, (g + 1) % CHUNKS)

                dve.wait_ge(cleared, CLEARED)
                take_h(0, 0)
                run(dve, body)


def combine(nc, x, w_out_t, ident_in, xnt, o_dram, inv_dram, out):
    with ExitStack() as ctx:
        sb = lambda n, s: ctx.enter_context(nc.sbuf_tensor(n, s, F32))
        ps = lambda n: ctx.enter_context(nc.psum_tensor(n, [P, CH], F32))
        sem = lambda n: ctx.enter_context(nc.semaphore(n))

        ident = sb("c_ident", [P, P])
        w_out = sb("w_out", [P, KD, D])
        sums = sb("sums", [P, CH])
        inv_sums = sb("inv_sums", [P, CH])
        o_in = sb("o_in", [P, 2, KD, CH])
        inv_in = sb("inv_in", [P, 2, KD, CH])
        x_in = sb("c_x_in", [P, 2, 4, D])
        o_n = sb("o_n", [P, 2, KD, CH])
        silu = sb("silu", [P, 2, KD, CH])
        gated = sb("gated", [P, 2, KD, CH])
        result = sb("result", [P, 2, 4, D])

        ps_s = [[ps(f"ps_s{c}{m}") for m in range(KD)] for c in range(2)]
        ps_t = [[ps(f"ps_t{c}{m}") for m in range(2)] for c in range(2)]

        consts_in = sem("c_consts_in")
        sums_in = sem("sums_in")
        inverted = sem("inverted")
        inv_stored = sem("inv_stored")
        chunk_in = [sem(f"chunk_in{c}") for c in range(2)]
        divided = sem("divided")
        silu_done = sem("silu_done")
        s_ready = sem("s_ready")
        gated_done = sem("gated_done")
        turned_back = sem("turned_back")
        summed = sem("summed")
        out_stored = [sem(f"out_stored{c}") for c in range(2)]
        LOADS = 2 * KD + 1

        with nc.Block() as block:

            @block.sync
            def _(sp):
                def load(b, c):
                    for f in range(KD):
                        src = o_dram.rearrange("(i u) (j h r) n -> i h (u j) r n", u=4, j=2, h=2)
                        src = src[bass.ds(2 * b + f, 1), c, :, 1:1 + G_DIM, :].rearrange("o g r n -> (o g) r n")
                        sp.dma_start(o_in[:, c, f, :], src).then_inc(chunk_in[c], 16)
                        src = inv_dram.rearrange("(i g h) n -> i h g n", g=8, h=2)[bass.ds(2 * b + f, 1), c, :, :].rearrange("o g n -> (o g) n")
                        sp.dma_start(inv_in[:, c, f, :], src.unsqueeze(1).broadcast_to([8, G_DIM, CH])).then_inc(chunk_in[c], 16)
                    src = x[bass.ds(b, 1), c * CH:(c + 1) * CH, :].rearrange("o (t p) n -> p (o t) n", p=P)
                    sp.dma_start(x_in[:, c, :, :], src).then_inc(chunk_in[c], 16)

                def store(b, c):
                    sp.wait_ge(summed, 4 * b + 2 * c + 2)
                    dst = out[bass.ds(b, 1), c * CH:(c + 1) * CH, :].rearrange("o (t p) n -> p (o t) n", p=P)
                    sp.dma_start(dst, result[:, c, :, :]).then_inc(out_stored[c], 16)

                sp.dma_start(sums[:, :], o_dram.rearrange("p (s r) n -> (p s) r n", r=2 * G_DIM)[:, 0, :]).then_inc(sums_in, 16)
                sp.dma_start(ident[:, :], ident_in).then_inc(consts_in, 16)
                sp.dma_start(w_out[:, :, :], w_out_t.rearrange("(k p) n -> p k n", p=P)).then_inc(consts_in, 16)
                sp.wait_ge(inverted, 1)
                sp.dma_start(inv_dram, inv_sums[:, :]).then_inc(inv_stored, 16)
                sp.wait_ge(inv_stored, 16)
                load(0, 0)
                load(0, 1)
                with sp.Fori(0, B - 1) as b:
                    for c in range(2):
                        sp.wait_ge(summed, 4 * b + 2 * c + 2)
                        load(b + 1, c)
                        store(b, c)
                for c in range(2):
                    store(B - 1, c)
                for c in range(2):
                    sp.wait_ge(out_stored[c], 16 * B)

            @block.scalar
            def _(act):
                with act.Fori(0, B) as b:
                    for c in range(2):
                        for k in range(KD):
                            ins = nc.scalar.activation(silu[:, c, k, :], xnt[:, k, bass.ds(2 * b + c, 1), 1:].rearrange("p o n -> p (o n)"), ACT.Silu)
                        ins.then_inc(silu_done, 1)
                        act.wait_ge(gated_done, 4 * b + 2 * c + 2)

            @block.vector
            def _(dve):
                def divide(b, c):
                    dve.wait_ge(chunk_in[c], 16 * LOADS * (b + 1))
                    for f in range(KD):
                        nc.vector.tensor_tensor(o_n[:, c, f, :], o_in[:, c, f, :], inv_in[:, c, f, :], ALU.mult).then_inc(divided, 1)

                def gate(b, c, first):
                    dve.wait_ge(silu_done, 2 * b + c + 1)
                    for m in range(KD):
                        dve.wait_ge(s_ready, 4 * b + 2 * c + m + 1)
                        nc.vector.tensor_tensor(gated[:, c, m, :], ps_s[c][m][:, :], silu[:, c, m, :], ALU.mult).then_inc(gated_done, 1)

                def add(b, c, first):
                    if not first:
                        dve.wait_ge(out_stored[c], 16 * b)
                    for m in range(2):
                        dve.wait_ge(turned_back, 4 * b + 2 * c + m + 1)
                        nc.vector.tensor_tensor(result[:, c, 2 * m:2 * m + 2, :].rearrange("p t n -> p (t n)"), ps_t[c][m][:, :],
                                                x_in[:, c, 2 * m:2 * m + 2, :].rearrange("p t n -> p (t n)"), ALU.add).then_inc(summed, 1)

                def body(b, first, last):
                    gate(b, 0, first)
                    divide(b, 1)
                    add(b, 0, first)
                    gate(b, 1, first)
                    if not last:
                        divide(b + 1, 0)
                    add(b, 1, first)

                dve.wait_ge(sums_in, 16)
                nc.vector.reciprocal(inv_sums[:, :], sums[:, :]).then_inc(inverted, 1)
                divide(0, 0)
                body(0, True, False)
                with dve.Fori(1, B - 1) as b:
                    body(b, False, False)
                body(B - 1, False, True)

            @block.tensor
            def _(pe):
                def project(b, c, first):
                    pe.wait_ge(divided, 4 * b + 2 * c + 2)
                    if not first:
                        pe.wait_ge(gated_done, 4 * b + 2 * c - 2)
                    for m in range(KD):
                        for f in range(KD):
                            mm = nc.tensor.matmul(ps_s[c][m][:, :], w_out[:, f, m * P:(m + 1) * P], o_n[:, c, f, :], start=(f == 0), stop=(f == KD - 1))
                        mm.then_inc(s_ready, 1)

                def turn(b, c, first):
                    pe.wait_ge(gated_done, 4 * b + 2 * c + 2)
                    if not first:
                        pe.wait_ge(summed, 4 * b + 2 * c - 2)
                    for m in range(2):
                        for t in range(2):
                            for k in range(KD):
                                s = slice((2 * m + t) * P, (2 * m + t + 1) * P)
                                mm = nc.tensor.transpose(ps_t[c][m][:, t * D + k * P:t * D + (k + 1) * P], gated[:, c, k, s], ident[:, :])
                        mm.then_inc(turned_back, 1)

                def body(b, first, last):
                    turn(b, 0, first)
                    project(b, 1, first)
                    turn(b, 1, first)
                    if not last:
                        project(b + 1, 0, False)

                pe.wait_ge(consts_in, 32)
                project(0, 0, True)
                body(0, True, False)
                with pe.Fori(1, B - 1) as b:
                    body(b, False, False)
                body(B - 1, False, True)


def rope_table():
    half = G_DIM // 2
    freq = np.float32(1.0) / np.float32(10000.0) ** (np.arange(half, dtype=np.float32) / np.float32(half))
    angle = np.arange(L, dtype=np.float32)[:, None] * freq[None, :]
    c, s = np.cos(angle.astype(np.float64)), np.sin(angle.astype(np.float64))
    return np.stack([np.concatenate([c, c], 1), np.concatenate([-s, s], 1)], 1).astype(np.float32)


def xpos_table():
    idx = np.arange(0, HDIM, 2, dtype=np.float32)
    freq = np.float32(1.0) / np.float32(10000.0) ** (idx / np.float32(HDIM))
    angle = (np.arange(L, dtype=np.float32)[:, None] * freq[None, :]).astype(np.float64)
    base = (idx.astype(np.float64) + 0.4 * HDIM) / (1.4 * HDIM)
    scale = base[None, :] ** ((np.arange(L) - L // 2) / (P / 2.0))[:, None]
    c, s = np.cos(angle), np.sin(angle)
    cat = lambda a, b: np.concatenate([a, b], 1)
    return np.stack([cat(c * scale, c * scale) * QK_SCALE, cat(-s * scale, s * scale) * QK_SCALE,
                     cat(c / scale, c / scale), cat(-s / scale, s / scale)], 1).astype(np.float32)


def window_masks():
    r, c = np.arange(P)[:, None], np.arange(P)[None, :]
    return np.stack([np.full((P, P), MASKED), np.where(c >= r, 0.0, MASKED), np.where(c <= r, 0.0, MASKED)]).astype(np.float32)


def gated_attention_kernel(nc, x, w_qkv_t, w_out_t, wqkv, q_scale, k_scale, wo, ln_g, ln_b, w1, b1, w2, b2,
                           rope, xpos, masks, ident, out):
    with ExitStack() as ctx:
        internal = lambda n, s: nc.dram_tensor(n, s, F32, kind="Internal").ap()
        xnt = ctx.enter_context(nc.sbuf_tensor("xnt", [P, KD, CHUNKS, 1 + CH], F32))
        qs_dram = internal("qs", (2 * B, 8, 2, G_DIM, L))
        ks_dram = internal("ks", (2 * B, 8, 2, G_DIM, L))
        v_dram = internal("v", (2 * B, TILES, P, P))
        o_dram = internal("o", (UNITS, P, CH))
        inv_dram = internal("inv", (P, CH))
        prepare_tokens(nc, x, w_qkv_t, rope, ident, xnt, qs_dram, ks_dram, v_dram)
        global_attention(nc, ident, qs_dram, ks_dram, v_dram, o_dram)
        with ExitStack() as layers:
            wt = Weights(layers, nc)
            load_weights(nc, wt, wqkv, q_scale, k_scale, wo, ln_g, ln_b, w1, b1, w2, b2, xpos, masks, ident)
            local_layers(nc, wt, xnt)
        combine(nc, x, w_out_t, ident, xnt, o_dram, inv_dram, out)


_INS = ['L0_attn_x', 'L0_attn_w_qkv', 'L0_attn_w_out', 'L0_ffn_wqkv', 'L0_ffn_q_scale', 'L0_ffn_k_scale', 'L0_ffn_wo', 'L0_ffn_ln_g',
        'L0_ffn_ln_b', 'L0_ffn_w1', 'L0_ffn_b1', 'L0_ffn_w2', 'L0_ffn_b2']
_TURNED = ('L0_attn_w_qkv', 'L0_attn_w_out')
_OUTS = [((4, 1024, 256), 'float32')]


def kernel(**inputs):
    import numpy as _np
    import concourse.bacc as _bacc
    from concourse import mybir as _mybir
    from concourse.bass_utils import run_bass_kernel_spmd as _run

    nc = _bacc.Bacc("TRN2", target_bir_lowering=False, num_devices=1)
    arrays, args = {}, []
    tables = {'rope': rope_table(), 'xpos': xpos_table(), 'masks': window_masks(), 'ident': _np.eye(P, dtype=_np.float32)}
    laid_out = [(n, _np.ascontiguousarray(_np.asarray(inputs[n]).T if n in _TURNED else inputs[n])) for n in _INS] + list(tables.items())
    for name, a in laid_out:
        arrays[f"in_{name}_dram"] = a
        args.append(nc.dram_tensor(f"in_{name}_dram", a.shape, _mybir.dt.from_np(a.dtype), kind="ExternalInput").ap())
    for i, (shape, dtype) in enumerate(_OUTS):
        dt = _mybir.dt.from_np(_np.dtype(dtype))
        args.append(nc.dram_tensor(f"out_{i}_dram", shape, dt, kind="ExternalOutput").ap())
    gated_attention_kernel(nc, *args)
    r = _run(nc, [arrays], core_ids=[0])
    got = tuple(r.results[0][f"out_{i}_dram"] for i in range(len(_OUTS)))
    return got[0]
```

```python
from contextlib import ExitStack

import numpy as np
import concourse.bass as bass
from concourse import mybir

F32 = mybir.dt.float32
F32R = mybir.dt.float32r
ALU = mybir.AluOpType
ACT = mybir.ActivationFunctionType
AX_X = mybir.AxisListType.X

P = 128
B, L, D = 4, 1024, 256
KD = D // P
TILES = L // P
G_HEADS, G_DIM = 16, 16
UNITS = B * G_HEADS // 2
SPLIT = 4 * G_DIM
CH = 512
EPS = 1e-5
STORES = 4 * KD + KD


def flat(ap):
    return ap.rearrange("o p n -> (o p) n")


def apart(eng, passed):
    eng.sem_inc(passed, 1)


def prepare_tokens(nc, wt, x, wqkv_t, rope, ident_in, xnt, qs_dram, ks_dram, v_dram):
    with ExitStack() as ctx:
        sb = lambda n, s, d=F32: ctx.enter_context(nc.sbuf_tensor(n, s, d))
        ps = lambda n, s: ctx.enter_context(nc.psum_tensor(n, s, F32))
        sem = lambda n: ctx.enter_context(nc.semaphore(n))

        ident = sb("a_ident", [P, P])
        wqkv = sb("a_wqkv", [P, KD, 3 * D])
        table = sb("a_rope", [P, TILES, 2, G_DIM])
        x_in = sb("x_in", [P, 2, 4, D])
        stats = sb("stats", [P, 2, 4, 6])
        moments = sb("moments", [P, 2, 4, 2])
        half = sb("half", [P, 4])
        rstd = sb("rstd", [P, 2, 4])
        xn = sb("xn", [P, 2, 4, D])
        xs = sb("xs", [P, 2, KD, CH])
        roped = sb("roped", [P, 2, 2 * D])
        turned = sb("turned", [P, 2, 2 * D])
        qkr = sb("qkr", [P, 2, 2 * D])
        split = sb("split", [P, 2, 4, 2, CH], F32R)
        v_sb = sb("v_sb", [P, 2, 4, D])

        ps_x = [ps(f"ps_x{k}", [P, CH]) for k in range(KD)]
        ps_qk = [ps(f"ps_qk{k}", [P, CH]) for k in range(2)]
        ps_v = [ps(f"ps_v{k}", [P, CH]) for k in range(2)]
        ps_t = [ps(f"ps_t{k}", [P, CH]) for k in range(2)]

        dve_passed, pool_passed = sem("a_dve_passed"), sem("a_pool_passed")
        consts_in = sem("consts_in")
        x_loaded = [sem(f"x_loaded{c}") for c in range(2)]
        half_set = sem("half_set")
        stats_done = sem("stats_done")
        moments_done = sem("moments_done")
        eps_added = sem("eps_added")
        rstd_done = sem("rstd_done")
        xn_done = sem("xn_done")
        x_turned = sem("x_turned")
        xs_done = sem("xs_done")
        xnt_done = sem("xnt_done")
        qk_mm = sem("qk_mm")
        v_mm = sem("v_mm")
        v_copied = sem("v_copied")
        rope_cos = sem("rope_cos")
        rope_sin = sem("rope_sin")
        rope_sum = sem("rope_sum")
        qk_turned = sem("qk_turned")
        high_done = sem("high_done")
        low_done = sem("low_done")
        stored = [sem(f"stored{c}") for c in range(2)]

        with nc.Block() as block:

            @block.sync
            def _(sp):
                sp.dma_start(ident[:, :], ident_in).then_inc(consts_in, 16)
                sp.dma_start(wqkv[:, :, :], wqkv_t.rearrange("(k p) n -> p k n", p=P)).then_inc(consts_in, 16)
                sp.dma_start(table[:, :, :, :], rope.rearrange("(t p) s n -> p t s n", p=P)).then_inc(consts_in, 16)

                def load(i, c):
                    src = x[bass.ds(i, 1), c * CH:(c + 1) * CH, :].rearrange("o (t p) n -> p (o t) n", p=P)
                    sp.dma_start(x_in[:, c, :, :], src).then_inc(x_loaded[c], 16)

                def store(i, c):
                    sp.wait_ge(low_done, 8 * i + 4 * c + 4)
                    for part, dram in ((0, qs_dram), (1, ks_dram)):
                        for f in range(KD):
                            for s in range(2):
                                dst = dram[bass.ds(2 * i + f, 1), :, s, :, c * CH:(c + 1) * CH].rearrange("o h d n -> (o h) d n")
                                sp.dma_start(dst, split[:, c, 2 * part + f, s, :].bitcast(F32)).then_inc(stored[c], 16)
                    sp.wait_ge(v_copied, 8 * i + 4 * c + 4)
                    for f in range(KD):
                        dst = v_dram[bass.ds(2 * i + f, 1), c * 4:c * 4 + 4, :, :].rearrange("o t p n -> p (o t) n")
                        sp.dma_start(dst, v_sb[:, c, :, f * P:(f + 1) * P]).then_inc(stored[c], 16)

                load(0, 0)
                load(0, 1)
                if wt:
                    sp.wait_ge(wt.set, wt.SETS)
                    wt.load_small(nc, sp)
                    wt.load_wo(sp, 0)
                    wt.load_w2(sp, 0)
                    wt.copy_raw(sp)
                with sp.Fori(0, B - 1) as i:
                    for c in range(2):
                        sp.wait_ge(xn_done, 8 * i + 4 * c + 4)
                        load(i + 1, c)
                    for c in range(2):
                        store(i, c)
                for c in range(2):
                    store(B - 1, c)
                if wt:
                    sp.wait_ge(wt.raw, 32)
                    wt.load_wqkv(sp, 0)
                    wt.load_w1(sp, 0)
                for c in range(2):
                    sp.wait_ge(stored[c], B * STORES * 16)

            @block.gpsimd
            def _(pool):
                nc.gpsimd.memset(half[:, :], -0.5).then_inc(half_set, 1)
                nc.gpsimd.memset(xnt[:, :, :, 0:1], 0.0).then_inc(half_set, 1)
                pool.wait_ge(half_set, 2)

                def inverse_deviation(i, c):
                    pool.wait_ge(moments_done, 8 * i + 4 * c + 4)
                    apart(pool, pool_passed)
                    nc.gpsimd.tensor_scalar(rstd[:, c, :], moments[:, c, :, 1], EPS, None, ALU.add).then_inc(eps_added, 1)
                    pool.wait_ge(eps_added, 2 * i + c + 1)
                    nc.gpsimd.tensor_tensor(rstd[:, c, :], rstd[:, c, :], half[:, :], ALU.pow).then_inc(rstd_done, 1)

                def body(i, last):
                    for c in range(2):
                        pool.wait_ge(xs_done, 4 * i + 2 * c + 2)
                        apart(pool, pool_passed)
                        for k in range(KD):
                            nc.gpsimd.tensor_copy(xnt[:, k, bass.ds(2 * i + c, 1), 1:].rearrange("p o n -> p (o n)"),
                                                  xs[:, c, k, :]).then_inc(xnt_done, 1)
                        if c == 0:
                            nc.gpsimd.tensor_copy(xnt[:, :, bass.ds(2 * i + 1, 1), 0:1].rearrange("p k o n -> p k (o n)"),
                                                  xs[:, 0, :, CH - 1:]).then_inc(xnt_done, 1)
                        for t in range(4 * c, 4 * c + 4):
                            pool.wait_ge(rope_sin, 8 * i + t + 1)
                            if t >= 2:
                                pool.wait_ge(qk_turned, 8 * i + t - 1)
                            elif not isinstance(i, int) or i:
                                pool.wait_ge(qk_turned, 8 * i + t - 1)
                            nc.gpsimd.tensor_tensor(qkr[:, t % 2, :], roped[:, t % 2, :], turned[:, t % 2, :],
                                                    ALU.add).then_inc(rope_sum, 1)
                            if not last and t in (1, 4):
                                inverse_deviation(i + 1, t // 4)

                inverse_deviation(0, 0)
                inverse_deviation(0, 1)
                if wt:
                    pool.wait_ge(rstd_done, 2)
                    wt.clear(nc)
                body(0, False)
                with pool.Fori(1, B - 1) as i:
                    body(i, False)
                body(B - 1, True)

            @block.vector
            def _(dve):
                def normalise(i, c):
                    dve.wait_ge(x_loaded[c], 16 * i + 16)
                    for t in range(4):
                        nc.vector.bn_stats(stats[:, c, t, :], x_in[:, c, t, :]).then_inc(stats_done, 1)
                    dve.wait_ge(stats_done, 8 * i + 4 * c + 4)
                    apart(dve, dve_passed)
                    for t in range(4):
                        nc.vector.bn_aggr(moments[:, c, t, :], stats[:, c, t, :]).then_inc(moments_done, 1)

                def scale(i, c, before):
                    dve.wait_ge(rstd_done, 2 * i + c + 1)
                    if before:
                        dve.wait_ge(x_turned, 4 * i + 2 * c - 2)
                    for t in range(4):
                        nc.vector.tensor_scalar(xn[:, c, t, :], x_in[:, c, t, :], moments[:, c, t, 0:1],
                                                rstd[:, c, t:t + 1], ALU.subtract, ALU.mult).then_inc(xn_done, 1)

                def rotate(i, t, first):
                    dve.wait_ge(qk_mm, 8 * i + t + 1)
                    if t >= 2 or not first:
                        dve.wait_ge(rope_sum, 8 * i + t - 1)
                    src = ps_qk[t % 2][:, :].rearrange("p (h n) -> p h n", n=G_DIM)
                    cos = table[:, t, 0, :].rearrange("p (o n) -> p o n", o=1).broadcast_to([P, 2 * G_HEADS, G_DIM])
                    sin = table[:, t, 1, :].rearrange("p (o n) -> p o n", o=1)
                    a = roped[:, t % 2, :].rearrange("p (h n) -> p h n", n=G_DIM)
                    r = turned[:, t % 2, :].rearrange("p (h n) -> p h n", n=G_DIM)
                    hd = G_DIM // 2
                    nc.vector.tensor_tensor(a, src, cos, ALU.mult)
                    nc.vector.tensor_tensor(r[:, :, 0:hd], src[:, :, hd:], sin[:, :, 0:hd].broadcast_to([P, 2 * G_HEADS, hd]), ALU.mult)
                    nc.vector.tensor_tensor(r[:, :, hd:], src[:, :, 0:hd], sin[:, :, hd:].broadcast_to([P, 2 * G_HEADS, hd]),
                                            ALU.mult).then_inc(rope_sin, 1)

                def low(i, t):
                    dve.wait_ge(high_done, 8 * i + t + 1)
                    c, s = t // 4, slice((t % 4) * P, (t % 4 + 1) * P)
                    nc.vector.tensor_tensor(split[:, c, :, 1, s], ps_t[t % 2][:, :].rearrange("p (f n) -> p f n", f=4),
                                            split[:, c, :, 0, s], ALU.subtract).then_inc(low_done, 1)

                def body(i, first, last):
                    for t in range(TILES):
                        rotate(i, t, first)
                        if t:
                            low(i, t - 1)
                        if not last and t in (1, 4):
                            normalise(i + 1, t // 4)
                        if not last and t in (3, 6):
                            scale(i + 1, t // 4, True)
                    low(i, TILES - 1)

                dve.wait_ge(consts_in, 48)
                normalise(0, 0)
                normalise(0, 1)
                scale(0, 0, False)
                scale(0, 1, False)
                body(0, True, False)
                with dve.Fori(1, B - 1) as i:
                    body(i, False, False)
                body(B - 1, False, True)

            @block.scalar
            def _(act):
                def take_x(i, c, first):
                    if not first:
                        act.wait_ge(xnt_done, 5 * i + 2 * c - 2)
                        act.wait_ge(v_mm, 8 * i + 4 * c - 4)
                    act.wait_ge(x_turned, 2 * (2 * i + c) + 2)
                    for k in range(KD):
                        nc.scalar.copy(xs[:, c, k, :], ps_x[k][:, :]).then_inc(xs_done, 1)

                def body(i, first):
                    take_x(i, 0, first)
                    for t in range(TILES):
                        c = t // 4
                        if t % 4 == 0 and not first:
                            act.wait_ge(stored[c], 16 * STORES * i)
                        act.wait_ge(v_mm, 8 * i + t + 1)
                        nc.scalar.copy(v_sb[:, c, t % 4, :], ps_v[t % 2][:, 0:D]).then_inc(v_copied, 1)
                        if t == 2:
                            take_x(i, 1, first)
                        act.wait_ge(qk_turned, 8 * i + t + 1)
                        nc.scalar.copy(split[:, c, :, 0, (t % 4) * P:(t % 4 + 1) * P],
                                       ps_t[t % 2][:, :].rearrange("p (f n) -> p f n", f=4)).then_inc(high_done, 1)

                body(0, True)
                with act.Fori(1, B) as i:
                    body(i, False)

            @block.tensor
            def _(pe):
                def turn_x(i, c, first):
                    pe.wait_ge(xn_done, 8 * i + 4 * c + 4)
                    if c or not first:
                        pe.wait_ge(xs_done, 4 * i + 2 * c)
                    for k in range(KD):
                        for t in range(4):
                            mm = nc.tensor.transpose(ps_x[k][:, t * P:(t + 1) * P], xn[:, c, t, k * P:(k + 1) * P], ident[:, :])
                        mm.then_inc(x_turned, 1)

                def project(i, t, first):
                    c, s = t // 4, slice((t % 4) * P, (t % 4 + 1) * P)
                    if t % 4 == 0:
                        pe.wait_ge(xs_done, 4 * i + 2 * c + 2)
                    if t >= 2 or not first:
                        pe.wait_ge(rope_sin, 8 * i + t - 1)
                        pe.wait_ge(v_copied, 8 * i + t - 1)
                    for k in range(KD):
                        mm = nc.tensor.matmul(ps_qk[t % 2][:, :], xs[:, c, k, s], wqkv[:, k, 0:2 * D], start=(k == 0), stop=(k == KD - 1))
                    mm.then_inc(qk_mm, 1)
                    for k in range(KD):
                        mm = nc.tensor.matmul(ps_v[t % 2][:, 0:D], xs[:, c, k, s], wqkv[:, k, 2 * D:], start=(k == 0), stop=(k == KD - 1))
                    mm.then_inc(v_mm, 1)

                def turn_qk(i, t, first):
                    pe.wait_ge(rope_sum, 8 * i + t + 1)
                    if t >= 2 or not first:
                        pe.wait_ge(low_done, 8 * i + t - 1)
                    for f in range(4):
                        mm = nc.tensor.transpose(ps_t[t % 2][:, f * P:(f + 1) * P], qkr[:, t % 2, f * P:(f + 1) * P], ident[:, :])
                    mm.then_inc(qk_turned, 1)

                def body(i, first):
                    turn_x(i, 0, first)
                    for t in range(TILES):
                        project(i, t, first)
                        if t == 2:
                            turn_x(i, 1, first)
                        if t:
                            turn_qk(i, t - 1, first)
                    turn_qk(i, TILES - 1, first)

                pe.wait_ge(consts_in, 48)
                body(0, True)
                with pe.Fori(1, B) as i:
                    body(i, False)


def global_attention(nc, ident_in, qs_dram, ks_dram, v_dram, o_dram):
    with ExitStack() as ctx:
        sb = lambda n, s, d=F32: ctx.enter_context(nc.sbuf_tensor(n, s, d))
        ps = lambda n, s: ctx.enter_context(nc.psum_tensor(n, s, F32))
        sem = lambda n: ctx.enter_context(nc.semaphore(n))

        NB = 4
        ROWS = SPLIT + 2
        PADDED = 96
        ident = sb("g_ident", [P, P])
        q_st = [[sb(f"q_st{u}{j}", [PADDED, L], F32R) for j in range(2)] for u in range(NB)]
        k_st = [[sb(f"k_st{u}{j}", [PADDED, L], F32R) for j in range(2)] for u in range(NB)]
        v_in = sb("v_in", [P, TILES, P])
        v_st = sb("v_st", [P, TILES, 2 * NB, 2 * G_DIM])
        probs = sb("probs", [P, 4, 2, L])
        maxima = sb("maxima", [P, 2, 2, TILES, 2])
        row_max = sb("row_max", [P, 2, TILES])
        zeros = sb("zeros", [P, 2, TILES])
        max_hl = sb("max_hl", [P, 2, 2, TILES], F32R)
        max_rows = sb("max_rows", [4 * TILES, P])
        o_sb = sb("o_sb", [P, 2, CH])

        ps_st = [ps(f"ps_st{j}", [P, L]) for j in range(2)]
        ps_m = [ps(f"ps_m{k}", [P, CH]) for k in range(3)]
        ps_o = ps("ps_o", [P, CH])

        pool_passed = sem("g_pool_passed")
        ident_loaded = sem("g_ident_loaded")
        ones_set = sem("ones_set")
        qk_in = [sem(f"qk_in{u}") for u in range(NB)]
        v_loaded = sem("v_loaded")
        v_placed = sem("v_placed")
        rows_zeroed = sem("rows_zeroed")
        m_ready = sem("m_ready")
        m_used = sem("m_used")
        max_found = sem("max_found")
        max_high = sem("max_high")
        split_done = sem("split_done")
        turned = sem("turned_maxima")
        rows_out = sem("rows_out")
        rows_in = [sem(f"rows_in{u}") for u in range(NB)]
        st_ready = sem("st_ready")
        exp_done = sem("exp_done")
        pv_done = sem("pv_done")
        o_copied = sem("o_copied")
        o_stored = [sem(f"o_stored{c}") for c in range(2)]

        HALF = 2 * TILES
        USES = 2 * HALF
        LEAD = USES + HALF
        M_BANKS = 3
        TURN = 6
        ITERS = UNITS // NB

        def place(base, k):
            return (base + HALF + k) % USES if isinstance(base, int) else k

        def bank(base, k):
            return ps_m[place(base, k) % M_BANKS]

        def before(base, k):
            return USES % M_BANKS if place(base, k) < USES % M_BANKS else M_BANKS

        with nc.Block() as block:

            @block.sync
            def _(sp):
                def load(i, u):
                    for j in range(2):
                        head = 2 * u + j
                        src = qs_dram[bass.ds(i, 1), head, :, :, :].rearrange("o s d n -> (o s d) n")
                        sp.dma_start(q_st[u][j][0:SPLIT, :].bitcast(F32),
                                     src.unsqueeze(0).broadcast_to([2, 2 * G_DIM, L])).then_inc(qk_in[u], 16)
                        for s in range(2):
                            src = ks_dram[bass.ds(i, 1), head, s, :, :].rearrange("o d n -> (o d) n")
                            sp.dma_start(k_st[u][j][2 * s * G_DIM:2 * (s + 1) * G_DIM, :].bitcast(F32),
                                         src.unsqueeze(0).broadcast_to([2, G_DIM, L])).then_inc(qk_in[u], 16)

                def load_v(i):
                    sp.dma_start(v_in[:, :, :], v_dram[bass.ds(i, 1), :, :, :].rearrange("o t p n -> p (o t) n")).then_inc(v_loaded, 16)

                def place_rows(i, u):
                    sp.wait_ge(rows_out, NB * i + u + 1)
                    for j in range(2):
                        sp.dma_start(q_st[u][j][SPLIT:ROWS, :].bitcast(F32),
                                     max_rows[j * 2 * TILES:(j + 1) * 2 * TILES, :]).then_inc(rows_in[u], 16)

                def store_o(i, u):
                    sp.wait_ge(o_copied, NB * i + u + 1)
                    dst = o_dram[bass.ds(NB * i + u, 1), :, :].rearrange("o p n -> (o p) n")
                    sp.dma_start(dst, o_sb[:, u % 2, :]).then_inc(o_stored[u % 2], 16)

                def body(i, first, last):
                    for u in range(NB):
                        if u:
                            store_o(i, u - 1)
                        elif not first:
                            store_o(i - 1, NB - 1)
                        if u < NB - 1:
                            place_rows(i, u + 1)
                        elif not last:
                            place_rows(i + 1, 0)
                        if not last:
                            if u == 0:
                                sp.wait_ge(v_placed, TILES * (i + 1))
                                load_v(i + 1)
                            sp.wait_ge(st_ready, 2 * TILES * (NB * i + u) + 2 * TILES)
                            load(i + 1, u)
                    if last:
                        store_o(i, NB - 1)

                sp.dma_start(ident[:, :], ident_in).then_inc(ident_loaded, 16)
                for u in range(NB):
                    load(0, u)
                load_v(0)
                place_rows(0, 0)
                body(0, True, False)
                with sp.Fori(1, ITERS - 1) as i:
                    body(i, False, False)
                body(ITERS - 1, False, True)
                for c in range(2):
                    sp.wait_ge(o_stored[c], UNITS // 2 * 16)

            @block.gpsimd
            def _(pool):
                nc.gpsimd.memset(zeros[:, :, :], 0.0).then_inc(ones_set, 1)
                pool.wait_ge(ones_set, 1)
                for u in range(NB):
                    for j in range(2):
                        nc.gpsimd.memset(k_st[u][j][SPLIT:PADDED, :].bitcast(F32), -1.0).then_inc(ones_set, 1)
                pool.wait_ge(ones_set, 2 * NB + 1)
                for cols in (slice(0, 1), slice(1 + G_DIM, 2 * G_DIM)):
                    nc.gpsimd.memset(v_st[:, :, :, cols], 1.0).then_inc(ones_set, 1)

                def zero_rows(u, end):
                    for j in range(2):
                        nc.gpsimd.memset(q_st[u][j][SPLIT:end, :].bitcast(F32), 0.0).then_inc(rows_zeroed, 1)

                def place_v(i, kt):
                    pool.wait_ge(v_loaded, 16 * i + 16)
                    apart(pool, pool_passed)
                    nc.gpsimd.tensor_copy(v_st[:, kt, :, 1:1 + G_DIM], v_in[:, kt, :].rearrange("p (e n) -> p e n", n=G_DIM)).then_inc(v_placed, 1)

                def split_maxima(n):
                    pool.wait_ge(max_found, n + 1)
                    if not isinstance(n, int) or n:
                        pool.wait_ge(turned, n)
                    nc.gpsimd.tensor_tensor(max_hl[:, :, 0, :], row_max[:, :, :], zeros[:, :, :], ALU.add).then_inc(max_high, 1)
                    pool.wait_ge(max_high, n + 1)
                    nc.gpsimd.tensor_tensor(max_hl[:, :, 1, :], row_max[:, :, :], max_hl[:, :, 0, :], ALU.subtract).then_inc(split_done, 1)

                def body(i, last):
                    for u in range(NB):
                        n = NB * i + u
                        if not last or u + 1 < NB:
                            pool.wait_ge(rows_zeroed, 2 * UNITS if last else 2 * (NB + n))
                            pool.wait_ge(v_placed, TILES * (i + 1))
                            split_maxima(n + 1)
                        if not last:
                            if u == NB - 1:
                                for kt in range(TILES - 1):
                                    pool.wait_ge(pv_done, TILES * n + kt + 1)
                                    place_v(i + 1, kt)
                            pool.wait_ge(st_ready, 2 * TILES * n + 2 * TILES)
                            pool.wait_ge(split_done, n + 2)
                            if u == NB - 1:
                                pool.wait_ge(v_placed, TILES * (i + 2) - 1)
                            apart(pool, pool_passed)
                            zero_rows(u, ROWS)
                            if u == NB - 1:
                                pool.wait_ge(pv_done, TILES * n + TILES)
                                pool.wait_ge(rows_zeroed, 2 * (NB + n + 1))
                                place_v(i + 1, TILES - 1)

                pool.wait_ge(ones_set, 2 * NB + 3)
                for u in range(NB):
                    zero_rows(u, PADDED)
                pool.wait_ge(rows_zeroed, 2 * NB)
                for kt in range(TILES):
                    place_v(0, kt)
                split_maxima(0)
                body(0, False)
                with pool.Fori(1, ITERS - 1) as i:
                    body(i, False)
                body(ITERS - 1, True)

            @block.tensor
            def _(pe):
                def maxima_scores(base, use, u, qt, j, h):
                    if not isinstance(base, int) or base + use >= M_BANKS:
                        pe.wait_ge(m_used, base + use + 1 - before(base, use))
                    nc.tensor.matmul(bank(base, use)[:, :], q_st[u][j][:, qt * P:(qt + 1) * P],
                                     k_st[u][j][:, h * CH:(h + 1) * CH], start=True, stop=True).then_inc(m_ready, 1)

                def operands_in(i, u):
                    pe.wait_ge(qk_in[u], 96 * i + 96)
                    pe.wait_ge(rows_zeroed, 2 * (NB * i + u) + 2)

                def half_maxima(base, k, i, u, half):
                    if half == 0:
                        operands_in(i, u)
                    for n in range(HALF):
                        maxima_scores(base, k + n, u, 4 * half + n // 4, n // 2 % 2, n % 2)

                def turn_maxima(n, kt):
                    pe.wait_ge(split_done, n + 2)
                    if not isinstance(n, int) or n >= 0:
                        pe.wait_ge(exp_done, 2 * TILES * n + 2 * kt - 1)
                    nc.tensor.transpose(ps_st[0][0:4 * TILES, 0:P], max_hl[:, :, :, :].rearrange("p a b c -> p (a b c)").bitcast(F32),
                                        ident[:, :]).then_inc(turned, 1)

                def scores(n, kt, u, j, more):
                    g = 2 * TILES * n + 2 * kt + j
                    if not isinstance(n, int) or g >= 2:
                        pe.wait_ge(exp_done, g - 1)
                    if kt == TURN and j == 0 and more:
                        pe.wait_ge(rows_out, n + 2)
                    for h in range(2):
                        mm = nc.tensor.matmul(ps_st[j][:, h * CH:(h + 1) * CH], k_st[u][j][:, kt * P:(kt + 1) * P],
                                              q_st[u][j][:, h * CH:(h + 1) * CH], start=True, stop=True)
                    mm.then_inc(st_ready, 1)

                def product(n, kt, u):
                    pe.wait_ge(exp_done, 2 * TILES * n + 2 * kt + 2)
                    if kt == 0 and (not isinstance(n, int) or n):
                        pe.wait_ge(o_copied, n)
                    for j in range(2):
                        for h in range(2):
                            r = 32 * (2 * j + h)
                            mm = nc.tensor.matmul(ps_o[r:r + 32, :], v_st[:, kt, 2 * u + j, :],
                                                  probs[:, kt % 4, j, h * CH:(h + 1) * CH], start=(kt == 0), stop=(kt == TILES - 1))
                    mm.then_inc(pv_done, 1)

                def body(i, first, last):
                    for u in range(NB):
                        n = NB * i + u
                        base = LEAD + USES * n
                        i1, u1 = (i, u + 1) if u + 1 < NB else (i + 1, 0)
                        i2, u2 = (i, u + 2) if u + 2 < NB else (i + 1, u + 2 - NB)
                        more1, more2 = not last or u + 1 < NB, not last or u + 2 < NB
                        pe.wait_ge(rows_in[u], 32 * i + 32)
                        for kt in range(TILES):
                            if kt < 4:
                                m = [(4 * kt + e, u1, 4 + kt, e // 2, e % 2) for e in range(4)] if more1 else []
                            else:
                                m = [(HALF + 4 * (kt - 4) + e, u2, kt - 4, e // 2, e % 2) for e in range(4)] if more2 else []
                                if kt == 4 and more2:
                                    operands_in(i2, u2)
                            if kt == TURN and more1:
                                turn_maxima(n, kt)
                            for j in range(2):
                                if m:
                                    maxima_scores(base, *m[j])
                                scores(n, kt, u, j, more1)
                            if m:
                                maxima_scores(base, *m[2])
                            if u == (1 if kt == 0 else 0):
                                pe.wait_ge(v_placed, TILES * i + (kt - 1) % TILES + 1)
                            if kt:
                                product(n, kt - 1, u)
                            elif u:
                                product(n - 1, TILES - 1, u - 1)
                            elif not first:
                                product(n - 1, TILES - 1, NB - 1)
                            if m:
                                maxima_scores(base, *m[3])
                        if last and u == NB - 1:
                            product(n, TILES - 1, u)

                pe.wait_ge(ident_loaded, 16)
                pe.wait_ge(ones_set, 2 * NB + 3)
                for half in range(2):
                    half_maxima(0, HALF * half, 0, 0, half)
                turn_maxima(-1, 0)
                half_maxima(0, USES, 0, 1, 0)
                body(0, True, False)
                with pe.Fori(1, ITERS - 1) as i:
                    body(i, False, False)
                body(ITERS - 1, False, True)

            @block.vector
            def _(dve):
                def take_maxima(base, k, par, tile, count=1):
                    for e in range(4 * count):
                        dve.wait_ge(m_ready, base + k + e + 1)
                        nc.vector.tensor_reduce(maxima[:, par, e // 2 % 2, tile + e // 4, e % 2:e % 2 + 1], bank(base, k + e)[:, :],
                                                AX_X, ALU.max).then_inc(m_used, 1)

                def join_maxima(n, par, uses):
                    dve.wait_ge(m_used, uses)
                    if not isinstance(n, int) or n:
                        dve.wait_ge(split_done, n)
                    nc.vector.tensor_reduce(row_max[:, :, :], maxima[:, par, :, :, :], AX_X, ALU.max).then_inc(max_found, 1)

                def body(i, last):
                    for u in range(NB):
                        n = NB * i + u
                        base = LEAD + USES * n
                        if not last or u + 1 < NB:
                            take_maxima(base, 0, (u + 1) % 2, 4, 4)
                        if not last or u + 2 < NB:
                            take_maxima(base, HALF, u % 2, 0)
                        if not last or u + 1 < NB:
                            join_maxima(n + 1, (u + 1) % 2, base + HALF)
                        if not last or u + 2 < NB:
                            take_maxima(base, HALF + 4, u % 2, 1, 3)

                take_maxima(0, 0, 0, 0, 8)
                join_maxima(0, 0, USES)
                take_maxima(0, USES, 1, 0, 4)
                body(0, False)
                with dve.Fori(1, ITERS - 1) as i:
                    body(i, False)
                body(ITERS - 1, True)

            @block.scalar
            def _(act):
                def take_rows(n, i, u):
                    act.wait_ge(turned, n + 1)
                    if u:
                        act.wait_ge(rows_in[u - 1], 32 * i + 32)
                    elif not isinstance(i, int) or i:
                        act.wait_ge(rows_in[NB - 1], 32 * i)
                    nc.scalar.copy(max_rows[:, :], ps_st[0][0:4 * TILES, 0:P]).then_inc(rows_out, 1)

                def copy_o(n, i, u):
                    act.wait_ge(pv_done, TILES * (n + 1))
                    if not isinstance(i, int) or 2 * i + u // 2:
                        act.wait_ge(o_stored[u % 2], 16 * (2 * i + u // 2))
                    nc.scalar.copy(o_sb[:, u % 2, :], ps_o[:, :]).then_inc(o_copied, 1)

                def body(i, first, last):
                    for u in range(NB):
                        n = NB * i + u
                        for kt in range(TILES):
                            for j in range(2):
                                act.wait_ge(st_ready, 2 * TILES * n + 2 * kt + j + 1)
                                if not isinstance(n, int) or TILES * n + kt >= 4:
                                    act.wait_ge(pv_done, TILES * n + kt - 3)
                                nc.scalar.activation(probs[:, kt % 4, j, :], ps_st[j][:, :], ACT.Exp,
                                                     scale=float(G_DIM) ** -0.5).then_inc(exp_done, 1)
                            if kt == TURN - 1 and (not last or u + 1 < NB):
                                take_rows(n + 1, i if u + 1 < NB else i + 1, (u + 1) % NB)
                            if kt == 0:
                                if u:
                                    copy_o(n - 1, i, u - 1)
                                elif not first:
                                    copy_o(n - 1, i - 1, NB - 1)
                    if last:
                        copy_o(NB * i + NB - 1, i, NB - 1)

                take_rows(0, 0, 0)
                body(0, True, False)
                with act.Fori(1, ITERS - 1) as i:
                    body(i, False, False)
                body(ITERS - 1, False, True)


DEPTH = 2
HEADS, HDIM = 8, 64
INNER = HEADS * HDIM
HID = int(D * 4 * 2 / 3)
CHUNKS = B * L // CH
WPC = CH // P
WINDOWS = CHUNKS * WPC
FT = HID // P
TAIL = HID - FT * P
TAIL_AT = 64
LAST = DEPTH * CHUNKS
QK_SCALE = 8.0
MASKED = -3.0e38


class Weights:

    def __init__(self, ctx, nc, wqkv, wo, ln_g, ln_b, w1, b1, w2, b2, mask_in, ident_in):
        sb = lambda n, s, d=F32: ctx.enter_context(nc.sbuf_tensor(n, s, d))
        per = lambda n, s: [sb(f"{n}{l}", s) for l in range(DEPTH)]
        sem = lambda n: ctx.enter_context(nc.semaphore(n))
        self.dram = dict(wqkv=wqkv, wo=wo, ln_g=ln_g, ln_b=ln_b, w1=w1, b1=b1, w2=w2, b2=b2, mask=mask_in, ident=ident_in)
        self.wqkv = [sb(f"wqkv_{n}", [P, KD, 3 * INNER], F32R) for n in ("high", "low")]
        self.w1 = [sb(f"w1_{n}", [P, KD, (2 * FT + 1) * P], F32R) for n in ("high", "low")]
        self.wo = sb("wo_l", [P, INNER // P, D])
        self.w2 = sb("w2_l", [P, FT + 1, D])
        self.lnp = per("lnp_l", [P, 2, KD])
        self.b1 = per("b1_l", [P, 2, FT + 1])
        self.b2 = per("b2_l", [P, KD])
        self.mask = sb("l_mask", [P, 4, P])
        self.ident = sb("l_ident", [P, P])
        self.mean_w = sb("mean_w", [P, P])
        self.parity = sb("parity", [P, 2])
        self.wqkv_dram = nc.dram_tensor("wqkv_raw", (DEPTH, D, 3 * INNER), F32, kind="Internal").ap()
        self.w1_dram = nc.dram_tensor("w1_raw", (DEPTH, D, 2 * HID), F32, kind="Internal").ap()
        self.raw = sem("raw")
        self.set = sem("w_set")
        self.small_in = sem("small_in")
        self.wqkv_in, self.wo_in, self.w1_in, self.w2_in = sem("wqkv_in"), sem("wo_in"), sem("w1_in"), sem("w2_in")

    SETS = 6
    SMALLS = 16 * (3 + 7 * DEPTH)
    W1_LOADS, W2_LOADS = 16 * 4 * KD, 16 * 2

    def clear(self, nc):
        nc.gpsimd.memset(self.w1[1][:, :, 2 * FT * P:].bitcast(F32), 0.0).then_inc(self.set, 1)
        nc.gpsimd.memset(self.w2[:, FT, :], 0.0).then_inc(self.set, 1)
        for l in range(DEPTH):
            nc.gpsimd.memset(self.b1[l][:, :, FT:], 0.0).then_inc(self.set, 1)
        nc.gpsimd.memset(self.mean_w[:, :], 1.0 / D).then_inc(self.set, 1)
        nc.gpsimd.memset(self.parity[:, 0:1], 0.0)
        nc.gpsimd.memset(self.parity[:, 1:2], 1.0).then_inc(self.set, 1)

    def copy_raw(self, sp):
        sp.dma_start(self.wqkv_dram, self.dram["wqkv"]).then_inc(self.raw, 16)
        sp.dma_start(self.w1_dram, self.dram["w1"]).then_inc(self.raw, 16)

    def load_wqkv(self, sp, l):
        sp.dma_start(self.wqkv[1][:, :, :].bitcast(F32), self.wqkv_dram[l].rearrange("(k p) n -> p k n", p=P)).then_inc(self.wqkv_in, 16)

    def load_wo(self, sp, l):
        sp.dma_start(self.wo[:, :, :], self.dram["wo"][l].rearrange("(k p) n -> p k n", p=P)).then_inc(self.wo_in, 16)

    def load_w1(self, sp, l):
        for k in range(KD):
            rows = self.w1_dram[l, k * P:(k + 1) * P, :]
            dst = self.w1[1][:, k, :].bitcast(F32)
            for to, start, n in ((0, HID, FT * P), (FT * P, 0, FT * P), (2 * FT * P, HID + FT * P, TAIL), (2 * FT * P + TAIL_AT, FT * P, TAIL)):
                sp.dma_start(dst[:, to:to + n], rows[:, start:start + n]).then_inc(self.w1_in, 16)

    def load_w2(self, sp, l):
        w2 = self.dram["w2"]
        sp.dma_start(self.w2[:, 0:FT, :], w2[l, 0:FT * P, :].rearrange("(k p) n -> p k n", p=P)).then_inc(self.w2_in, 16)
        sp.dma_start(self.w2[TAIL_AT:TAIL_AT + TAIL, FT, :], w2[l, FT * P:, :]).then_inc(self.w2_in, 16)

    def load_small(self, nc, sp):
        get = lambda dst, src: sp.dma_start(dst, src).then_inc(self.small_in, 16)
        b1, b2, ln_g, ln_b = (self.dram[n] for n in ("b1", "b2", "ln_g", "ln_b"))
        get(self.ident[:, :], self.dram["ident"])
        get(self.mask[:, 0:2, :], self.dram["mask"][0:2].rearrange("s p n -> p s n"))
        get(self.mask[:, 3, :], self.dram["mask"][2])
        with nc.allow_non_contiguous_dma(reason="a bias has one element for a partition"):
            for l in range(DEPTH):
                get(self.b1[l][:, 0, 0:FT], b1[l, 0:FT * P].rearrange("(k p) -> p k", p=P))
                get(self.b1[l][:, 1, 0:FT], b1[l, HID:HID + FT * P].rearrange("(k p) -> p k", p=P))
                get(self.b1[l][TAIL_AT:TAIL_AT + TAIL, 0, FT:FT + 1], b1[l, FT * P:HID].rearrange("(p o) -> p o", o=1))
                get(self.b1[l][0:TAIL, 1, FT:FT + 1], b1[l, HID + FT * P:].rearrange("(p o) -> p o", o=1))
                get(self.b2[l][:, :], b2[l].rearrange("(k p) -> p k", p=P))
                get(self.lnp[l][:, 0, :], ln_g[l].rearrange("(k p) -> p k", p=P))
                get(self.lnp[l][:, 1, :], ln_b[l].rearrange("(k p) -> p k", p=P))


def local_layers(nc, wt, xpos, q_scale, k_scale, xnt):
    with ExitStack() as ctx:
        sb = lambda n, s, d=F32: ctx.enter_context(nc.sbuf_tensor(n, s, d))
        ps = lambda n: ctx.enter_context(nc.psum_tensor(n, [P, CH], F32))
        sem = lambda n: ctx.enter_context(nc.semaphore(n))

        tables = [sb(f"tables{l}", [P, TILES, 4, HDIM]) for l in range(DEPTH)]
        scales = sb("scales", [P, DEPTH, 2, HDIM])
        h = [sb(f"h_{n}", [P, KD, CH], F32R) for n in ("high", "low")]
        v_ring = sb("v_ring", [P, WPC, INNER])
        k_ring = sb("k_ring", [P, HEADS // 2, WPC * P])
        q_pad = [sb(f"q_pad{j}", [P, HEADS // 2, P]) for j in range(2)]
        rope_a = sb("rope_a", [P, 2, INNER])
        rope_b = sb("rope_b", [P, 2, INNER])
        qk_n = sb("qk_n", [P, 2, INNER])
        sumsq = sb("sumsq", [P, 2 * HEADS])
        clipped = sb("clipped", [P, 2 * HEADS])
        halves = sb("halves", [P, 2 * HEADS])
        inv_norm = sb("inv_norm", [P, 2 * HEADS])
        probs = sb("l_probs", [P, HEADS, 2 * P])
        neg_max = sb("l_neg_max", [P, HEADS])
        total = sb("l_total", [P, HEADS])
        inv_total = sb("l_inv_total", [P, HEADS])
        p_turned = sb("p_turned", [P, 2, 2, 2, P])
        o_ring = sb("o_ring", [P, 2, HEADS // 2, CH])
        mid = sb("mid", [P, KD, 1 + CH])
        f_high, f_low = (sb(f"f_{n}", [P, KD, CH], F32R) for n in ("high", "low"))
        dev = sb("dev", [P, CH])
        gate = sb("gate", [P, 2, CH])
        hidden = sb("hidden", [P, FT + 1, CH])
        centred = hidden[:, KD:2 * KD, :]
        eps_col = sb("eps_col", [P, 1])

        ps_q, ps_k, ps_v, ps_o = ps("ps_q"), ps("ps_k"), ps("ps_v"), ps("l_ps_o")
        ring = [ps(f"ring{b}") for b in range(2)]
        ffn = [ps(f"ffn{b}") for b in range(2)]

        dve_passed, pool_passed = sem("l_dve_passed"), sem("l_pool_passed")
        cleared = sem("cleared")
        mask_picked = sem("mask_picked")
        tables_in = sem("tables_in")
        tables_done = sem("tables_done")
        wqkv_high, wqkv_low = sem("wqkv_high"), sem("wqkv_low")
        w1_high, w1_low = sem("w1_high"), sem("w1_low")
        h_high = sem("h_high")
        h_ready = sem("h_ready")
        q_mm, k_mm, v_mm = sem("q_mm"), sem("k_mm"), sem("l_v_mm")
        squared = sem("squared")
        v_out = sem("v_out")
        cos_done = sem("cos_done")
        sums_done = sem("sums_done")
        roped = sem("l_roped")
        clip_done = sem("clip_done")
        inv_done = sem("inv_done")
        added = sem("added")
        qk_ready = sem("qk_ready")
        ring_ready = [sem(f"ring_ready{b}") for b in range(2)]
        ring_taken = [sem(f"ring_taken{b}") for b in range(2)]
        exp_done = sem("l_exp_done")
        inv_total_done = sem("inv_total_done")
        p_ready = sem("p_ready")
        pv_mm = sem("pv_mm")
        o_out = sem("o_out")
        ffn_ready = [sem(f"ffn_ready{b}") for b in range(2)]
        ffn_taken = [sem(f"ffn_taken{b}") for b in range(2)]
        carried = sem("carried")
        sq_dev = sem("sq_dev")
        ln_done = sem("ln_done")
        dev_done = sem("dev_done")
        scaled = sem("l_scaled")
        shifted_done = sem("shifted_done")
        f_high_done = sem("f_high_done")
        normed = sem("normed")
        tail_gated = sem("tail_gated")
        x_out = sem("x_out")

        PT, TQ, TK, SC = 0, 4, 5, 6

        def ring_use(W, r):
            return 5 * W - 7 + r // 2

        USES = (9, 8)
        WO, MEAN, GATE, W2 = 0, 1, 2, 7
        TAILS = 7

        PLAN = ((0, 0, None, ("wqkv", 0)), (1, 0, None, None), (2, 0, 0, ("w1", 0)), ((3, CHUNKS), 0, 0, None),
                ((CHUNKS, CHUNKS + 2), 1, 0, ("wqkv", 1)), ((CHUNKS + 2, LAST), 1, 1, ("w1", 1)), (LAST, None, 1, None),
                (LAST + 1, None, 1, None))

        def run(eng, body, prepare=None):
            for g, la, lf, weights in PLAN:
                if weights and prepare:
                    prepare(*weights)
                if isinstance(g, int):
                    body(g, la, lf)
                else:
                    with eng.Fori(*g) as i:
                        body(i, la, lf)

        def parts(g, w):
            if not isinstance(g, int):
                return True, True, True
            W = WPC * g + w
            n = WPC * LAST
            return W < n, 1 <= W <= n, 2 <= W <= n + 1

        CLEARED = 8
        EXP_LN = "natural_log_exp_and_others"
        THREE = [(k, a, b) for k in range(KD) for a, b in ((0, 0), (0, 1), (1, 0))]
        with nc.Block() as block:

            @block.gpsimd
            def _(pool):
                nc.gpsimd.memset(halves[:, :], -0.5).then_inc(cleared, 1)
                nc.gpsimd.memset(v_ring[:, WPC - 1, :], 0.0).then_inc(cleared, 1)
                nc.gpsimd.memset(k_ring[:, :, (WPC - 1) * P:], 0.0).then_inc(cleared, 1)
                for j in range(2):
                    nc.gpsimd.memset(q_pad[j][:, :, :], 0.0).then_inc(cleared, 1)
                nc.gpsimd.memset(mid[:, :, :], 0.0).then_inc(cleared, 1)
                nc.gpsimd.memset(hidden[:, FT, :], 0.0).then_inc(cleared, 1)
                nc.gpsimd.memset(eps_col[:, :], EPS).then_inc(cleared, 1)
                pool.wait_ge(cleared, CLEARED)

                def body(g, la, lf):
                    for w in range(WPC):
                        W = WPC * g + w
                        if not parts(g, w)[0]:
                            continue
                        pool.wait_ge(sums_done, W + 1)
                        apart(pool, pool_passed)
                        nc.gpsimd.tensor_scalar(clipped[:, :], sumsq[:, :], 1e-24, None, ALU.max).then_inc(clip_done, 1)
                        pool.wait_ge(clip_done, W + 1)
                        nc.gpsimd.tensor_tensor(inv_norm[:, :], clipped[:, :], halves[:, :], ALU.pow).then_inc(inv_done, 1)
                        pool.wait_ge(roped, W + 1)
                        nc.gpsimd.tensor_tensor(rope_a[:, :, :], rope_a[:, :, :], rope_b[:, :, :], ALU.add).then_inc(added, 1)
                        pool.wait_ge(inv_done, W + 1)
                        pool.wait_ge(added, W + 1)
                        if not isinstance(g, int) or W:
                            pool.wait_ge(ring_ready[TK % 2], ring_use(W, TK) + 1)
                        nc.gpsimd.tensor_tensor(qk_n[:, :, :].rearrange("p s (h n) -> p (s h) n", n=HDIM),
                                                rope_a[:, :, :].rearrange("p s (h n) -> p (s h) n", n=HDIM),
                                                inv_norm[:, :].unsqueeze(2).broadcast_to([P, 2 * HEADS, HDIM]),
                                                ALU.mult).then_inc(qk_ready, 1)

                run(pool, body)

            @block.tensor
            def _(pe):
                def project(g, w, la):
                    W = WPC * g + w
                    if w == 0:
                        pe.wait_ge(h_ready, KD * (g + 1))
                    for n, (bank, done, free) in enumerate(((ps_q, q_mm, roped), (ps_k, k_mm, roped), (ps_v, v_mm, v_out))):
                        if not isinstance(g, int) or W:
                            pe.wait_ge(free, W)
                        for e, (k, a, b) in enumerate(THREE):
                            mm = nc.tensor.matmul(bank[:, :], h[a][:, k, w * P:(w + 1) * P], wt.wqkv[b][:, k, n * INNER:(n + 1) * INNER],
                                                  start=(e == 0), stop=(e == len(THREE) - 1))
                        mm.then_inc(done, 1)

                def ring_wait(W, r):
                    if not isinstance(W, int) or ring_use(W, r) > 0:
                        pe.wait_ge(ring_taken[r % 2], ring_use(W, r))

                def turn_probs(W, p):
                    pe.wait_ge(p_ready, 4 * (W - 2) + p + 1)
                    ring_wait(W, PT + p)
                    for j in range(2):
                        for s in range(2):
                            mm = nc.tensor.transpose(ring[(PT + p) % 2][:, (2 * j + s) * P:(2 * j + s + 1) * P],
                                                     probs[:, 2 * p + j, s * P:(s + 1) * P], wt.ident[:, :])
                    mm.then_inc(ring_ready[(PT + p) % 2], 1)

                def values(W, w, p):
                    ws = (w - 2) % WPC
                    pe.wait_ge(ring_taken[(PT + p) % 2], ring_use(W, PT + p) + 1)
                    if p == 0 and (not isinstance(W, int) or W > 2):
                        pe.wait_ge(o_out, W - 2)
                    for s, slot in enumerate(((ws - 1) % WPC, ws)):
                        for j in range(2):
                            head = 2 * p + j
                            mm = nc.tensor.matmul(ps_o[j * HDIM:(j + 1) * HDIM, p * P:(p + 1) * P],
                                                  v_ring[:, slot, head * HDIM:(head + 1) * HDIM], p_turned[:, p % 2, j, s, :],
                                                  start=(s == 0), stop=(s == 1))
                    if p == HEADS // 2 - 1:
                        mm.then_inc(pv_mm, 1)

                def turn_qk(W):
                    pe.wait_ge(qk_ready, W)
                    for s, r in ((0, TQ), (1, TK)):
                        ring_wait(W, r)
                        for p in range(HEADS // 2):
                            mm = nc.tensor.transpose(ring[r % 2][:, p * P:(p + 1) * P], qk_n[:, s, p * P:(p + 1) * P], wt.ident[:, :])
                        mm.then_inc(ring_ready[r % 2], 1)

                def scores(W, w):
                    ws = (w - 1) % WPC
                    pe.wait_ge(ring_taken[TQ % 2], ring_use(W, TQ) + 1)
                    pe.wait_ge(ring_taken[TK % 2], ring_use(W, TK) + 1)
                    for p in range(HEADS // 2):
                        r = SC + p
                        ring_wait(W, r)
                        for j in range(2):
                            out = ring[r % 2][:, 2 * j * P:(2 * j + 2) * P]
                            if ws:
                                mm = nc.tensor.matmul(out, q_pad[j][:, p, :], k_ring[:, p, (ws - 1) * P:(ws + 1) * P], start=True, stop=True)
                            else:
                                nc.tensor.matmul(out[:, 0:P], q_pad[j][:, p, :], k_ring[:, p, (WPC - 1) * P:], start=True, stop=True)
                                mm = nc.tensor.matmul(out[:, P:], q_pad[j][:, p, :], k_ring[:, p, 0:P], start=True, stop=True)
                        mm.then_inc(ring_ready[r % 2], 1)

                def ffn_fill(g, bank, use, operands):
                    if not isinstance(g, int) or (g - 2) * USES[bank] + use > 0:
                        pe.wait_ge(ffn_taken[bank], (g - 2) * USES[bank] + use)
                    for n, (a, b) in enumerate(operands):
                        mm = nc.tensor.matmul(ffn[bank][:, :], a, b, start=(n == 0), stop=(n == len(operands) - 1))
                    mm.then_inc(ffn_ready[bank], 1)

                def output_product(g, lf):
                    pe.wait_ge(o_out, WPC * (g - 1))
                    for m in range(KD):
                        ffn_fill(g, m, WO, [(wt.wo[:, p, m * P:(m + 1) * P], o_ring[:, bass.ds(g % 2, 1), p, :].rearrange("p o n -> p (o n)"))
                                            for p in range(HEADS // 2)])

                def shifted(src):
                    return src[:, 0, 1:], src[:, 1, 0:CH]

                def mean(g):
                    for m in range(KD):
                        pe.wait_ge(ffn_taken[m], (g - 2) * USES[m] + WO + 1)
                    ffn_fill(g, 0, MEAN, [(wt.mean_w[:, :], x) for x in shifted(mid)])

                def variance(g):
                    pe.wait_ge(sq_dev, g - 1)
                    ffn_fill(g, 1, MEAN, [(wt.mean_w[:, :], hidden[:, k, :]) for k in range(KD)])

                def hidden_tile(g, lf, f):
                    if f == 0:
                        pe.wait_ge(normed, KD * (g - 1))
                    for bank in range(2):
                        c = (bank * FT + f) * P
                        ffn_fill(g, bank, GATE + f, [(wt.w1[a][:, k, c:c + P], (f_high, f_low)[b][:, k, :]) for k, a, b in THREE])

                def tails(g, lf):
                    ffn_fill(g, 0, TAILS, [(wt.w1[a][:, k, 2 * FT * P:], (f_high, f_low)[b][:, k, :]) for k, a, b in THREE])

                def down(g, lf, m):
                    pe.wait_ge(ffn_taken[1], (g - 2) * USES[1] + GATE + FT)
                    pe.wait_ge(ffn_taken[0], (g - 2) * USES[0] + TAILS + 1)
                    ffn_fill(g, 1 - m, W2 + m, [(wt.w2[:, f, m * P:(m + 1) * P], hidden[:, f, :]) for f in range(FT + 1)])

                def body(g, la, lf):
                    for w in range(WPC):
                        W = WPC * g + w
                        new, mid_, old = parts(g, w)
                        forward = lf is not None
                        if new:
                            project(g, w, la)
                        if old:
                            turn_probs(W, 0)
                            turn_probs(W, 1)
                        if forward and w == 0:
                            output_product(g, lf)
                        if forward and w == 2:
                            hidden_tile(g, lf, 1)
                        if forward and w == 3:
                            hidden_tile(g, lf, 4)
                        if old:
                            values(W, w, 0)
                            turn_probs(W, 2)
                            values(W, w, 1)
                            turn_probs(W, 3)
                            values(W, w, 2)
                        if mid_:
                            turn_qk(W)
                        if old:
                            values(W, w, 3)
                        if forward and w == 0:
                            mean(g)
                        if forward and w == 2:
                            hidden_tile(g, lf, 2)
                        if forward and w == 3:
                            tails(g, lf)
                        if mid_:
                            scores(W, w)
                        if forward and w == 0:
                            variance(g)
                        if forward and w == 1:
                            hidden_tile(g, lf, 0)
                        if forward and w == 2:
                            hidden_tile(g, lf, 3)
                        if forward and w == 3:
                            down(g, lf, 0)
                            down(g, lf, 1)

                def prepare(name, l):
                    if name == "wqkv":
                        pe.wait_ge(wqkv_low, l + 1)
                    else:
                        pe.wait_ge(w1_low, l + 1)
                        pe.wait_ge(wt.wo_in, 16 * (l + 1))
                        pe.wait_ge(wt.w2_in, wt.W2_LOADS * (l + 1))

                pe.wait_ge(cleared, CLEARED)
                pe.wait_ge(wt.small_in, wt.SMALLS)
                run(pe, body, prepare)

            @block.sync
            def _(sp):
                for l in range(DEPTH):
                    sp.dma_start(tables[l][:, :, :, :], xpos.rearrange("(t p) s n -> p t s n", p=P)).then_inc(tables_in, 16)
                for s, scale in enumerate((q_scale, k_scale)):
                    sp.dma_start(scales[:, :, s, :], scale.unsqueeze(0).broadcast_to([P, DEPTH, HDIM])).then_inc(tables_in, 16)
                sp.wait_ge(v_mm, WPC * CHUNKS)
                wt.load_wqkv(sp, 1)
                for m in range(KD):
                    sp.wait_ge(ffn_ready[m], (CHUNKS - 1) * USES[m] + WO + 1)
                wt.load_wo(sp, 1)
                sp.wait_ge(ffn_ready[0], (CHUNKS - 1) * USES[0] + TAILS + 1)
                wt.load_w1(sp, 1)
                for m in range(KD):
                    sp.wait_ge(ffn_ready[1 - m], (CHUNKS - 1) * USES[1 - m] + W2 + m + 1)
                wt.load_w2(sp, 1)

            @block.scalar
            def _(act):
                def head_squares(W):
                    for s, (bank, mm) in enumerate(((ps_q, q_mm), (ps_k, k_mm))):
                        act.wait_ge(mm, W + 1)
                        if not isinstance(W, int) or W:
                            act.wait_ge(added, W)
                        nc.scalar.activation(rope_b[:, s, :], bank[:, :], ACT.Square).then_inc(squared, 1)

                def take_v(W, w):
                    act.wait_ge(v_mm, W + 1)
                    nc.scalar.copy(v_ring[:, w, :], ps_v[:, :]).then_inc(v_out, 1)

                def take_probs(W, p):
                    r = PT + p
                    act.wait_ge(ring_ready[r % 2], ring_use(W, r) + 1)
                    nc.scalar.copy(p_turned[:, p % 2, :, :, :].rearrange("p j s n -> p (j s n)"), ring[r % 2][:, :]).then_inc(ring_taken[r % 2], 1)

                def take_o(g, w):
                    act.wait_ge(pv_mm, WPC * g + w - 1)
                    chunk, ws = (g, w - 2) if w >= 2 else (g - 1, w + 2)
                    nc.scalar.copy(o_ring[:, bass.ds(chunk % 2, 1), :, ws * P:(ws + 1) * P].rearrange("p o h n -> p (o h) n"),
                                   ps_o[:, :].rearrange("p (h n) -> p h n", n=P)).then_inc(o_out, 1)

                def take_qk(W, w):
                    ws = (w - 1) % WPC
                    act.wait_ge(ring_ready[TQ % 2], ring_use(W, TQ) + 1)
                    nc.scalar.copy(q_pad[0][0:HDIM, :, :], ring[TQ % 2][0:HDIM, :].rearrange("p (h n) -> p h n", n=P))
                    nc.scalar.copy(q_pad[1][HDIM:, :, :], ring[TQ % 2][HDIM:, :].rearrange("p (h n) -> p h n", n=P)).then_inc(ring_taken[TQ % 2], 1)
                    act.wait_ge(ring_ready[TK % 2], ring_use(W, TK) + 1)
                    nc.scalar.copy(k_ring[:, :, ws * P:(ws + 1) * P], ring[TK % 2][:, :].rearrange("p (h n) -> p h n", n=P)).then_inc(ring_taken[TK % 2], 1)

                def exponentials(W):
                    for head in range(HEADS):
                        if head % 2 == 0:
                            r = SC + head // 2
                            act.wait_ge(ring_taken[r % 2], ring_use(W, r) + 1)
                        nc.scalar.activation(probs[:, head, :], probs[:, head, :], ACT.Exp, bias=neg_max[:, head:head + 1], scale=-1.0,
                                             accum_out=total[:, head:head + 1]).then_inc(exp_done, 1)

                def square_deviations(g):
                    act.wait_ge(ffn_taken[0], (g - 2) * USES[0] + MEAN + 1)
                    for k in range(KD):
                        ins = nc.scalar.activation(hidden[:, k, :], centred[:, k, :], ACT.Square)
                    ins.then_inc(sq_dev, 1)

                def inverse_deviation(g):
                    act.wait_ge(ffn_ready[1], (g - 2) * USES[1] + MEAN + 1)
                    nc.scalar.activation(dev[:, :], ffn[1][:, :], ACT.Ln, bias=eps_col[:, :]).then_inc(ffn_taken[1], 1)
                    act.wait_ge(ffn_taken[1], (g - 2) * USES[1] + MEAN + 1)
                    nc.scalar.activation(dev[:, :], dev[:, :], ACT.Exp, scale=-0.5).then_inc(dev_done, 1)

                def gate_tile(g, lf, f):
                    act.wait_ge(ffn_ready[0], (g - 2) * USES[0] + GATE + f + 1)
                    if f < FT:
                        nc.scalar.activation(gate[:, f % 2, :], ffn[0][:, :], ACT.Gelu, bias=wt.b1[lf][:, 1, f:f + 1]).then_inc(ffn_taken[0], 1)
                    else:
                        nc.scalar.activation(gate[TAIL_AT:TAIL_AT + TAIL, f % 2, :], ffn[0][0:TAIL, :], ACT.Gelu,
                                             bias=wt.b1[lf][0:TAIL, 1, f:f + 1]).then_inc(tail_gated, 1)

                def body(g, la, lf):
                    for w in range(WPC):
                        W = WPC * g + w
                        new, mid_, old = parts(g, w)
                        forward = lf is not None
                        if new:
                            head_squares(W)
                            take_v(W, w)
                        if old:
                            take_probs(W, 0)
                            take_probs(W, 1)
                        if forward and w == 2:
                            gate_tile(g, lf, 1)
                        if forward and w == 3:
                            gate_tile(g, lf, 4)
                        if old:
                            take_probs(W, 2)
                            take_probs(W, 3)
                        if mid_:
                            take_qk(W, w)
                        if old:
                            take_o(g, w)
                        if forward and w == 0:
                            square_deviations(g)
                        if forward and w == 2:
                            gate_tile(g, lf, 2)
                        if forward and w == 3:
                            gate_tile(g, lf, FT)
                        if w >= 2 and forward:
                            nc.scalar.preload_act_table_set(EXP_LN)
                        if mid_:
                            exponentials(W)
                        if forward and w == 0:
                            inverse_deviation(g)
                        if forward and w == 1:
                            gate_tile(g, lf, 0)
                        if forward and w == 2:
                            gate_tile(g, lf, 3)

                def prepare(name, l):
                    w, loaded, count, done = ((wt.wqkv, wt.wqkv_in, 16, wqkv_high) if name == "wqkv" else
                                              (wt.w1, wt.w1_in, wt.W1_LOADS, w1_high))
                    act.wait_ge(loaded, count * (l + 1))
                    for k in range(KD):
                        nc.scalar.copy(w[0][:, k, :], w[1][:, k, :].bitcast(F32)).then_inc(done, 1)

                nc.scalar.preload_act_table_set(EXP_LN)
                act.wait_ge(cleared, CLEARED)
                act.wait_ge(wt.small_in, wt.SMALLS)
                run(act, body, prepare)

            @block.vector
            def _(dve):
                def take_h(g, n):
                    if not isinstance(g, int) or g:
                        dve.wait_ge(v_mm, WPC * g)
                    src = lambda k, s: xnt[:, k, bass.ds(n, 1), s].rearrange("p o n -> p (o n)")
                    cols = (slice(1, 1 + CH), slice(0, CH))
                    for k in range(KD):
                        nc.vector.tensor_copy(h[0][:, k, :], src(k, cols[k])).then_inc(h_high, 1)
                    for k in range(KD):
                        dve.wait_ge(h_high, KD * g + k + 1)
                        nc.vector.tensor_tensor(h[1][:, k, :], src(k, cols[k]), h[0][:, k, :], ALU.subtract).then_inc(h_ready, 1)

                def rotate(g, w, la):
                    W = WPC * g + w
                    tab = tables[la][:, bass.ds((g % 2) * WPC + w, 1), :, :].rearrange("p o s n -> p (o s) n")
                    if not isinstance(W, int) or W:
                        dve.wait_ge(qk_ready, W)
                    view = lambda x: x.rearrange("p (h n) -> p h n", n=HDIM)
                    for s, bank in enumerate((ps_q, ps_k)):
                        dve.wait_ge(squared, 2 * W + s + 1)
                        nc.vector.tensor_tensor(view(rope_a[:, s, :]), view(bank[:, :]), tab[:, 2 * s:2 * s + 1, :].broadcast_to([P, HEADS, HDIM]),
                                                ALU.mult).then_inc(cos_done, 1)
                    if not isinstance(W, int) or W:
                        dve.wait_ge(clip_done, W)
                    nc.vector.tensor_reduce(sumsq[:, :], rope_b[:, :, :].rearrange("p s (h n) -> p (s h) n", n=HDIM), AX_X, ALU.add).then_inc(sums_done, 1)
                    dve.wait_ge(sums_done, W + 1)
                    for s, bank in enumerate((ps_q, ps_k)):
                        halves_ = lambda x: x.rearrange("p (h a n) -> p h a n", a=2, n=HDIM // 2)
                        sin = tab[:, 2 * s + 1, :].rearrange("p (a n) -> p a n", a=2).unsqueeze(1).broadcast_to([P, HEADS, 2, HDIM // 2])
                        ins = nc.vector.tensor_tensor(halves_(rope_b[:, s, :]), halves_(bank[:, :])[:, :, ::-1, :], sin, ALU.mult)
                    ins.then_inc(roped, 1)

                def mask_and_max(g, w):
                    W = WPC * g + w
                    mask = wt.mask[:, 1::2, :]
                    if w == 1:
                        dve.wait_ge(mask_picked, g + 1)
                        mask = wt.mask[:, 2:4, :]
                    pair = lambda x: x.rearrange("p (s n) -> p s n", s=2)
                    for head in range(HEADS):
                        r = SC + head // 2
                        if head % 2 == 0:
                            dve.wait_ge(ring_ready[r % 2], ring_use(W, r) + 1)
                            apart(dve, dve_passed)
                        src = ring[r % 2][:, (head % 2) * 2 * P:(head % 2 + 1) * 2 * P]
                        ins = nc.vector.tensor_tensor_reduce(pair(probs[:, head, :]), pair(src), mask, -1.0, 3.4e38, ALU.add, ALU.min, neg_max[:, head:head + 1])
                        if head % 2:
                            ins.then_inc(ring_taken[r % 2], 1)

                def normalise(W):
                    dve.wait_ge(exp_done, HEADS * W)
                    nc.vector.reciprocal(inv_total[:, :], total[:, :]).then_inc(inv_total_done, 1)
                    dve.wait_ge(inv_total_done, W)
                    for p in range(HEADS // 2):
                        for j in range(2):
                            head = 2 * p + j
                            ins = nc.vector.tensor_scalar(probs[:, head, :], probs[:, head, :], inv_total[:, head:head + 1], None, ALU.mult)
                        ins.then_inc(p_ready, 1)

                def x_chunk(n, k, s):
                    return xnt[:, k, bass.ds(n, 1), s].rearrange("p o n -> p (o n)")

                def add_attention(g, n):
                    nc.vector.tensor_scalar(mid[:, :, 0:1], mid[:, :, CH:CH + 1], wt.parity[:, bass.ds(g % 2, 1)], None, ALU.mult).then_inc(carried, 1)
                    dve.wait_ge(carried, g - 1)
                    for m in range(KD):
                        dve.wait_ge(ffn_ready[m], (g - 2) * USES[m] + WO + 1)
                        ins = nc.vector.tensor_tensor(mid[:, m, 1:], ffn[m][:, :], x_chunk(n, m, slice(1, 1 + CH)), ALU.add)
                        ins.then_inc(ffn_taken[m], 1)

                def centre(g):
                    dve.wait_ge(ffn_ready[0], (g - 2) * USES[0] + MEAN + 1)
                    nc.vector.scalar_tensor_tensor(out=centred[:, 0, :], in0=ffn[0][:, :], scalar=-1.0, in1=mid[:, 0, 1:], op0=ALU.mult, op1=ALU.add)
                    nc.vector.scalar_tensor_tensor(out=centred[:, 1, :], in0=ffn[0][:, :], scalar=-1.0, in1=mid[:, 1, 0:CH], op0=ALU.mult,
                                                   op1=ALU.add).then_inc(ffn_taken[0], 1)

                def scale(g, lf):
                    dve.wait_ge(dev_done, g - 1)
                    dve.wait_ge(sq_dev, g - 1)
                    for k in range(KD):
                        nc.vector.tensor_tensor(centred[:, k, :], centred[:, k, :], dev[:, :], ALU.mult).then_inc(scaled, 1)

                def shift(g, lf):
                    for k in range(KD):
                        dve.wait_ge(scaled, 2 * (g - 2) + k + 1)
                        nc.vector.tensor_scalar(centred[:, k, :], centred[:, k, :], wt.lnp[lf][:, 0, k:k + 1], wt.lnp[lf][:, 1, k:k + 1],
                                                ALU.mult, ALU.add).then_inc(shifted_done, 1)
                    for k in range(KD):
                        dve.wait_ge(shifted_done, 2 * (g - 2) + k + 1)
                        nc.vector.tensor_copy(f_high[:, k, :], centred[:, k, :]).then_inc(f_high_done, 1)
                    for k in range(KD):
                        dve.wait_ge(f_high_done, 2 * (g - 2) + k + 1)
                        nc.vector.tensor_tensor(f_low[:, k, :], centred[:, k, :], f_high[:, k, :], ALU.subtract).then_inc(normed, 1)

                def hidden_tile(g, lf, f):
                    if f < FT:
                        dve.wait_ge(ffn_taken[0], (g - 2) * USES[0] + GATE + f + 1)
                    else:
                        dve.wait_ge(tail_gated, g - 1)
                    rows, bank, use = (slice(0, P), 1, GATE + f) if f < FT else (slice(TAIL_AT, TAIL_AT + TAIL), 0, TAILS)
                    dve.wait_ge(ffn_ready[bank], (g - 2) * USES[bank] + use + 1)
                    nc.vector.scalar_tensor_tensor(out=hidden[rows, f, :], in0=ffn[bank][rows, :], scalar=wt.b1[lf][rows, 0, f:f + 1],
                                                   in1=gate[rows, f % 2, :], op0=ALU.add, op1=ALU.mult).then_inc(ffn_taken[bank], 1)

                def add_ffn(g, lf, n, m):
                    dve.wait_ge(ffn_ready[1 - m], (g - 2) * USES[1 - m] + W2 + m + 1)
                    nc.vector.scalar_tensor_tensor(out=x_chunk(n, m, slice(1, 1 + CH)), in0=ffn[1 - m][:, :], scalar=wt.b2[lf][:, m:m + 1],
                                                   in1=mid[:, m, 1:], op0=ALU.add, op1=ALU.add).then_inc(ffn_taken[1 - m], 1)

                def carry(g, n):
                    for m in range(KD):
                        dve.wait_ge(ffn_taken[1 - m], (g - 2) * USES[1 - m] + W2 + m + 1)
                    nc.vector.tensor_scalar(xnt[:, :, bass.ds((n + 1) % CHUNKS, 1), 0:1].rearrange("p k o n -> p k (o n)"),
                                            xnt[:, :, bass.ds(n, 1), CH:CH + 1].rearrange("p k o n -> p k (o n)"),
                                            wt.parity[:, bass.ds((g + 1) % 2, 1)], None, ALU.mult).then_inc(x_out, 1)

                def body(g, la, lf):
                    n = g - 2 - CHUNKS * lf if lf is not None else None
                    for w in range(WPC):
                        W = WPC * g + w
                        new, mid_, old = parts(g, w)
                        forward = lf is not None
                        if w == 0 and (not isinstance(g, int) or g < LAST):
                            nc.vector.tensor_copy(wt.mask[:, 2:3, :], wt.mask[:, bass.ds(g % 2, 1), :]).then_inc(mask_picked, 1)
                        if new:
                            rotate(g, w, la)
                        if forward and w == 0:
                            add_attention(g, n)
                            centre(g)
                        if forward and w == 1:
                            scale(g, lf)
                            shift(g, lf)
                        if forward and w == 2:
                            hidden_tile(g, lf, 1)
                            hidden_tile(g, lf, 2)
                        if forward and w == 3:
                            hidden_tile(g, lf, 4)
                            hidden_tile(g, lf, FT)
                        if mid_:
                            mask_and_max(g, w)
                            normalise(W)
                        if forward and w == 1:
                            hidden_tile(g, lf, 0)
                        if forward and w == 2:
                            hidden_tile(g, lf, 3)
                        if w == WPC - 1 and new and not (isinstance(g, int) and g + 1 == LAST):
                            take_next(g, la, lf)
                        if forward and w == 3:
                            add_ffn(g, lf, n, 0)
                            add_ffn(g, lf, n, 1)
                            carry(g, n)

                def take_next(g, la, lf):
                    if not isinstance(g, int) or g > 2:
                        dve.wait_ge(x_out, g - 2)
                    take_h(g + 1, (g + 1) % CHUNKS)

                def prepare(name, l):
                    w, high, done = (wt.wqkv, wqkv_high, wqkv_low) if name == "wqkv" else (wt.w1, w1_high, w1_low)
                    for k in range(KD):
                        dve.wait_ge(high, KD * l + k + 1)
                        ins = nc.vector.tensor_tensor(w[1][:, k, :], w[1][:, k, :].bitcast(F32), w[0][:, k, :], ALU.subtract)
                    ins.then_inc(done, 1)

                def scale_tables():
                    half = HDIM // 2
                    dve.wait_ge(tables_in, 16 * (DEPTH + 2))
                    for l in range(DEPTH):
                        for s in range(2):
                            sc = scales[:, l, s, :].rearrange("p (o n) -> p o n", o=1)
                            for t, to, of in ((0, slice(0, HDIM), slice(0, HDIM)), (1, slice(0, half), slice(half, HDIM)), (1, slice(half, HDIM), slice(0, half))):
                                tab = tables[l][:, :, 2 * s + t, to]
                                ins = nc.vector.tensor_tensor(tab, tab, sc[:, :, of].broadcast_to([P, TILES, to.stop - to.start]), ALU.mult)
                    ins.then_inc(tables_done, 1)

                dve.wait_ge(cleared, CLEARED)
                dve.wait_ge(wt.small_in, wt.SMALLS)
                take_h(0, 0)
                scale_tables()
                dve.wait_ge(tables_done, 1)
                run(dve, body, prepare)


def combine(nc, x, w_out_t, ident_in, xnt, o_dram, inv_dram, out):
    with ExitStack() as ctx:
        sb = lambda n, s: ctx.enter_context(nc.sbuf_tensor(n, s, F32))
        ps = lambda n: ctx.enter_context(nc.psum_tensor(n, [P, CH], F32))
        sem = lambda n: ctx.enter_context(nc.semaphore(n))

        ident = sb("c_ident", [P, P])
        w_out = sb("w_out", [P, KD, D])
        sums = sb("sums", [P, CH])
        inv_sums = sb("inv_sums", [P, CH])
        o_in = sb("o_in", [P, 2, KD, CH])
        inv_in = sb("inv_in", [P, 2, KD, CH])
        x_in = sb("c_x_in", [P, 2, 4, D])
        o_n = sb("o_n", [P, 2, KD, CH])
        silu = sb("silu", [P, 2, KD, CH])
        gated = sb("gated", [P, 2, KD, CH])
        result = sb("result", [P, 2, 4, D])

        ps_s = [[ps(f"ps_s{c}{m}") for m in range(KD)] for c in range(2)]
        ps_t = [[ps(f"ps_t{c}{m}") for m in range(2)] for c in range(2)]

        consts_in = sem("c_consts_in")
        sums_in = sem("sums_in")
        inverted = sem("inverted")
        inv_stored = sem("inv_stored")
        chunk_in = [sem(f"chunk_in{c}") for c in range(2)]
        divided = sem("divided")
        silu_done = sem("silu_done")
        s_ready = sem("s_ready")
        gated_done = sem("gated_done")
        turned_back = sem("turned_back")
        summed = sem("summed")
        out_stored = [sem(f"out_stored{c}") for c in range(2)]
        LOADS = 2 * KD + 1

        with nc.Block() as block:

            @block.sync
            def _(sp):
                def load(b, c):
                    for f in range(KD):
                        src = o_dram.rearrange("(i u) (j h r) n -> i h (u j) r n", u=4, j=2, h=2)
                        src = src[bass.ds(2 * b + f, 1), c, :, 1:1 + G_DIM, :].rearrange("o g r n -> (o g) r n")
                        sp.dma_start(o_in[:, c, f, :], src).then_inc(chunk_in[c], 16)
                        src = inv_dram.rearrange("(i g h) n -> i h g n", g=8, h=2)[bass.ds(2 * b + f, 1), c, :, :].rearrange("o g n -> (o g) n")
                        sp.dma_start(inv_in[:, c, f, :], src.unsqueeze(1).broadcast_to([8, G_DIM, CH])).then_inc(chunk_in[c], 16)
                    src = x[bass.ds(b, 1), c * CH:(c + 1) * CH, :].rearrange("o (t p) n -> p (o t) n", p=P)
                    sp.dma_start(x_in[:, c, :, :], src).then_inc(chunk_in[c], 16)

                def store(b, c):
                    sp.wait_ge(summed, 4 * b + 2 * c + 2)
                    dst = out[bass.ds(b, 1), c * CH:(c + 1) * CH, :].rearrange("o (t p) n -> p (o t) n", p=P)
                    sp.dma_start(dst, result[:, c, :, :]).then_inc(out_stored[c], 16)

                sp.dma_start(sums[:, :], o_dram.rearrange("p (s r) n -> (p s) r n", r=2 * G_DIM)[:, 0, :]).then_inc(sums_in, 16)
                sp.dma_start(ident[:, :], ident_in).then_inc(consts_in, 16)
                sp.dma_start(w_out[:, :, :], w_out_t.rearrange("(k p) n -> p k n", p=P)).then_inc(consts_in, 16)
                sp.wait_ge(inverted, 1)
                sp.dma_start(inv_dram, inv_sums[:, :]).then_inc(inv_stored, 16)
                sp.wait_ge(inv_stored, 16)
                load(0, 0)
                load(0, 1)
                with sp.Fori(0, B - 1) as b:
                    for c in range(2):
                        sp.wait_ge(summed, 4 * b + 2 * c + 2)
                        load(b + 1, c)
                        store(b, c)
                for c in range(2):
                    store(B - 1, c)
                for c in range(2):
                    sp.wait_ge(out_stored[c], 16 * B)

            @block.scalar
            def _(act):
                with act.Fori(0, B) as b:
                    for c in range(2):
                        for k in range(KD):
                            ins = nc.scalar.activation(silu[:, c, k, :], xnt[:, k, bass.ds(2 * b + c, 1), 1:].rearrange("p o n -> p (o n)"), ACT.Silu)
                        ins.then_inc(silu_done, 1)
                        act.wait_ge(gated_done, 4 * b + 2 * c + 2)

            @block.vector
            def _(dve):
                def divide(b, c):
                    dve.wait_ge(chunk_in[c], 16 * LOADS * (b + 1))
                    for f in range(KD):
                        nc.vector.tensor_tensor(o_n[:, c, f, :], o_in[:, c, f, :], inv_in[:, c, f, :], ALU.mult).then_inc(divided, 1)

                def gate(b, c, first):
                    dve.wait_ge(silu_done, 2 * b + c + 1)
                    for m in range(KD):
                        dve.wait_ge(s_ready, 4 * b + 2 * c + m + 1)
                        nc.vector.tensor_tensor(gated[:, c, m, :], ps_s[c][m][:, :], silu[:, c, m, :], ALU.mult).then_inc(gated_done, 1)

                def add(b, c, first):
                    if not first:
                        dve.wait_ge(out_stored[c], 16 * b)
                    for m in range(2):
                        dve.wait_ge(turned_back, 4 * b + 2 * c + m + 1)
                        nc.vector.tensor_tensor(result[:, c, 2 * m:2 * m + 2, :].rearrange("p t n -> p (t n)"), ps_t[c][m][:, :],
                                                x_in[:, c, 2 * m:2 * m + 2, :].rearrange("p t n -> p (t n)"), ALU.add).then_inc(summed, 1)

                def body(b, first, last):
                    gate(b, 0, first)
                    divide(b, 1)
                    add(b, 0, first)
                    gate(b, 1, first)
                    if not last:
                        divide(b + 1, 0)
                    add(b, 1, first)

                dve.wait_ge(sums_in, 16)
                nc.vector.reciprocal(inv_sums[:, :], sums[:, :]).then_inc(inverted, 1)
                divide(0, 0)
                body(0, True, False)
                with dve.Fori(1, B - 1) as b:
                    body(b, False, False)
                body(B - 1, False, True)

            @block.tensor
            def _(pe):
                def project(b, c, first):
                    pe.wait_ge(divided, 4 * b + 2 * c + 2)
                    if not first:
                        pe.wait_ge(gated_done, 4 * b + 2 * c - 2)
                    for m in range(KD):
                        for f in range(KD):
                            mm = nc.tensor.matmul(ps_s[c][m][:, :], w_out[:, f, m * P:(m + 1) * P], o_n[:, c, f, :], start=(f == 0), stop=(f == KD - 1))
                        mm.then_inc(s_ready, 1)

                def turn(b, c, first):
                    pe.wait_ge(gated_done, 4 * b + 2 * c + 2)
                    if not first:
                        pe.wait_ge(summed, 4 * b + 2 * c - 2)
                    for m in range(2):
                        for t in range(2):
                            for k in range(KD):
                                s = slice((2 * m + t) * P, (2 * m + t + 1) * P)
                                mm = nc.tensor.transpose(ps_t[c][m][:, t * D + k * P:t * D + (k + 1) * P], gated[:, c, k, s], ident[:, :])
                        mm.then_inc(turned_back, 1)

                def body(b, first, last):
                    turn(b, 0, first)
                    project(b, 1, first)
                    turn(b, 1, first)
                    if not last:
                        project(b + 1, 0, False)

                pe.wait_ge(consts_in, 32)
                project(0, 0, True)
                body(0, True, False)
                with pe.Fori(1, B - 1) as b:
                    body(b, False, False)
                body(B - 1, False, True)


def rope_table():
    half = G_DIM // 2
    freq = np.float32(1.0) / np.float32(10000.0) ** (np.arange(half, dtype=np.float32) / np.float32(half))
    angle = np.arange(L, dtype=np.float32)[:, None] * freq[None, :]
    c, s = np.cos(angle.astype(np.float64)), np.sin(angle.astype(np.float64))
    return np.stack([np.concatenate([c, c], 1), np.concatenate([-s, s], 1)], 1).astype(np.float32)


def xpos_table():
    idx = np.arange(0, HDIM, 2, dtype=np.float32)
    freq = np.float32(1.0) / np.float32(10000.0) ** (idx / np.float32(HDIM))
    angle = (np.arange(L, dtype=np.float32)[:, None] * freq[None, :]).astype(np.float64)
    base = (idx.astype(np.float64) + 0.4 * HDIM) / (1.4 * HDIM)
    scale = base[None, :] ** ((np.arange(L) - L // 2) / (P / 2.0))[:, None]
    c, s = np.cos(angle), np.sin(angle)
    cat = lambda a, b: np.concatenate([a, b], 1)
    return np.stack([cat(c * scale, c * scale) * QK_SCALE, cat(-s * scale, s * scale) * QK_SCALE,
                     cat(c / scale, c / scale), cat(-s / scale, s / scale)], 1).astype(np.float32)


def window_masks():
    r, c = np.arange(P)[:, None], np.arange(P)[None, :]
    return np.stack([np.full((P, P), MASKED), np.where(c >= r, 0.0, MASKED), np.where(c <= r, 0.0, MASKED)]).astype(np.float32)


def gated_attention_kernel(nc, x, w_qkv_t, w_out_t, wqkv, q_scale, k_scale, wo, ln_g, ln_b, w1, b1, w2, b2,
                           rope, xpos, masks, ident, out):
    with ExitStack() as ctx:
        internal = lambda n, s: nc.dram_tensor(n, s, F32, kind="Internal").ap()
        xnt = ctx.enter_context(nc.sbuf_tensor("xnt", [P, KD, CHUNKS, 1 + CH], F32))
        qs_dram = internal("qs", (2 * B, 8, 2, G_DIM, L))
        ks_dram = internal("ks", (2 * B, 8, 2, G_DIM, L))
        v_dram = internal("v", (2 * B, TILES, P, P))
        o_dram = internal("o", (UNITS, P, CH))
        inv_dram = internal("inv", (P, CH))
        with ExitStack() as layers:
            wt = Weights(layers, nc, wqkv, wo, ln_g, ln_b, w1, b1, w2, b2, masks, ident)
            prepare_tokens(nc, wt, x, w_qkv_t, rope, ident, xnt, qs_dram, ks_dram, v_dram)
            global_attention(nc, ident, qs_dram, ks_dram, v_dram, o_dram)
            local_layers(nc, wt, xpos, q_scale, k_scale, xnt)
        combine(nc, x, w_out_t, ident, xnt, o_dram, inv_dram, out)


_INS = ['L0_attn_x', 'L0_attn_w_qkv', 'L0_attn_w_out', 'L0_ffn_wqkv', 'L0_ffn_q_scale', 'L0_ffn_k_scale', 'L0_ffn_wo', 'L0_ffn_ln_g',
        'L0_ffn_ln_b', 'L0_ffn_w1', 'L0_ffn_b1', 'L0_ffn_w2', 'L0_ffn_b2']
_TURNED = ('L0_attn_w_qkv', 'L0_attn_w_out')
_OUTS = [((4, 1024, 256), 'float32')]


def kernel(**inputs):
    import numpy as _np
    import concourse.bacc as _bacc
    from concourse import mybir as _mybir
    from concourse.bass_utils import run_bass_kernel_spmd as _run

    nc = _bacc.Bacc("TRN2", target_bir_lowering=False, num_devices=1)
    arrays, args = {}, []
    tables = {'rope': rope_table(), 'xpos': xpos_table(), 'masks': window_masks(), 'ident': _np.eye(P, dtype=_np.float32)}
    laid_out = [(n, _np.ascontiguousarray(_np.asarray(inputs[n]).T if n in _TURNED else inputs[n])) for n in _INS] + list(tables.items())
    for name, a in laid_out:
        arrays[f"in_{name}_dram"] = a
        args.append(nc.dram_tensor(f"in_{name}_dram", a.shape, _mybir.dt.from_np(a.dtype), kind="ExternalInput").ap())
    for i, (shape, dtype) in enumerate(_OUTS):
        dt = _mybir.dt.from_np(_np.dtype(dtype))
        args.append(nc.dram_tensor(f"out_{i}_dram", shape, dt, kind="ExternalOutput").ap())
    gated_attention_kernel(nc, *args)
    r = _run(nc, [arrays], core_ids=[0])
    got = tuple(r.results[0][f"out_{i}_dram"] for i in range(len(_OUTS)))
    return got[0]
```

```python
from contextlib import ExitStack

import numpy as np
import concourse.bass as bass
from concourse import mybir

F32 = mybir.dt.float32
F32R = mybir.dt.float32r
ALU = mybir.AluOpType
ACT = mybir.ActivationFunctionType
AX_X = mybir.AxisListType.X

P = 128
B, L, D = 4, 1024, 256
KD = D // P
TILES = L // P
G_HEADS, G_DIM = 16, 16
UNITS = B * G_HEADS // 2
SPLIT = 4 * G_DIM
CH = 512
EPS = 1e-5
STORES = 2 * KD + KD


def flat(ap):
    return ap.rearrange("o p n -> (o p) n")


def apart(eng, passed):
    eng.sem_inc(passed, 1)


def prepare_tokens(nc, wt, x, wqkv_t, rope, ident_in, xnt, qs_dram, ks_dram, v_dram, stored):
    with ExitStack() as ctx:
        sb = lambda n, s, d=F32: ctx.enter_context(nc.sbuf_tensor(n, s, d))
        ps = lambda n, s: ctx.enter_context(nc.psum_tensor(n, s, F32))
        sem = lambda n: ctx.enter_context(nc.semaphore(n))

        ident = sb("a_ident", [P, P])
        wqkv = sb("a_wqkv", [P, KD, 3 * D])
        table = sb("a_rope", [P, TILES, 2, G_DIM])
        x_in = sb("x_in", [P, 2, 4, D])
        stats = sb("stats", [P, 2, 4, 6])
        moments = sb("moments", [P, 2, 4, 2])
        half = sb("half", [P, 4])
        rstd = sb("rstd", [P, 2, 4])
        xn = sb("xn", [P, 2, 4, D])
        xs = sb("xs", [P, 2, KD, CH])
        roped = sb("roped", [P, 2, 2 * D])
        turned = sb("turned", [P, 2, 2 * D])
        qkr = sb("qkr", [P, 2, 2 * D])
        split = sb("split", [P, 2, 4, 2, CH], F32R)
        v_sb = sb("v_sb", [P, 2, 4, D])

        ps_x = [ps(f"ps_x{k}", [P, CH]) for k in range(KD)]
        ps_qk = [ps(f"ps_qk{k}", [P, CH]) for k in range(2)]
        ps_v = [ps(f"ps_v{k}", [P, CH]) for k in range(2)]
        ps_t = [ps(f"ps_t{k}", [P, CH]) for k in range(2)]

        dve_passed, pool_passed = sem("a_dve_passed"), sem("a_pool_passed")
        consts_in = sem("consts_in")
        x_loaded = [sem(f"x_loaded{c}") for c in range(2)]
        half_set = sem("half_set")
        stats_done = sem("stats_done")
        moments_done = sem("moments_done")
        eps_added = sem("eps_added")
        rstd_done = sem("rstd_done")
        xn_done = sem("xn_done")
        x_turned = sem("x_turned")
        xs_done = sem("xs_done")
        xnt_done = sem("xnt_done")
        qk_mm = sem("qk_mm")
        v_mm = sem("v_mm")
        v_copied = sem("v_copied")
        rope_cos = sem("rope_cos")
        rope_sin = sem("rope_sin")
        rope_sum = sem("rope_sum")
        qk_turned = sem("qk_turned")
        high_done = sem("high_done")
        low_done = sem("low_done")

        with nc.Block() as block:

            @block.sync
            def _(sp):
                def load(i, c):
                    src = x[bass.ds(i, 1), c * CH:(c + 1) * CH, :].rearrange("o (t p) n -> p (o t) n", p=P)
                    sp.dma_start(x_in[:, c, :, :], src).then_inc(x_loaded[c], 16)

                def store(i, c):
                    sp.wait_ge(low_done, 8 * i + 4 * c + 4)
                    for part, dram in ((0, qs_dram), (1, ks_dram)):
                        for f in range(KD):
                            dst = dram[bass.ds(2 * i + f, 1), :, :, :, c * CH:(c + 1) * CH].rearrange("o h d s n -> (o h d) s n")
                            sp.dma_start(dst, split[:, c, 2 * part + f, :, :].bitcast(F32)).then_inc(stored[c], 16)
                    sp.wait_ge(v_copied, 8 * i + 4 * c + 4)
                    for f in range(KD):
                        dst = v_dram[bass.ds(2 * i + f, 1), c * 4:c * 4 + 4, :, :].rearrange("o t p n -> p (o t) n")
                        sp.dma_start(dst, v_sb[:, c, :, f * P:(f + 1) * P]).then_inc(stored[c], 16)

                load(0, 0)
                sp.dma_start(ident[:, :], ident_in).then_inc(consts_in, 16)
                sp.dma_start(wqkv[:, :, :], wqkv_t.rearrange("(k p) n -> p k n", p=P)).then_inc(consts_in, 16)
                sp.dma_start(table[:, :, :, :], rope.rearrange("(t p) s n -> p t s n", p=P)).then_inc(consts_in, 16)
                load(0, 1)
                def load_next(i):
                    for c in range(2):
                        sp.wait_ge(xn_done, 8 * i + 4 * c + 4)
                        load(i + 1, c)

                load_next(0)
                with sp.Fori(0, B - 2) as i:
                    store(i, 0)
                    load_next(i + 1)
                    store(i, 1)
                for i in (B - 2, B - 1):
                    for c in range(2):
                        store(i, c)

            @block.gpsimd
            def _(pool):
                nc.gpsimd.memset(half[:, :], -0.5).then_inc(half_set, 1)
                nc.gpsimd.memset(xnt[:, :, :, 0:1], 0.0).then_inc(half_set, 1)
                pool.wait_ge(half_set, 2)

                def inverse_deviation(i, c):
                    pool.wait_ge(moments_done, 8 * i + 4 * c + 4)
                    apart(pool, pool_passed)
                    nc.gpsimd.tensor_scalar(rstd[:, c, :], moments[:, c, :, 1], EPS, None, ALU.add).then_inc(eps_added, 1)
                    pool.wait_ge(eps_added, 2 * i + c + 1)
                    nc.gpsimd.tensor_tensor(rstd[:, c, :], rstd[:, c, :], half[:, :], ALU.pow).then_inc(rstd_done, 1)

                def body(i, last):
                    for c in range(2):
                        pool.wait_ge(xs_done, 4 * i + 2 * c + 2)
                        apart(pool, pool_passed)
                        for k in range(KD):
                            nc.gpsimd.tensor_copy(xnt[:, k, bass.ds(2 * i + c, 1), 1:].rearrange("p o n -> p (o n)"),
                                                  xs[:, c, k, :]).then_inc(xnt_done, 1)
                        if c == 0:
                            nc.gpsimd.tensor_copy(xnt[:, :, bass.ds(2 * i + 1, 1), 0:1].rearrange("p k o n -> p k (o n)"),
                                                  xs[:, 0, :, CH - 1:]).then_inc(xnt_done, 1)
                        for t in range(4 * c, 4 * c + 4):
                            pool.wait_ge(rope_sin, 8 * i + t + 1)
                            if t >= 2:
                                pool.wait_ge(qk_turned, 8 * i + t - 1)
                            elif not isinstance(i, int) or i:
                                pool.wait_ge(qk_turned, 8 * i + t - 1)
                            nc.gpsimd.tensor_tensor(qkr[:, t % 2, :], roped[:, t % 2, :], turned[:, t % 2, :],
                                                    ALU.add).then_inc(rope_sum, 1)
                            if not last and t in (1, 4):
                                inverse_deviation(i + 1, t // 4)

                inverse_deviation(0, 0)
                inverse_deviation(0, 1)
                if wt:
                    pool.wait_ge(rstd_done, 2)
                    wt.clear(nc)
                body(0, False)
                with pool.Fori(1, B - 1) as i:
                    body(i, False)
                body(B - 1, True)

            @block.vector
            def _(dve):
                def normalise(i, c):
                    dve.wait_ge(x_loaded[c], 16 * i + 16)
                    for t in range(4):
                        nc.vector.bn_stats(stats[:, c, t, :], x_in[:, c, t, :]).then_inc(stats_done, 1)
                    dve.wait_ge(stats_done, 8 * i + 4 * c + 4)
                    apart(dve, dve_passed)
                    for t in range(4):
                        nc.vector.bn_aggr(moments[:, c, t, :], stats[:, c, t, :]).then_inc(moments_done, 1)

                def scale(i, c, before):
                    dve.wait_ge(rstd_done, 2 * i + c + 1)
                    if before:
                        dve.wait_ge(x_turned, 4 * i + 2 * c - 2)
                    for t in range(4):
                        nc.vector.tensor_scalar(xn[:, c, t, :], x_in[:, c, t, :], moments[:, c, t, 0:1],
                                                rstd[:, c, t:t + 1], ALU.subtract, ALU.mult).then_inc(xn_done, 1)

                def rotate(i, t, first):
                    dve.wait_ge(qk_mm, 8 * i + t + 1)
                    if t >= 2 or not first:
                        dve.wait_ge(rope_sum, 8 * i + t - 1)
                    src = ps_qk[t % 2][:, :].rearrange("p (h n) -> p h n", n=G_DIM)
                    cos = table[:, t, 0, :].rearrange("p (o n) -> p o n", o=1).broadcast_to([P, 2 * G_HEADS, G_DIM])
                    sin = table[:, t, 1, :].rearrange("p (o n) -> p o n", o=1)
                    a = roped[:, t % 2, :].rearrange("p (h n) -> p h n", n=G_DIM)
                    r = turned[:, t % 2, :].rearrange("p (h n) -> p h n", n=G_DIM)
                    hd = G_DIM // 2
                    nc.vector.tensor_tensor(a, src, cos, ALU.mult)
                    nc.vector.tensor_tensor(r[:, :, 0:hd], src[:, :, hd:], sin[:, :, 0:hd].broadcast_to([P, 2 * G_HEADS, hd]), ALU.mult)
                    nc.vector.tensor_tensor(r[:, :, hd:], src[:, :, 0:hd], sin[:, :, hd:].broadcast_to([P, 2 * G_HEADS, hd]),
                                            ALU.mult).then_inc(rope_sin, 1)

                def low(i, t):
                    dve.wait_ge(high_done, 8 * i + t + 1)
                    c, s = t // 4, slice((t % 4) * P, (t % 4 + 1) * P)
                    nc.vector.tensor_tensor(split[:, c, :, 1, s], ps_t[t % 2][:, :].rearrange("p (f n) -> p f n", f=4),
                                            split[:, c, :, 0, s], ALU.subtract).then_inc(low_done, 1)

                def body(i, first, last):
                    for t in range(TILES):
                        rotate(i, t, first)
                        if t:
                            low(i, t - 1)
                        elif not first:
                            low(i - 1, TILES - 1)
                        if not last and t in (1, 4):
                            normalise(i + 1, t // 4)
                        if not last and t in (3, 6):
                            scale(i + 1, t // 4, True)
                    if last:
                        low(i, TILES - 1)

                normalise(0, 0)
                normalise(0, 1)
                scale(0, 0, False)
                scale(0, 1, False)
                dve.wait_ge(consts_in, 48)
                body(0, True, False)
                with dve.Fori(1, B - 1) as i:
                    body(i, False, False)
                body(B - 1, False, True)

            @block.scalar
            def _(act):
                def take_x(i, c, first):
                    if not first:
                        act.wait_ge(xnt_done, 5 * i + 2 * c - 2)
                        act.wait_ge(v_mm, 8 * i + 4 * c - 4)
                    act.wait_ge(x_turned, 2 * (2 * i + c) + 2)
                    for k in range(KD):
                        nc.scalar.copy(xs[:, c, k, :], ps_x[k][:, :]).then_inc(xs_done, 1)

                def body(i, first, last):
                    if first:
                        take_x(i, 0, True)
                    for t in range(TILES):
                        c = t // 4
                        if t % 4 == 0 and not first:
                            act.wait_ge(stored[c], 16 * STORES * i)
                        act.wait_ge(v_mm, 8 * i + t + 1)
                        nc.scalar.copy(v_sb[:, c, t % 4, :], ps_v[t % 2][:, 0:D]).then_inc(v_copied, 1)
                        if t == 2:
                            take_x(i, 1, first)
                        if t == TILES - 1 and not last:
                            take_x(i + 1, 0, False)
                        act.wait_ge(qk_turned, 8 * i + t + 1)
                        nc.scalar.copy(split[:, c, :, 0, (t % 4) * P:(t % 4 + 1) * P],
                                       ps_t[t % 2][:, :].rearrange("p (f n) -> p f n", f=4)).then_inc(high_done, 1)

                body(0, True, False)
                with act.Fori(1, B - 1) as i:
                    body(i, False, False)
                body(B - 1, False, True)

            @block.tensor
            def _(pe):
                def turn_x(i, c, first):
                    pe.wait_ge(xn_done, 8 * i + 4 * c + 4)
                    if c or not first:
                        pe.wait_ge(xs_done, 4 * i + 2 * c)
                    for k in range(KD):
                        for t in range(4):
                            mm = nc.tensor.transpose(ps_x[k][:, t * P:(t + 1) * P], xn[:, c, t, k * P:(k + 1) * P], ident[:, :])
                        mm.then_inc(x_turned, 1)

                def project(i, t, first):
                    c, s = t // 4, slice((t % 4) * P, (t % 4 + 1) * P)
                    if t % 4 == 0:
                        pe.wait_ge(xs_done, 4 * i + 2 * c + 2)
                    if t >= 2 or not first:
                        pe.wait_ge(rope_sin, 8 * i + t - 1)
                        pe.wait_ge(v_copied, 8 * i + t - 1)
                    for k in range(KD):
                        mm = nc.tensor.matmul(ps_qk[t % 2][:, :], xs[:, c, k, s], wqkv[:, k, 0:2 * D], start=(k == 0), stop=(k == KD - 1))
                    mm.then_inc(qk_mm, 1)
                    for k in range(KD):
                        mm = nc.tensor.matmul(ps_v[t % 2][:, 0:D], xs[:, c, k, s], wqkv[:, k, 2 * D:], start=(k == 0), stop=(k == KD - 1))
                    mm.then_inc(v_mm, 1)

                def turn_qk(i, t, first):
                    pe.wait_ge(rope_sum, 8 * i + t + 1)
                    if t >= 2 or not first:
                        pe.wait_ge(low_done, 8 * i + t - 1)
                    for f in range(4):
                        mm = nc.tensor.transpose(ps_t[t % 2][:, f * P:(f + 1) * P], qkr[:, t % 2, f * P:(f + 1) * P], ident[:, :])
                    mm.then_inc(qk_turned, 1)

                def body(i, first, last):
                    if first:
                        turn_x(i, 0, True)
                    for t in range(TILES):
                        project(i, t, first)
                        if t == 2:
                            turn_x(i, 1, first)
                        if t == TILES - 1 and not last:
                            turn_x(i + 1, 0, False)
                        if t:
                            turn_qk(i, t - 1, first)
                        elif not first:
                            turn_qk(i - 1, TILES - 1, False)
                    if last:
                        turn_qk(i, TILES - 1, False)

                pe.wait_ge(consts_in, 48)
                body(0, True, False)
                with pe.Fori(1, B - 1) as i:
                    body(i, False, False)
                body(B - 1, False, True)


def global_attention(nc, wt, ident_in, qs_dram, ks_dram, v_dram, stored, o_dram):
    with ExitStack() as ctx:
        sb = lambda n, s, d=F32: ctx.enter_context(nc.sbuf_tensor(n, s, d))
        ps = lambda n, s: ctx.enter_context(nc.psum_tensor(n, s, F32))
        sem = lambda n: ctx.enter_context(nc.semaphore(n))

        NB = 4
        ROWS = SPLIT + 2
        PADDED = 96
        ident = sb("g_ident", [P, P])
        stacks = lambda u: [[sb(f"{n}_st{u}{j}", [PADDED, L], F32R) for j in range(2)] for n in "qk"]
        first_stacks = [stacks(u) for u in range(2)]
        v_st = sb("v_st", [P, TILES, 2 * NB, 2 * G_DIM])
        v_in = sb("v_in", [P, TILES, P])
        probs = sb("probs", [P, 4, 2, L])
        o_sb = sb("o_sb", [P, 2, CH])
        last_stacks = stacks(NB - 1)
        q_st, k_st = zip(*(first_stacks + [stacks(u) for u in range(2, NB - 1)] + [last_stacks]))
        maxima = sb("maxima", [P, 2, 2, TILES, 2])
        row_max = sb("row_max", [P, 2, TILES])
        zeros = sb("zeros", [P, 2, TILES])
        max_hl = sb("max_hl", [P, 2, 2, TILES], F32R)
        max_rows = sb("max_rows", [4 * TILES, P])

        ps_st = [ps(f"ps_st{j}", [P, L]) for j in range(2)]
        ps_m = [ps(f"ps_m{k}", [P, CH]) for k in range(3)]
        ps_o = ps("ps_o", [P, CH])

        pool_passed = sem("g_pool_passed")
        ident_loaded = sem("g_ident_loaded")
        v_ones = sem("v_ones")
        k_ones = sem("k_ones")
        qk_in = [sem(f"qk_in{u}") for u in range(NB)]
        v_loaded = sem("v_loaded")
        v_placed = sem("v_placed")
        rows_zeroed = sem("rows_zeroed")
        m_ready = sem("m_ready")
        m_used = sem("m_used")
        max_found = sem("max_found")
        max_high = sem("max_high")
        split_done = sem("split_done")
        turned = sem("turned_maxima")
        rows_out = sem("rows_out")
        rows_in = [sem(f"rows_in{u}") for u in range(NB)]
        st_ready = sem("st_ready")
        exp_done = sem("exp_done")
        pv_done = sem("pv_done")
        o_copied = sem("o_copied")
        o_stored = [sem(f"o_stored{c}") for c in range(2)]

        HALF = 2 * TILES
        USES = 2 * HALF
        LEAD = USES + HALF
        M_BANKS = 3
        TURN = 6
        ITERS = UNITS // NB

        def place(base, k):
            return (base + HALF + k) % USES if isinstance(base, int) else k

        def bank(base, k):
            return ps_m[place(base, k) % M_BANKS]

        def before(base, k):
            return USES % M_BANKS if place(base, k) < USES % M_BANKS else M_BANKS

        with nc.Block() as block:

            @block.sync
            def _(sp):
                def load(i, u):
                    for j in range(2):
                        head = 2 * u + j
                        src = qs_dram[bass.ds(i, 1), head, :, :, :].rearrange("o d s n -> (o d s) n")
                        sp.dma_start(q_st[u][j][0:SPLIT, :].bitcast(F32),
                                     src.unsqueeze(0).broadcast_to([2, 2 * G_DIM, L])).then_inc(qk_in[u], 16)
                        for s in range(2):
                            src = ks_dram[bass.ds(i, 1), head, :, s, :].rearrange("o d n -> (o d) n")
                            sp.dma_start(k_st[u][j][2 * s * G_DIM:2 * (s + 1) * G_DIM, :].bitcast(F32),
                                         src.unsqueeze(1).broadcast_to([G_DIM, 2, L])).then_inc(qk_in[u], 16)

                def load_v(i):
                    sp.dma_start(v_in[:, :, :], v_dram[bass.ds(i, 1), :, :, :].rearrange("o t p n -> p (o t) n")).then_inc(v_loaded, 16)

                def place_rows(i, u):
                    sp.wait_ge(rows_out, NB * i + u + 1)
                    for j in range(2):
                        sp.dma_start(q_st[u][j][SPLIT:ROWS, :].bitcast(F32),
                                     max_rows[j * 2 * TILES:(j + 1) * 2 * TILES, :]).then_inc(rows_in[u], 16)

                def store_o(i, u):
                    sp.wait_ge(o_copied, NB * i + u + 1)
                    dst = o_dram[bass.ds(NB * i + u, 1), :, :].rearrange("o p n -> (o p) n")
                    sp.dma_start(dst, o_sb[:, u % 2, :]).then_inc(o_stored[u % 2], 16)

                def body(i, first, last):
                    for u in range(NB):
                        if u:
                            store_o(i, u - 1)
                        elif not first:
                            store_o(i - 1, NB - 1)
                        if u < NB - 1:
                            place_rows(i, u + 1)
                        elif not last:
                            place_rows(i + 1, 0)
                        if not last:
                            if u == 0:
                                sp.wait_ge(v_placed, TILES * (i + 1))
                                load_v(i + 1)
                            sp.wait_ge(st_ready, 2 * TILES * (NB * i + u) + 2 * TILES)
                            load(i + 1, u)
                    if last:
                        store_o(i, NB - 1)

                for c in range(2):
                    sp.wait_ge(stored[c], 16 * STORES * (B - 1))
                for u in range(NB - 1):
                    load(0, u)
                    if u == 0:
                        sp.dma_start(ident[:, :], ident_in).then_inc(ident_loaded, 16)
                for c in range(2):
                    sp.wait_ge(stored[c], 16 * STORES * B)
                load(0, NB - 1)
                load_v(0)
                sp.wait_ge(wt.set, wt.SETS)
                wt.copy_raw(sp)
                place_rows(0, 0)
                wt.load_small(nc, sp)
                wt.load_wo(sp, 0)
                wt.load_w2(sp, 0)
                sp.wait_ge(wt.raw, 32)
                wt.load_wqkv(sp, 0)
                wt.load_w1(sp, 0)
                body(0, True, False)
                with sp.Fori(1, ITERS - 1) as i:
                    body(i, False, False)
                body(ITERS - 1, False, True)
                for c in range(2):
                    sp.wait_ge(o_stored[c], UNITS // 2 * 16)

            @block.gpsimd
            def _(pool):
                def zero_rows(u, end):
                    for j in range(2):
                        nc.gpsimd.memset(q_st[u][j][SPLIT:end, :].bitcast(F32), 0.0).then_inc(rows_zeroed, 1)

                for u in range(NB):
                    if u == NB - 1:
                        for c in range(2):
                            pool.wait_ge(stored[c], 16 * STORES * B)
                    zero_rows(u, PADDED)
                pool.wait_ge(rows_zeroed, 2 * NB)
                for cols in (slice(0, 1), slice(1 + G_DIM, 2 * G_DIM)):
                    nc.gpsimd.memset(v_st[:, :, :, cols], 1.0).then_inc(v_ones, 1)

                def place_v(i, kt):
                    pool.wait_ge(v_loaded, 16 * i + 16)
                    apart(pool, pool_passed)
                    nc.gpsimd.tensor_copy(v_st[:, kt, :, 1:1 + G_DIM], v_in[:, kt, :].rearrange("p (e n) -> p e n", n=G_DIM)).then_inc(v_placed, 1)

                def split_maxima(n):
                    pool.wait_ge(max_found, n + 1)
                    if not isinstance(n, int) or n:
                        pool.wait_ge(turned, n)
                    nc.gpsimd.tensor_tensor(max_hl[:, :, 0, :], row_max[:, :, :], zeros[:, :, :], ALU.add).then_inc(max_high, 1)
                    pool.wait_ge(max_high, n + 1)
                    nc.gpsimd.tensor_tensor(max_hl[:, :, 1, :], row_max[:, :, :], max_hl[:, :, 0, :], ALU.subtract).then_inc(split_done, 1)

                def body(i, last):
                    for u in range(NB):
                        n = NB * i + u
                        if not last or u + 1 < NB:
                            pool.wait_ge(rows_zeroed, 2 * UNITS if last else 2 * (NB + n))
                            pool.wait_ge(v_placed, TILES * (i + 1))
                            split_maxima(n + 1)
                        if not last:
                            if u == NB - 1:
                                for kt in range(TILES - 1):
                                    pool.wait_ge(pv_done, TILES * n + kt + 1)
                                    place_v(i + 1, kt)
                            pool.wait_ge(st_ready, 2 * TILES * n + 2 * TILES)
                            pool.wait_ge(split_done, n + 2)
                            if u == NB - 1:
                                pool.wait_ge(v_placed, TILES * (i + 2) - 1)
                            apart(pool, pool_passed)
                            zero_rows(u, ROWS)
                            if isinstance(i, int):
                                pool.wait_ge(rows_zeroed, 2 * (NB + n + 1))
                                wt.split_part(nc, pool, u)
                            if u == NB - 1:
                                pool.wait_ge(pv_done, TILES * n + TILES)
                                pool.wait_ge(rows_zeroed, 2 * (NB + n + 1))
                                place_v(i + 1, TILES - 1)

                nc.gpsimd.memset(zeros[:, :, :], 0.0).then_inc(v_ones, 1)
                pool.wait_ge(v_ones, 3)
                for kt in range(TILES):
                    place_v(0, kt)
                split_maxima(0)
                body(0, False)
                with pool.Fori(1, ITERS - 1) as i:
                    body(i, False)
                body(ITERS - 1, True)

            @block.tensor
            def _(pe):
                def maxima_scores(base, use, u, qt, j, h):
                    if not isinstance(base, int) or base + use >= M_BANKS:
                        pe.wait_ge(m_used, base + use + 1 - before(base, use))
                    nc.tensor.matmul(bank(base, use)[:, :], q_st[u][j][:, qt * P:(qt + 1) * P],
                                     k_st[u][j][:, h * CH:(h + 1) * CH], start=True, stop=True).then_inc(m_ready, 1)

                def operands_in(i, u):
                    if isinstance(i, int) and i == 0:
                        pe.wait_ge(k_ones, 2 * (u + 1))
                    pe.wait_ge(qk_in[u], 96 * i + 96)
                    pe.wait_ge(rows_zeroed, 2 * (NB * i + u) + 2)

                def half_maxima(base, k, i, u, half):
                    if half == 0:
                        operands_in(i, u)
                    for n in range(HALF):
                        maxima_scores(base, k + n, u, 4 * half + n // 4, n // 2 % 2, n % 2)

                def turn_maxima(n, kt):
                    pe.wait_ge(split_done, n + 2)
                    if not isinstance(n, int) or n >= 0:
                        pe.wait_ge(exp_done, 2 * TILES * n + 2 * kt - 1)
                    nc.tensor.transpose(ps_st[0][0:4 * TILES, 0:P], max_hl[:, :, :, :].rearrange("p a b c -> p (a b c)").bitcast(F32),
                                        ident[:, :]).then_inc(turned, 1)

                def scores(n, kt, u, j, more):
                    g = 2 * TILES * n + 2 * kt + j
                    if not isinstance(n, int) or g >= 2:
                        pe.wait_ge(exp_done, g - 1)
                    if kt == TURN and j == 0 and more:
                        pe.wait_ge(rows_out, n + 2)
                    for h in range(2):
                        mm = nc.tensor.matmul(ps_st[j][:, h * CH:(h + 1) * CH], k_st[u][j][:, kt * P:(kt + 1) * P],
                                              q_st[u][j][:, h * CH:(h + 1) * CH], start=True, stop=True)
                    mm.then_inc(st_ready, 1)

                def product(n, kt, u):
                    pe.wait_ge(exp_done, 2 * TILES * n + 2 * kt + 2)
                    if kt == 0 and (not isinstance(n, int) or n):
                        pe.wait_ge(o_copied, n)
                    for j in range(2):
                        for h in range(2):
                            r = 32 * (2 * j + h)
                            mm = nc.tensor.matmul(ps_o[r:r + 32, :], v_st[:, kt, 2 * u + j, :],
                                                  probs[:, kt % 4, j, h * CH:(h + 1) * CH], start=(kt == 0), stop=(kt == TILES - 1))
                    mm.then_inc(pv_done, 1)

                def body(i, first, last):
                    for u in range(NB):
                        n = NB * i + u
                        base = LEAD + USES * n
                        i1, u1 = (i, u + 1) if u + 1 < NB else (i + 1, 0)
                        i2, u2 = (i, u + 2) if u + 2 < NB else (i + 1, u + 2 - NB)
                        more1, more2 = not last or u + 1 < NB, not last or u + 2 < NB
                        pe.wait_ge(rows_in[u], 32 * i + 32)
                        for kt in range(TILES):
                            if kt < 4:
                                m = [(4 * kt + e, u1, 4 + kt, e // 2, e % 2) for e in range(4)] if more1 else []
                            else:
                                m = [(HALF + 4 * (kt - 4) + e, u2, kt - 4, e // 2, e % 2) for e in range(4)] if more2 else []
                                if kt == 4 and more2:
                                    operands_in(i2, u2)
                            if kt == TURN and more1:
                                turn_maxima(n, kt)
                            early = 2 if kt == TURN else 1
                            for j in range(2):
                                for e in (range(early) if j == 0 else range(early, 2)):
                                    if m:
                                        maxima_scores(base, *m[e])
                                scores(n, kt, u, j, more1)
                            if m:
                                maxima_scores(base, *m[2])
                            if u == (1 if kt == 0 else 0):
                                pe.wait_ge(v_placed, TILES * i + (kt - 1) % TILES + 1)
                            if kt:
                                product(n, kt - 1, u)
                            elif u:
                                product(n - 1, TILES - 1, u - 1)
                            elif not first:
                                product(n - 1, TILES - 1, NB - 1)
                            if m:
                                maxima_scores(base, *m[3])
                        if last and u == NB - 1:
                            product(n, TILES - 1, u)

                for half in range(2):
                    half_maxima(0, HALF * half, 0, 0, half)
                pe.wait_ge(ident_loaded, 16)
                turn_maxima(-1, 0)
                half_maxima(0, USES, 0, 1, 0)
                body(0, True, False)
                with pe.Fori(1, ITERS - 1) as i:
                    body(i, False, False)
                body(ITERS - 1, False, True)

            @block.vector
            def _(dve):
                def take_maxima(base, k, par, tile, count=1):
                    for e in range(4 * count):
                        dve.wait_ge(m_ready, base + k + e + 1)
                        nc.vector.tensor_reduce(maxima[:, par, e // 2 % 2, tile + e // 4, e % 2:e % 2 + 1], bank(base, k + e)[:, :],
                                                AX_X, ALU.max).then_inc(m_used, 1)

                def join_maxima(n, par, uses):
                    dve.wait_ge(m_used, uses)
                    if not isinstance(n, int) or n:
                        dve.wait_ge(split_done, n)
                    nc.vector.tensor_reduce(row_max[:, :, :], maxima[:, par, :, :, :], AX_X, ALU.max).then_inc(max_found, 1)

                def body(i, last):
                    for u in range(NB):
                        n = NB * i + u
                        base = LEAD + USES * n
                        if not last or u + 1 < NB:
                            take_maxima(base, 0, (u + 1) % 2, 4, 4)
                        if not last or u + 2 < NB:
                            take_maxima(base, HALF, u % 2, 0)
                        if not last or u + 1 < NB:
                            join_maxima(n + 1, (u + 1) % 2, base + HALF)
                        if not last or u + 2 < NB:
                            take_maxima(base, HALF + 4, u % 2, 1, 3)

                def set_ones(u):
                    for j in range(2):
                        nc.vector.memset(k_st[u][j][SPLIT:PADDED, :].bitcast(F32), -1.0).then_inc(k_ones, 1)

                set_ones(0)
                set_ones(1)
                take_maxima(0, 0, 0, 0, 8)
                join_maxima(0, 0, USES)
                take_maxima(0, USES, 1, 0, 4)
                for c in range(2):
                    dve.wait_ge(stored[c], 16 * STORES * B)
                set_ones(2)
                set_ones(3)
                body(0, False)
                with dve.Fori(1, ITERS - 1) as i:
                    body(i, False)
                body(ITERS - 1, True)

            @block.scalar
            def _(act):
                def take_rows(n, i, u):
                    act.wait_ge(turned, n + 1)
                    if u:
                        act.wait_ge(rows_in[u - 1], 32 * i + 32)
                    elif not isinstance(i, int) or i:
                        act.wait_ge(rows_in[NB - 1], 32 * i)
                    nc.scalar.copy(max_rows[:, :], ps_st[0][0:4 * TILES, 0:P]).then_inc(rows_out, 1)

                def copy_o(n, i, u):
                    act.wait_ge(pv_done, TILES * (n + 1))
                    if not isinstance(i, int) or 2 * i + u // 2:
                        act.wait_ge(o_stored[u % 2], 16 * (2 * i + u // 2))
                    nc.scalar.copy(o_sb[:, u % 2, :], ps_o[:, :]).then_inc(o_copied, 1)

                def body(i, first, last):
                    for u in range(NB):
                        n = NB * i + u
                        for kt in range(TILES):
                            for j in range(2):
                                act.wait_ge(st_ready, 2 * TILES * n + 2 * kt + j + 1)
                                if not isinstance(n, int) or TILES * n + kt >= 4:
                                    act.wait_ge(pv_done, TILES * n + kt - 3)
                                nc.scalar.activation(probs[:, kt % 4, j, :], ps_st[j][:, :], ACT.Exp,
                                                     scale=float(G_DIM) ** -0.5).then_inc(exp_done, 1)
                            if kt == TURN - 1 and (not last or u + 1 < NB):
                                take_rows(n + 1, i if u + 1 < NB else i + 1, (u + 1) % NB)
                            if kt == 0:
                                if u:
                                    copy_o(n - 1, i, u - 1)
                                elif not first:
                                    copy_o(n - 1, i - 1, NB - 1)
                    if last:
                        copy_o(NB * i + NB - 1, i, NB - 1)

                for c in range(2):
                    act.wait_ge(stored[c], 16 * STORES * B)
                take_rows(0, 0, 0)
                body(0, True, False)
                with act.Fori(1, ITERS - 1) as i:
                    body(i, False, False)
                body(ITERS - 1, False, True)


DEPTH = 2
HEADS, HDIM = 8, 64
INNER = HEADS * HDIM
HID = int(D * 4 * 2 / 3)
CHUNKS = B * L // CH
WPC = CH // P
WINDOWS = CHUNKS * WPC
FT = HID // P
TAIL = HID - FT * P
TAIL_AT = 64
LAST = DEPTH * CHUNKS
QK_SCALE = 8.0
MASKED = -3.0e38


class Weights:

    def __init__(self, ctx, nc, wqkv, wo, ln_g, ln_b, w1, b1, w2, b2, mask_in, ident_in):
        sb = lambda n, s, d=F32: ctx.enter_context(nc.sbuf_tensor(n, s, d))
        per = lambda n, s: [sb(f"{n}{l}", s) for l in range(DEPTH)]
        sem = lambda n: ctx.enter_context(nc.semaphore(n))
        self.dram = dict(wqkv=wqkv, wo=wo, ln_g=ln_g, ln_b=ln_b, w1=w1, b1=b1, w2=w2, b2=b2, mask=mask_in, ident=ident_in)
        self.wqkv = [sb(f"wqkv_{n}", [P, KD, 3 * INNER], F32R) for n in ("high", "low")]
        self.w1 = [sb(f"w1_{n}", [P, KD, (2 * FT + 1) * P], F32R) for n in ("high", "low")]
        self.wo = sb("wo_l", [P, INNER // P, D])
        self.w2 = sb("w2_l", [P, FT + 1, D])
        self.lnp = per("lnp_l", [P, 2, KD])
        self.b1 = per("b1_l", [P, 2, FT + 1])
        self.b2 = per("b2_l", [P, KD])
        self.mask = sb("l_mask", [P, 4, P])
        self.ident = sb("l_ident", [P, P])
        self.mean_w = sb("mean_w", [P, P])
        self.parity = sb("parity", [P, 2])
        self.wqkv_dram = nc.dram_tensor("wqkv_raw", (DEPTH, D, 3 * INNER), F32, kind="Internal").ap()
        self.w1_dram = nc.dram_tensor("w1_raw", (DEPTH, D, 2 * HID), F32, kind="Internal").ap()
        self.raw = sem("raw")
        self.wqkv_high, self.wqkv_low = sem("wqkv_high"), sem("wqkv_low")
        self.w1_high, self.w1_low = sem("w1_high"), sem("w1_low")
        self.set = sem("w_set")
        self.small_in = sem("small_in")
        self.wqkv_in, self.wo_in, self.w1_in, self.w2_in = sem("wqkv_in"), sem("wo_in"), sem("w1_in"), sem("w2_in")

    SETS = 6
    SMALLS = 16 * (3 + 7 * DEPTH)
    W1_LOADS, W2_LOADS = 16 * 4 * KD, 16 * 2

    def clear(self, nc):
        nc.gpsimd.memset(self.w1[1][:, :, 2 * FT * P:].bitcast(F32), 0.0).then_inc(self.set, 1)
        nc.gpsimd.memset(self.w2[:, FT, :], 0.0).then_inc(self.set, 1)
        for l in range(DEPTH):
            nc.gpsimd.memset(self.b1[l][:, :, FT:], 0.0).then_inc(self.set, 1)
        nc.gpsimd.memset(self.mean_w[:, :], 1.0 / D).then_inc(self.set, 1)
        nc.gpsimd.memset(self.parity[:, 0:1], 0.0)
        nc.gpsimd.memset(self.parity[:, 1:2], 1.0).then_inc(self.set, 1)

    def copy_raw(self, sp):
        sp.dma_start(self.wqkv_dram, self.dram["wqkv"]).then_inc(self.raw, 16)
        sp.dma_start(self.w1_dram, self.dram["w1"]).then_inc(self.raw, 16)

    def load_wqkv(self, sp, l):
        sp.dma_start(self.wqkv[1][:, :, :].bitcast(F32), self.wqkv_dram[l].rearrange("(k p) n -> p k n", p=P)).then_inc(self.wqkv_in, 16)

    def load_wo(self, sp, l):
        sp.dma_start(self.wo[:, :, :], self.dram["wo"][l].rearrange("(k p) n -> p k n", p=P)).then_inc(self.wo_in, 16)

    def load_w1(self, sp, l):
        for k in range(KD):
            rows = self.w1_dram[l, k * P:(k + 1) * P, :]
            dst = self.w1[1][:, k, :].bitcast(F32)
            for to, start, n in ((0, HID, FT * P), (FT * P, 0, FT * P), (2 * FT * P, HID + FT * P, TAIL), (2 * FT * P + TAIL_AT, FT * P, TAIL)):
                sp.dma_start(dst[:, to:to + n], rows[:, start:start + n]).then_inc(self.w1_in, 16)

    def load_w2(self, sp, l):
        w2 = self.dram["w2"]
        sp.dma_start(self.w2[:, 0:FT, :], w2[l, 0:FT * P, :].rearrange("(k p) n -> p k n", p=P)).then_inc(self.w2_in, 16)
        sp.dma_start(self.w2[TAIL_AT:TAIL_AT + TAIL, FT, :], w2[l, FT * P:, :]).then_inc(self.w2_in, 16)

    def split_part(self, nc, pool, part):
        k, (w, loaded, count, high, low) = part % 2, ((self.wqkv, self.wqkv_in, 16, self.wqkv_high, self.wqkv_low),
                                                     (self.w1, self.w1_in, self.W1_LOADS, self.w1_high, self.w1_low))[part // 2]
        pool.wait_ge(loaded, count)
        nc.gpsimd.tensor_copy(w[0][:, k, :], w[1][:, k, :].bitcast(F32)).then_inc(high, 1)
        pool.wait_ge(high, k + 1)
        nc.gpsimd.tensor_tensor(w[1][:, k, :], w[1][:, k, :].bitcast(F32), w[0][:, k, :], ALU.subtract).then_inc(low, 1)
        pool.wait_ge(low, k + 1)

    def load_small(self, nc, sp):
        get = lambda dst, src: sp.dma_start(dst, src).then_inc(self.small_in, 16)
        b1, b2, ln_g, ln_b = (self.dram[n] for n in ("b1", "b2", "ln_g", "ln_b"))
        get(self.ident[:, :], self.dram["ident"])
        get(self.mask[:, 0:2, :], self.dram["mask"][0:2].rearrange("s p n -> p s n"))
        get(self.mask[:, 3, :], self.dram["mask"][2])
        with nc.allow_non_contiguous_dma(reason="a bias has one element for a partition"):
            for l in range(DEPTH):
                get(self.b1[l][:, 0, 0:FT], b1[l, 0:FT * P].rearrange("(k p) -> p k", p=P))
                get(self.b1[l][:, 1, 0:FT], b1[l, HID:HID + FT * P].rearrange("(k p) -> p k", p=P))
                get(self.b1[l][TAIL_AT:TAIL_AT + TAIL, 0, FT:FT + 1], b1[l, FT * P:HID].rearrange("(p o) -> p o", o=1))
                get(self.b1[l][0:TAIL, 1, FT:FT + 1], b1[l, HID + FT * P:].rearrange("(p o) -> p o", o=1))
                get(self.b2[l][:, :], b2[l].rearrange("(k p) -> p k", p=P))
                get(self.lnp[l][:, 0, :], ln_g[l].rearrange("(k p) -> p k", p=P))
                get(self.lnp[l][:, 1, :], ln_b[l].rearrange("(k p) -> p k", p=P))


def local_layers(nc, wt, xpos, q_scale, k_scale, xnt):
    with ExitStack() as ctx:
        sb = lambda n, s, d=F32: ctx.enter_context(nc.sbuf_tensor(n, s, d))
        ps = lambda n: ctx.enter_context(nc.psum_tensor(n, [P, CH], F32))
        sem = lambda n: ctx.enter_context(nc.semaphore(n))

        tables = [sb(f"tables{l}", [P, TILES, 4, HDIM]) for l in range(DEPTH)]
        scales = sb("scales", [P, DEPTH, 2, HDIM])
        h = [sb(f"h_{n}", [P, KD, CH], F32R) for n in ("high", "low")]
        v_ring = sb("v_ring", [P, WPC, INNER])
        k_ring = sb("k_ring", [P, HEADS // 2, WPC * P])
        q_pad = [sb(f"q_pad{j}", [P, HEADS // 2, P]) for j in range(2)]
        rope_a = sb("rope_a", [P, 2, INNER])
        rope_b = sb("rope_b", [P, 2, INNER])
        qk_n = sb("qk_n", [P, 2, INNER])
        sumsq = sb("sumsq", [P, 2 * HEADS])
        clipped = sb("clipped", [P, 2 * HEADS])
        halves = sb("halves", [P, 2 * HEADS])
        inv_norm = sb("inv_norm", [P, 2 * HEADS])
        probs = sb("l_probs", [P, HEADS, 2 * P])
        neg_max = sb("l_neg_max", [P, HEADS])
        total = sb("l_total", [P, HEADS])
        inv_total = sb("l_inv_total", [P, HEADS])
        p_turned = sb("p_turned", [P, 2, 2, 2, P])
        o_ring = sb("o_ring", [P, 2, HEADS // 2, CH])
        mid = sb("mid", [P, KD, 1 + CH])
        f_high, f_low = (sb(f"f_{n}", [P, KD, CH], F32R) for n in ("high", "low"))
        dev = sb("dev", [P, CH])
        gate = sb("gate", [P, 2, CH])
        hidden = sb("hidden", [P, FT + 1, CH])
        centred = hidden[:, KD:2 * KD, :]
        eps_col = sb("eps_col", [P, 1])

        ps_q, ps_k, ps_v, ps_o = ps("ps_q"), ps("ps_k"), ps("ps_v"), ps("l_ps_o")
        ring = [ps(f"ring{b}") for b in range(2)]
        ffn = [ps(f"ffn{b}") for b in range(2)]

        dve_passed, pool_passed = sem("l_dve_passed"), sem("l_pool_passed")
        cleared = sem("cleared")
        mask_picked = sem("mask_picked")
        scales_in = sem("scales_in")
        tables_in = [sem(f"tables_in{l}") for l in range(DEPTH)]
        tables_done = sem("tables_done")
        h_high = sem("h_high")
        h_ready = sem("h_ready")
        q_mm, k_mm, v_mm = sem("q_mm"), sem("k_mm"), sem("l_v_mm")
        squared = sem("squared")
        v_out = sem("v_out")
        cos_done = sem("cos_done")
        sums_done = sem("sums_done")
        roped = sem("l_roped")
        clip_done = sem("clip_done")
        inv_done = sem("inv_done")
        added = sem("added")
        qk_ready = sem("qk_ready")
        ring_ready = [sem(f"ring_ready{b}") for b in range(2)]
        ring_taken = [sem(f"ring_taken{b}") for b in range(2)]
        exp_done = sem("l_exp_done")
        inv_total_done = sem("inv_total_done")
        p_ready = sem("p_ready")
        pv_mm = sem("pv_mm")
        o_out = sem("o_out")
        ffn_ready = [sem(f"ffn_ready{b}") for b in range(2)]
        ffn_taken = [sem(f"ffn_taken{b}") for b in range(2)]
        carried = sem("carried")
        sq_dev = sem("sq_dev")
        ln_done = sem("ln_done")
        dev_done = sem("dev_done")
        scaled = sem("l_scaled")
        shifted_done = sem("shifted_done")
        f_high_done = sem("f_high_done")
        normed = sem("normed")
        tail_gated = sem("tail_gated")
        x_out = sem("x_out")

        PT, TQ, TK, SC = 0, 4, 5, 6

        def ring_use(W, r):
            return 5 * W - 7 + r // 2

        USES = (9, 8)
        WO, MEAN, GATE, W2 = 0, 1, 2, 7
        TAILS = 7

        PLAN = ((0, 0, None, ("wqkv", 0)), (1, 0, None, None), (2, 0, 0, ("w1", 0)), ((3, CHUNKS), 0, 0, None),
                ((CHUNKS, CHUNKS + 2), 1, 0, ("wqkv", 1)), (CHUNKS + 2, 1, 1, ("w1", 1)), ((CHUNKS + 3, LAST), 1, 1, None),
                (LAST, None, 1, None), (LAST + 1, None, 1, None))

        def run(eng, body, prepare=None):
            for g, la, lf, weights in PLAN:
                if weights and weights[0] == "wqkv" and prepare:
                    prepare(*weights)
                if isinstance(g, int):
                    first = (lambda: prepare(*weights)) if weights and weights[0] == "w1" and prepare else None
                    body(g, la, lf, first)
                else:
                    with eng.Fori(*g) as i:
                        body(i, la, lf)

        def parts(g, w):
            if not isinstance(g, int):
                return True, True, True
            W = WPC * g + w
            n = WPC * LAST
            return W < n, 1 <= W <= n, 2 <= W <= n + 1

        CLEARED = 8
        EXP_LN = "natural_log_exp_and_others"
        THREE = [(k, a, b) for k in range(KD) for a, b in ((0, 0), (0, 1), (1, 0))]
        with nc.Block() as block:

            @block.gpsimd
            def _(pool):
                nc.gpsimd.memset(halves[:, :], -0.5).then_inc(cleared, 1)
                nc.gpsimd.memset(v_ring[:, WPC - 1, :], 0.0).then_inc(cleared, 1)
                nc.gpsimd.memset(k_ring[:, :, (WPC - 1) * P:], 0.0).then_inc(cleared, 1)
                for j in range(2):
                    nc.gpsimd.memset(q_pad[j][:, :, :], 0.0).then_inc(cleared, 1)
                nc.gpsimd.memset(mid[:, :, :], 0.0).then_inc(cleared, 1)
                nc.gpsimd.memset(hidden[:, FT, :], 0.0).then_inc(cleared, 1)
                nc.gpsimd.memset(eps_col[:, :], EPS).then_inc(cleared, 1)
                pool.wait_ge(cleared, CLEARED)

                def body(g, la, lf, before_hidden=None):
                    for w in range(WPC):
                        W = WPC * g + w
                        if not parts(g, w)[0]:
                            continue
                        pool.wait_ge(sums_done, W + 1)
                        apart(pool, pool_passed)
                        nc.gpsimd.tensor_scalar(clipped[:, :], sumsq[:, :], 1e-24, None, ALU.max).then_inc(clip_done, 1)
                        pool.wait_ge(clip_done, W + 1)
                        nc.gpsimd.tensor_tensor(inv_norm[:, :], clipped[:, :], halves[:, :], ALU.pow).then_inc(inv_done, 1)
                        pool.wait_ge(roped, W + 1)
                        nc.gpsimd.tensor_tensor(rope_a[:, :, :], rope_a[:, :, :], rope_b[:, :, :], ALU.add).then_inc(added, 1)
                        pool.wait_ge(inv_done, W + 1)
                        pool.wait_ge(added, W + 1)
                        if not isinstance(g, int) or W:
                            pool.wait_ge(ring_ready[TK % 2], ring_use(W, TK) + 1)
                        nc.gpsimd.tensor_tensor(qk_n[:, :, :].rearrange("p s (h n) -> p (s h) n", n=HDIM),
                                                rope_a[:, :, :].rearrange("p s (h n) -> p (s h) n", n=HDIM),
                                                inv_norm[:, :].unsqueeze(2).broadcast_to([P, 2 * HEADS, HDIM]),
                                                ALU.mult).then_inc(qk_ready, 1)

                run(pool, body)

            @block.tensor
            def _(pe):
                def project(g, w, la):
                    W = WPC * g + w
                    if w == 0:
                        pe.wait_ge(h_ready, KD * (g + 1))
                    for n, (bank, done, free) in enumerate(((ps_q, q_mm, roped), (ps_k, k_mm, roped), (ps_v, v_mm, v_out))):
                        if not isinstance(g, int) or W:
                            pe.wait_ge(free, W)
                        for e, (k, a, b) in enumerate(THREE):
                            mm = nc.tensor.matmul(bank[:, :], h[a][:, k, w * P:(w + 1) * P], wt.wqkv[b][:, k, n * INNER:(n + 1) * INNER],
                                                  start=(e == 0), stop=(e == len(THREE) - 1))
                        mm.then_inc(done, 1)

                def ring_wait(W, r):
                    if not isinstance(W, int) or ring_use(W, r) > 0:
                        pe.wait_ge(ring_taken[r % 2], ring_use(W, r))

                def turn_probs(W, p):
                    pe.wait_ge(p_ready, 4 * (W - 2) + p + 1)
                    ring_wait(W, PT + p)
                    for j in range(2):
                        for s in range(2):
                            mm = nc.tensor.transpose(ring[(PT + p) % 2][:, (2 * j + s) * P:(2 * j + s + 1) * P],
                                                     probs[:, 2 * p + j, s * P:(s + 1) * P], wt.ident[:, :])
                    mm.then_inc(ring_ready[(PT + p) % 2], 1)

                def values(W, w, p):
                    ws = (w - 2) % WPC
                    pe.wait_ge(ring_taken[(PT + p) % 2], ring_use(W, PT + p) + 1)
                    if p == 0 and (not isinstance(W, int) or W > 2):
                        pe.wait_ge(o_out, W - 2)
                    for s, slot in enumerate(((ws - 1) % WPC, ws)):
                        for j in range(2):
                            head = 2 * p + j
                            mm = nc.tensor.matmul(ps_o[j * HDIM:(j + 1) * HDIM, p * P:(p + 1) * P],
                                                  v_ring[:, slot, head * HDIM:(head + 1) * HDIM], p_turned[:, p % 2, j, s, :],
                                                  start=(s == 0), stop=(s == 1))
                    if p == HEADS // 2 - 1:
                        mm.then_inc(pv_mm, 1)

                def turn_qk(W, s):
                    r = (TQ, TK)[s]
                    pe.wait_ge(qk_ready, W)
                    ring_wait(W, r)
                    for p in range(HEADS // 2):
                        mm = nc.tensor.transpose(ring[r % 2][:, p * P:(p + 1) * P], qk_n[:, s, p * P:(p + 1) * P], wt.ident[:, :])
                    mm.then_inc(ring_ready[r % 2], 1)

                def scores(W, w):
                    ws = (w - 1) % WPC
                    pe.wait_ge(ring_taken[TQ % 2], ring_use(W, TQ) + 1)
                    pe.wait_ge(ring_taken[TK % 2], ring_use(W, TK) + 1)
                    for p in range(HEADS // 2):
                        r = SC + p
                        ring_wait(W, r)
                        for j in range(2):
                            out = ring[r % 2][:, 2 * j * P:(2 * j + 2) * P]
                            if ws:
                                mm = nc.tensor.matmul(out, q_pad[j][:, p, :], k_ring[:, p, (ws - 1) * P:(ws + 1) * P], start=True, stop=True)
                            else:
                                nc.tensor.matmul(out[:, 0:P], q_pad[j][:, p, :], k_ring[:, p, (WPC - 1) * P:], start=True, stop=True)
                                mm = nc.tensor.matmul(out[:, P:], q_pad[j][:, p, :], k_ring[:, p, 0:P], start=True, stop=True)
                        mm.then_inc(ring_ready[r % 2], 1)

                def ffn_fill(g, bank, use, operands):
                    if not isinstance(g, int) or (g - 2) * USES[bank] + use > 0:
                        pe.wait_ge(ffn_taken[bank], (g - 2) * USES[bank] + use)
                    for n, (a, b) in enumerate(operands):
                        mm = nc.tensor.matmul(ffn[bank][:, :], a, b, start=(n == 0), stop=(n == len(operands) - 1))
                    mm.then_inc(ffn_ready[bank], 1)

                def output_product(g, lf):
                    pe.wait_ge(o_out, WPC * (g - 1))
                    for m in range(KD):
                        ffn_fill(g, m, WO, [(wt.wo[:, p, m * P:(m + 1) * P], o_ring[:, bass.ds(g % 2, 1), p, :].rearrange("p o n -> p (o n)"))
                                            for p in range(HEADS // 2)])

                def shifted(src):
                    return src[:, 0, 1:], src[:, 1, 0:CH]

                def mean(g):
                    for m in range(KD):
                        pe.wait_ge(ffn_taken[m], (g - 2) * USES[m] + WO + 1)
                    ffn_fill(g, 0, MEAN, [(wt.mean_w[:, :], x) for x in shifted(mid)])

                def variance(g):
                    pe.wait_ge(sq_dev, g - 1)
                    ffn_fill(g, 1, MEAN, [(wt.mean_w[:, :], hidden[:, k, :]) for k in range(KD)])

                def hidden_tile(g, lf, f):
                    if f == 0:
                        pe.wait_ge(normed, KD * (g - 1))
                    for bank in range(2):
                        c = (bank * FT + f) * P
                        ffn_fill(g, bank, GATE + f, [(wt.w1[a][:, k, c:c + P], (f_high, f_low)[b][:, k, :]) for k, a, b in THREE])

                def tails(g, lf):
                    ffn_fill(g, 0, TAILS, [(wt.w1[a][:, k, 2 * FT * P:], (f_high, f_low)[b][:, k, :]) for k, a, b in THREE])

                def down(g, lf, m):
                    pe.wait_ge(ffn_taken[1], (g - 2) * USES[1] + GATE + FT)
                    pe.wait_ge(ffn_taken[0], (g - 2) * USES[0] + TAILS + 1)
                    ffn_fill(g, 1 - m, W2 + m, [(wt.w2[:, f, m * P:(m + 1) * P], hidden[:, f, :]) for f in range(FT + 1)])

                def body(g, la, lf, before_hidden=None):
                    for w in range(WPC):
                        W = WPC * g + w
                        new, mid_, old = parts(g, w)
                        forward = lf is not None
                        if w == 0 and before_hidden:
                            pe.wait_ge(wt.wo_in, 16 * (lf + 1))
                        if new:
                            project(g, w, la)
                        if w == 1 and isinstance(g, int) and g == 0:
                            pe.wait_ge(cleared, CLEARED)
                        if old:
                            turn_probs(W, 0)
                            turn_probs(W, 1)
                        if forward and w == 0:
                            output_product(g, lf)
                        if forward and w == 2:
                            hidden_tile(g, lf, 1)
                        if forward and w == 3:
                            hidden_tile(g, lf, 4)
                        if old:
                            values(W, w, 0)
                            turn_probs(W, 2)
                            values(W, w, 1)
                            turn_probs(W, 3)
                        if mid_:
                            turn_qk(W, 0)
                        if old:
                            values(W, w, 2)
                        if mid_:
                            turn_qk(W, 1)
                        if old:
                            values(W, w, 3)
                        if forward and w == 0:
                            mean(g)
                        if forward and w == 2:
                            hidden_tile(g, lf, 2)
                        if forward and w == 3:
                            tails(g, lf)
                        if mid_:
                            scores(W, w)
                        if forward and w == 0:
                            variance(g)
                        if forward and w == 1:
                            if before_hidden:
                                before_hidden()
                            hidden_tile(g, lf, 0)
                        if forward and w == 2:
                            hidden_tile(g, lf, 3)
                        if forward and w == 3:
                            down(g, lf, 0)
                            down(g, lf, 1)

                def prepare(name, l):
                    if name == "wqkv":
                        pe.wait_ge(wt.wqkv_low, KD * (l + 1))
                    else:
                        pe.wait_ge(wt.w1_low, KD * (l + 1))
                        pe.wait_ge(wt.w2_in, wt.W2_LOADS * (l + 1))

                pe.wait_ge(wt.small_in, wt.SMALLS)
                run(pe, body, prepare)

            @block.sync
            def _(sp):
                load_tables = lambda l: sp.dma_start(tables[l][:, :, :, :], xpos.rearrange("(t p) s n -> p t s n", p=P)).then_inc(tables_in[l], 16)
                load_tables(0)
                for s, scale in enumerate((q_scale, k_scale)):
                    sp.dma_start(scales[:, :, s, :], scale.unsqueeze(0).broadcast_to([P, DEPTH, HDIM])).then_inc(scales_in, 16)
                load_tables(1)
                sp.wait_ge(v_mm, WPC * CHUNKS)
                wt.load_wqkv(sp, 1)
                for m in range(KD):
                    sp.wait_ge(ffn_ready[m], (CHUNKS - 1) * USES[m] + WO + 1)
                wt.load_wo(sp, 1)
                sp.wait_ge(ffn_ready[0], (CHUNKS - 1) * USES[0] + TAILS + 1)
                wt.load_w1(sp, 1)
                for m in range(KD):
                    sp.wait_ge(ffn_ready[1 - m], (CHUNKS - 1) * USES[1 - m] + W2 + m + 1)
                wt.load_w2(sp, 1)

            @block.scalar
            def _(act):
                def head_squares(W):
                    for s, (bank, mm) in enumerate(((ps_q, q_mm), (ps_k, k_mm))):
                        act.wait_ge(mm, W + 1)
                        if not isinstance(W, int) or W:
                            act.wait_ge(added, W)
                        nc.scalar.activation(rope_b[:, s, :], bank[:, :], ACT.Square).then_inc(squared, 1)

                def take_v(W, w):
                    act.wait_ge(v_mm, W + 1)
                    nc.scalar.copy(v_ring[:, w, :], ps_v[:, :]).then_inc(v_out, 1)

                def take_probs(W, p):
                    r = PT + p
                    act.wait_ge(ring_ready[r % 2], ring_use(W, r) + 1)
                    nc.scalar.copy(p_turned[:, p % 2, :, :, :].rearrange("p j s n -> p (j s n)"), ring[r % 2][:, :]).then_inc(ring_taken[r % 2], 1)

                def take_o(g, w):
                    act.wait_ge(pv_mm, WPC * g + w - 1)
                    chunk, ws = (g, w - 2) if w >= 2 else (g - 1, w + 2)
                    nc.scalar.copy(o_ring[:, bass.ds(chunk % 2, 1), :, ws * P:(ws + 1) * P].rearrange("p o h n -> p (o h) n"),
                                   ps_o[:, :].rearrange("p (h n) -> p h n", n=P)).then_inc(o_out, 1)

                def take_qk(W, w):
                    ws = (w - 1) % WPC
                    act.wait_ge(ring_ready[TQ % 2], ring_use(W, TQ) + 1)
                    nc.scalar.copy(q_pad[0][0:HDIM, :, :], ring[TQ % 2][0:HDIM, :].rearrange("p (h n) -> p h n", n=P))
                    nc.scalar.copy(q_pad[1][HDIM:, :, :], ring[TQ % 2][HDIM:, :].rearrange("p (h n) -> p h n", n=P)).then_inc(ring_taken[TQ % 2], 1)
                    act.wait_ge(ring_ready[TK % 2], ring_use(W, TK) + 1)
                    nc.scalar.copy(k_ring[:, :, ws * P:(ws + 1) * P], ring[TK % 2][:, :].rearrange("p (h n) -> p h n", n=P)).then_inc(ring_taken[TK % 2], 1)

                def exponentials(W):
                    for head in range(HEADS):
                        if head % 2 == 0:
                            r = SC + head // 2
                            act.wait_ge(ring_taken[r % 2], ring_use(W, r) + 1)
                        nc.scalar.activation(probs[:, head, :], probs[:, head, :], ACT.Exp, bias=neg_max[:, head:head + 1], scale=-1.0,
                                             accum_out=total[:, head:head + 1]).then_inc(exp_done, 1)

                def square_deviations(g):
                    act.wait_ge(ffn_taken[0], (g - 2) * USES[0] + MEAN + 1)
                    for k in range(KD):
                        ins = nc.scalar.activation(hidden[:, k, :], centred[:, k, :], ACT.Square)
                    ins.then_inc(sq_dev, 1)

                def inverse_deviation(g):
                    act.wait_ge(ffn_ready[1], (g - 2) * USES[1] + MEAN + 1)
                    nc.scalar.activation(dev[:, :], ffn[1][:, :], ACT.Ln, bias=eps_col[:, :]).then_inc(ffn_taken[1], 1)
                    act.wait_ge(ffn_taken[1], (g - 2) * USES[1] + MEAN + 1)
                    nc.scalar.activation(dev[:, :], dev[:, :], ACT.Exp, scale=-0.5).then_inc(dev_done, 1)

                def gate_tile(g, lf, f):
                    act.wait_ge(ffn_ready[0], (g - 2) * USES[0] + GATE + f + 1)
                    if f < FT:
                        nc.scalar.activation(gate[:, f % 2, :], ffn[0][:, :], ACT.Gelu, bias=wt.b1[lf][:, 1, f:f + 1]).then_inc(ffn_taken[0], 1)
                    else:
                        nc.scalar.activation(gate[TAIL_AT:TAIL_AT + TAIL, f % 2, :], ffn[0][0:TAIL, :], ACT.Gelu,
                                             bias=wt.b1[lf][0:TAIL, 1, f:f + 1]).then_inc(tail_gated, 1)

                def body(g, la, lf, before_hidden=None):
                    for w in range(WPC):
                        W = WPC * g + w
                        new, mid_, old = parts(g, w)
                        forward = lf is not None
                        if new:
                            head_squares(W)
                            take_v(W, w)
                        if w == 1 and before_hidden:
                            before_hidden()
                        if old:
                            take_probs(W, 0)
                            take_probs(W, 1)
                        if forward and w == 2:
                            gate_tile(g, lf, 1)
                        if forward and w == 3:
                            gate_tile(g, lf, 4)
                        if old:
                            take_probs(W, 2)
                            take_probs(W, 3)
                        if mid_:
                            take_qk(W, w)
                        if old:
                            take_o(g, w)
                        if forward and w == 0:
                            square_deviations(g)
                        if forward and w == 2:
                            gate_tile(g, lf, 2)
                        if forward and w == 3:
                            gate_tile(g, lf, FT)
                        if w >= 2 and forward:
                            nc.scalar.preload_act_table_set(EXP_LN)
                        if mid_:
                            exponentials(W)
                        if forward and w == 0:
                            inverse_deviation(g)
                        if forward and w == 1:
                            gate_tile(g, lf, 0)
                        if forward and w == 2:
                            gate_tile(g, lf, 3)

                def prepare(name, l):
                    if l == 0:
                        return
                    w, loaded, count, done = ((wt.wqkv, wt.wqkv_in, 16, wt.wqkv_high) if name == "wqkv" else
                                              (wt.w1, wt.w1_in, wt.W1_LOADS, wt.w1_high))
                    act.wait_ge(loaded, count * (l + 1))
                    for k in range(KD):
                        nc.scalar.copy(w[0][:, k, :], w[1][:, k, :].bitcast(F32)).then_inc(done, 1)

                nc.scalar.preload_act_table_set(EXP_LN)
                act.wait_ge(cleared, CLEARED)
                act.wait_ge(wt.small_in, wt.SMALLS)
                run(act, body, prepare)

            @block.vector
            def _(dve):
                def take_h(g, n):
                    if not isinstance(g, int) or g:
                        dve.wait_ge(v_mm, WPC * g)
                    src = lambda k, s: xnt[:, k, bass.ds(n, 1), s].rearrange("p o n -> p (o n)")
                    cols = (slice(1, 1 + CH), slice(0, CH))
                    for k in range(KD):
                        nc.vector.tensor_copy(h[0][:, k, :], src(k, cols[k])).then_inc(h_high, 1)
                    for k in range(KD):
                        dve.wait_ge(h_high, KD * g + k + 1)
                        nc.vector.tensor_tensor(h[1][:, k, :], src(k, cols[k]), h[0][:, k, :], ALU.subtract).then_inc(h_ready, 1)

                def rotate(g, w, la):
                    W = WPC * g + w
                    tab = tables[la][:, bass.ds((g % 2) * WPC + w, 1), :, :].rearrange("p o s n -> p (o s) n")
                    if not isinstance(W, int) or W:
                        dve.wait_ge(qk_ready, W)
                    view = lambda x: x.rearrange("p (h n) -> p h n", n=HDIM)
                    for s, bank in enumerate((ps_q, ps_k)):
                        dve.wait_ge(squared, 2 * W + s + 1)
                        nc.vector.tensor_tensor(view(rope_a[:, s, :]), view(bank[:, :]), tab[:, 2 * s:2 * s + 1, :].broadcast_to([P, HEADS, HDIM]),
                                                ALU.mult).then_inc(cos_done, 1)
                    if not isinstance(W, int) or W:
                        dve.wait_ge(clip_done, W)
                    nc.vector.tensor_reduce(sumsq[:, :], rope_b[:, :, :].rearrange("p s (h n) -> p (s h) n", n=HDIM), AX_X, ALU.add).then_inc(sums_done, 1)
                    dve.wait_ge(sums_done, W + 1)
                    for s, bank in enumerate((ps_q, ps_k)):
                        halves_ = lambda x: x.rearrange("p (h a n) -> p h a n", a=2, n=HDIM // 2)
                        sin = tab[:, 2 * s + 1, :].rearrange("p (a n) -> p a n", a=2).unsqueeze(1).broadcast_to([P, HEADS, 2, HDIM // 2])
                        ins = nc.vector.tensor_tensor(halves_(rope_b[:, s, :]), halves_(bank[:, :])[:, :, ::-1, :], sin, ALU.mult)
                    ins.then_inc(roped, 1)

                def mask_and_max(g, w, pairs):
                    W = WPC * g + w
                    mask = wt.mask[:, 1::2, :]
                    if w == 1:
                        dve.wait_ge(mask_picked, g + 1)
                        mask = wt.mask[:, 2:4, :]
                    pair = lambda x: x.rearrange("p (s n) -> p s n", s=2)
                    for head in range(2 * pairs.start, 2 * pairs.stop):
                        r = SC + head // 2
                        if head % 2 == 0:
                            dve.wait_ge(ring_ready[r % 2], ring_use(W, r) + 1)
                            apart(dve, dve_passed)
                        src = ring[r % 2][:, (head % 2) * 2 * P:(head % 2 + 1) * 2 * P]
                        ins = nc.vector.tensor_tensor_reduce(pair(probs[:, head, :]), pair(src), mask, -1.0, 3.4e38, ALU.add, ALU.min, neg_max[:, head:head + 1])
                        if head % 2:
                            ins.then_inc(ring_taken[r % 2], 1)

                def normalise(W):
                    dve.wait_ge(exp_done, HEADS * W)
                    nc.vector.reciprocal(inv_total[:, :], total[:, :]).then_inc(inv_total_done, 1)
                    dve.wait_ge(inv_total_done, W)
                    for p in range(HEADS // 2):
                        for j in range(2):
                            head = 2 * p + j
                            ins = nc.vector.tensor_scalar(probs[:, head, :], probs[:, head, :], inv_total[:, head:head + 1], None, ALU.mult)
                        ins.then_inc(p_ready, 1)

                def x_chunk(n, k, s):
                    return xnt[:, k, bass.ds(n, 1), s].rearrange("p o n -> p (o n)")

                def add_attention(g, n):
                    nc.vector.tensor_scalar(mid[:, :, 0:1], mid[:, :, CH:CH + 1], wt.parity[:, bass.ds(g % 2, 1)], None, ALU.mult).then_inc(carried, 1)
                    dve.wait_ge(carried, g - 1)
                    for m in range(KD):
                        dve.wait_ge(ffn_ready[m], (g - 2) * USES[m] + WO + 1)
                        ins = nc.vector.tensor_tensor(mid[:, m, 1:], ffn[m][:, :], x_chunk(n, m, slice(1, 1 + CH)), ALU.add)
                        ins.then_inc(ffn_taken[m], 1)

                def centre(g):
                    dve.wait_ge(ffn_ready[0], (g - 2) * USES[0] + MEAN + 1)
                    nc.vector.scalar_tensor_tensor(out=centred[:, 0, :], in0=ffn[0][:, :], scalar=-1.0, in1=mid[:, 0, 1:], op0=ALU.mult, op1=ALU.add)
                    nc.vector.scalar_tensor_tensor(out=centred[:, 1, :], in0=ffn[0][:, :], scalar=-1.0, in1=mid[:, 1, 0:CH], op0=ALU.mult,
                                                   op1=ALU.add).then_inc(ffn_taken[0], 1)

                def scale(g, lf):
                    dve.wait_ge(dev_done, g - 1)
                    dve.wait_ge(sq_dev, g - 1)
                    for k in range(KD):
                        nc.vector.tensor_tensor(centred[:, k, :], centred[:, k, :], dev[:, :], ALU.mult).then_inc(scaled, 1)

                def shift(g, lf):
                    for k in range(KD):
                        dve.wait_ge(scaled, 2 * (g - 2) + k + 1)
                        nc.vector.tensor_scalar(centred[:, k, :], centred[:, k, :], wt.lnp[lf][:, 0, k:k + 1], wt.lnp[lf][:, 1, k:k + 1],
                                                ALU.mult, ALU.add).then_inc(shifted_done, 1)
                    for k in range(KD):
                        dve.wait_ge(shifted_done, 2 * (g - 2) + k + 1)
                        nc.vector.tensor_copy(f_high[:, k, :], centred[:, k, :]).then_inc(f_high_done, 1)
                    for k in range(KD):
                        dve.wait_ge(f_high_done, 2 * (g - 2) + k + 1)
                        nc.vector.tensor_tensor(f_low[:, k, :], centred[:, k, :], f_high[:, k, :], ALU.subtract).then_inc(normed, 1)

                def hidden_tile(g, lf, f):
                    if f < FT:
                        dve.wait_ge(ffn_taken[0], (g - 2) * USES[0] + GATE + f + 1)
                    else:
                        dve.wait_ge(tail_gated, g - 1)
                    rows, bank, use = (slice(0, P), 1, GATE + f) if f < FT else (slice(TAIL_AT, TAIL_AT + TAIL), 0, TAILS)
                    dve.wait_ge(ffn_ready[bank], (g - 2) * USES[bank] + use + 1)
                    nc.vector.scalar_tensor_tensor(out=hidden[rows, f, :], in0=ffn[bank][rows, :], scalar=wt.b1[lf][rows, 0, f:f + 1],
                                                   in1=gate[rows, f % 2, :], op0=ALU.add, op1=ALU.mult).then_inc(ffn_taken[bank], 1)

                def add_ffn(g, lf, n, m):
                    dve.wait_ge(ffn_ready[1 - m], (g - 2) * USES[1 - m] + W2 + m + 1)
                    nc.vector.scalar_tensor_tensor(out=x_chunk(n, m, slice(1, 1 + CH)), in0=ffn[1 - m][:, :], scalar=wt.b2[lf][:, m:m + 1],
                                                   in1=mid[:, m, 1:], op0=ALU.add, op1=ALU.add).then_inc(ffn_taken[1 - m], 1)

                def carry(g, n):
                    for m in range(KD):
                        dve.wait_ge(ffn_taken[1 - m], (g - 2) * USES[1 - m] + W2 + m + 1)
                    nc.vector.tensor_scalar(xnt[:, :, bass.ds((n + 1) % CHUNKS, 1), 0:1].rearrange("p k o n -> p k (o n)"),
                                            xnt[:, :, bass.ds(n, 1), CH:CH + 1].rearrange("p k o n -> p k (o n)"),
                                            wt.parity[:, bass.ds((g + 1) % 2, 1)], None, ALU.mult).then_inc(x_out, 1)

                def body(g, la, lf, before_hidden=None):
                    n = g - 2 - CHUNKS * lf if lf is not None else None
                    for w in range(WPC):
                        W = WPC * g + w
                        new, mid_, old = parts(g, w)
                        forward = lf is not None
                        if w == 0 and (not isinstance(g, int) or g < LAST):
                            nc.vector.tensor_copy(wt.mask[:, 2:3, :], wt.mask[:, bass.ds(g % 2, 1), :]).then_inc(mask_picked, 1)
                        next_one = w == WPC - 1 and new and not (isinstance(g, int) and g + 1 == LAST)
                        if new:
                            rotate(g, w, la)
                        if next_one and not forward:
                            take_next(g, la, lf)
                        if forward and w == 0:
                            add_attention(g, n)
                            centre(g)
                        if w == 1 and before_hidden:
                            before_hidden()
                        if forward and w == 1:
                            scale(g, lf)
                            shift(g, lf)
                        if forward and w == 2:
                            hidden_tile(g, lf, 1)
                            hidden_tile(g, lf, 2)
                        if forward and w == 3:
                            hidden_tile(g, lf, 4)
                        if mid_:
                            mask_and_max(g, w, range(0, 2))
                        if forward and w == 3:
                            hidden_tile(g, lf, FT)
                        if mid_:
                            mask_and_max(g, w, range(2, HEADS // 2))
                            normalise(W)
                        if forward and w == 1:
                            hidden_tile(g, lf, 0)
                        if forward and w == 2:
                            hidden_tile(g, lf, 3)
                        if next_one and forward:
                            take_next(g, la, lf)
                        if forward and w == 3:
                            add_ffn(g, lf, n, 0)
                            add_ffn(g, lf, n, 1)
                            carry(g, n)

                def take_next(g, la, lf):
                    if not isinstance(g, int) or g > 2:
                        dve.wait_ge(x_out, g - 2)
                    take_h(g + 1, (g + 1) % CHUNKS)

                def prepare(name, l):
                    if l == 0:
                        scale_tables(0 if name == "wqkv" else 1)
                        return
                    w, high, done = (wt.wqkv, wt.wqkv_high, wt.wqkv_low) if name == "wqkv" else (wt.w1, wt.w1_high, wt.w1_low)
                    for k in range(KD):
                        dve.wait_ge(high, KD * l + k + 1)
                        nc.vector.tensor_tensor(w[1][:, k, :], w[1][:, k, :].bitcast(F32), w[0][:, k, :], ALU.subtract).then_inc(done, 1)

                def scale_tables(l):
                    half = HDIM // 2
                    dve.wait_ge(scales_in, 16 * 2)
                    dve.wait_ge(tables_in[l], 16)
                    for s in range(2):
                        sc = scales[:, l, s, :].rearrange("p (o n) -> p o n", o=1)
                        for t, to, of in ((0, slice(0, HDIM), slice(0, HDIM)), (1, slice(0, half), slice(half, HDIM)), (1, slice(half, HDIM), slice(0, half))):
                            tab = tables[l][:, :, 2 * s + t, to]
                            ins = nc.vector.tensor_tensor(tab, tab, sc[:, :, of].broadcast_to([P, TILES, to.stop - to.start]), ALU.mult)
                    ins.then_inc(tables_done, 1)
                    dve.wait_ge(tables_done, l + 1)

                take_h(0, 0)
                dve.wait_ge(cleared, CLEARED)
                dve.wait_ge(wt.small_in, wt.SMALLS)
                run(dve, body, prepare)


def combine(nc, x, w_out_t, ident_in, spread_in, xnt, o_dram, out):
    with ExitStack() as ctx:
        sb = lambda n, s: ctx.enter_context(nc.sbuf_tensor(n, s, F32))
        ps = lambda n: ctx.enter_context(nc.psum_tensor(n, [P, CH], F32))
        sem = lambda n: ctx.enter_context(nc.semaphore(n))

        SUMS = 4 * KD * 4
        ident = sb("c_ident", [P, P])
        w_out = sb("w_out", [P, KD, D])
        spread = sb("c_spread", [P, KD, 2, P])
        sums = sb("sums", [SUMS, CH])
        inv_sums = sb("inv_sums", [P, 2, CH])
        o_in = sb("o_in", [P, 2, KD, CH])
        x_in = sb("c_x_in", [P, 2, 4, D])
        o_n = sb("o_n", [P, 2, KD, CH])
        silu = sb("silu", [P, 2, KD, CH])
        gated = sb("gated", [P, 2, KD, CH])
        result = sb("result", [P, 2, 4, D])

        ps_i = [ps(f"ps_i{f}") for f in range(KD)]
        ps_s = [ps(f"ps_s{m}") for m in range(KD)]
        ps_t = [[ps(f"ps_t{c}{m}") for m in range(2)] for c in range(2)]

        consts_in = sem("c_consts_in")
        sums_in = sem("sums_in")
        rows_zero = sem("rows_zero")
        inverted = sem("inverted")
        spread_done = sem("spread_done")
        chunk_in = [sem(f"chunk_in{c}") for c in range(2)]
        x_arrived = [sem(f"x_arrived{c}") for c in range(2)]
        divided = sem("divided")
        silu_done = sem("silu_done")
        s_ready = sem("s_ready")
        gated_done = sem("gated_done")
        turned_back = sem("turned_back")
        summed = sem("summed")
        out_stored = [sem(f"out_stored{c}") for c in range(2)]

        with nc.Block() as block:

            @block.sync
            def _(sp):
                def load_sums(b):
                    src = o_dram.rearrange("(b u) (s r) n -> b (u s) r n", b=B, r=2 * G_DIM)[bass.ds(b, 1), :, 0, :].rearrange("o g n -> (o g) n")
                    sp.dma_start(sums[:, :], src).then_inc(sums_in, 16)

                def load_o(b, c):
                    for f in range(KD):
                        src = o_dram.rearrange("(i u) (j h r) n -> i h (u j) r n", u=4, j=2, h=2)
                        src = src[bass.ds(2 * b + f, 1), c, :, 1:1 + G_DIM, :].rearrange("o g r n -> (o g) r n")
                        sp.dma_start(o_in[:, c, f, :], src).then_inc(chunk_in[c], 16)

                def load_x(b, c):
                    src = x[bass.ds(b, 1), c * CH:(c + 1) * CH, :].rearrange("o (t p) n -> p (o t) n", p=P)
                    sp.dma_start(x_in[:, c, :, :], src).then_inc(x_arrived[c], 16)

                def store(b, c):
                    sp.wait_ge(summed, 4 * b + 2 * c + 2)
                    dst = out[bass.ds(b, 1), c * CH:(c + 1) * CH, :].rearrange("o (t p) n -> p (o t) n", p=P)
                    sp.dma_start(dst, result[:, c, :, :]).then_inc(out_stored[c], 16)

                load_sums(0)
                sp.dma_start(spread[:, :, :, :], spread_in).then_inc(consts_in, 16)
                load_o(0, 0)
                sp.dma_start(w_out[:, :, :], w_out_t.rearrange("(k p) n -> p k n", p=P)).then_inc(consts_in, 16)
                sp.dma_start(ident[:, :], ident_in).then_inc(consts_in, 16)
                load_o(0, 1)
                load_x(0, 0)
                load_x(0, 1)
                with sp.Fori(0, B - 1) as b:
                    sp.wait_ge(inverted, b + 1)
                    load_sums(b + 1)
                    for c in range(2):
                        sp.wait_ge(divided, 4 * b + 2 * c + 2)
                        load_o(b + 1, c)
                    for c in range(2):
                        sp.wait_ge(summed, 4 * b + 2 * c + 2)
                        load_x(b + 1, c)
                        store(b, c)
                for c in range(2):
                    store(B - 1, c)
                for c in range(2):
                    sp.wait_ge(out_stored[c], 16 * B)

            @block.scalar
            def _(act):
                with act.Fori(0, B) as b:
                    for c in range(2):
                        for k in range(KD):
                            ins = nc.scalar.activation(silu[:, c, k, :], xnt[:, k, bass.ds(2 * b + c, 1), 1:].rearrange("p o n -> p (o n)"), ACT.Silu)
                        ins.then_inc(silu_done, 1)
                        act.wait_ge(gated_done, 4 * b + 2 * c + 2)

            @block.vector
            def _(dve):
                def divide(b, c):
                    dve.wait_ge(chunk_in[c], 16 * KD * (b + 1))
                    for f in range(KD):
                        dve.wait_ge(spread_done, 4 * b + 2 * c + f + 1)
                        nc.vector.tensor_tensor(o_n[:, c, f, :], o_in[:, c, f, :], ps_i[f][:, :], ALU.mult).then_inc(divided, 1)

                def invert(b):
                    dve.wait_ge(sums_in, 16 * (b + 1))
                    nc.vector.reciprocal(inv_sums[0:SUMS, bass.ds(b % 2, 1), :].rearrange("p o n -> p (o n)"), sums[:, :]).then_inc(inverted, 1)

                def gate(b, c, first):
                    dve.wait_ge(silu_done, 2 * b + c + 1)
                    for m in range(KD):
                        dve.wait_ge(s_ready, 4 * b + 2 * c + m + 1)
                        nc.vector.tensor_tensor(gated[:, c, m, :], ps_s[m][:, :], silu[:, c, m, :], ALU.mult).then_inc(gated_done, 1)

                def add(b, c, first):
                    dve.wait_ge(x_arrived[c], 16 * (b + 1))
                    if not first:
                        dve.wait_ge(out_stored[c], 16 * b)
                    for m in range(2):
                        dve.wait_ge(turned_back, 4 * b + 2 * c + m + 1)
                        nc.vector.tensor_tensor(result[:, c, 2 * m:2 * m + 2, :].rearrange("p t n -> p (t n)"), ps_t[c][m][:, :],
                                                x_in[:, c, 2 * m:2 * m + 2, :].rearrange("p t n -> p (t n)"), ALU.add).then_inc(summed, 1)

                def body(b, first, last):
                    gate(b, 0, first)
                    divide(b, 1)
                    add(b, 0, first)
                    if not last:
                        invert(b + 1)
                    gate(b, 1, first)
                    if not last:
                        divide(b + 1, 0)
                    add(b, 1, first)

                nc.vector.memset(inv_sums[:, :, :], 0.0).then_inc(rows_zero, 1)
                dve.wait_ge(rows_zero, 1)
                invert(0)
                divide(0, 0)
                body(0, True, False)
                with dve.Fori(1, B - 1) as b:
                    body(b, False, False)
                body(B - 1, False, True)

            @block.tensor
            def _(pe):
                def spread_sums(b, c, first):
                    pe.wait_ge(inverted, b + 1)
                    if not first:
                        pe.wait_ge(divided, 4 * b + 2 * c)
                    for f in range(KD):
                        nc.tensor.matmul(ps_i[f][:, :], spread[:, f, c, :], inv_sums[:, bass.ds(b % 2, 1), :].rearrange("p o n -> p (o n)"),
                                         start=True, stop=True).then_inc(spread_done, 1)

                def project(b, c, first):
                    pe.wait_ge(divided, 4 * b + 2 * c + 2)
                    if not first:
                        pe.wait_ge(gated_done, 4 * b + 2 * c)
                    for m in range(KD):
                        for f in range(KD):
                            mm = nc.tensor.matmul(ps_s[m][:, :], w_out[:, f, m * P:(m + 1) * P], o_n[:, c, f, :], start=(f == 0), stop=(f == KD - 1))
                        mm.then_inc(s_ready, 1)

                def turn(b, c, first):
                    pe.wait_ge(gated_done, 4 * b + 2 * c + 2)
                    if not first:
                        pe.wait_ge(summed, 4 * b + 2 * c - 2)
                    for m in range(2):
                        for t in range(2):
                            for k in range(KD):
                                s = slice((2 * m + t) * P, (2 * m + t + 1) * P)
                                mm = nc.tensor.transpose(ps_t[c][m][:, t * D + k * P:t * D + (k + 1) * P], gated[:, c, k, s], ident[:, :])
                        mm.then_inc(turned_back, 1)

                def body(b, first, last):
                    project(b, 0, first)
                    spread_sums(b, 1, False)
                    turn(b, 0, first)
                    project(b, 1, False)
                    if not last:
                        spread_sums(b + 1, 0, False)
                    turn(b, 1, first)

                pe.wait_ge(consts_in, 48)
                spread_sums(0, 0, True)
                body(0, True, False)
                with pe.Fori(1, B - 1) as b:
                    body(b, False, False)
                body(B - 1, False, True)


def rope_table():
    half = G_DIM // 2
    freq = np.float32(1.0) / np.float32(10000.0) ** (np.arange(half, dtype=np.float32) / np.float32(half))
    angle = np.arange(L, dtype=np.float32)[:, None] * freq[None, :]
    c, s = np.cos(angle.astype(np.float64)), np.sin(angle.astype(np.float64))
    return np.stack([np.concatenate([c, c], 1), np.concatenate([-s, s], 1)], 1).astype(np.float32)


def xpos_table():
    idx = np.arange(0, HDIM, 2, dtype=np.float32)
    freq = np.float32(1.0) / np.float32(10000.0) ** (idx / np.float32(HDIM))
    angle = (np.arange(L, dtype=np.float32)[:, None] * freq[None, :]).astype(np.float64)
    base = (idx.astype(np.float64) + 0.4 * HDIM) / (1.4 * HDIM)
    scale = base[None, :] ** ((np.arange(L) - L // 2) / (P / 2.0))[:, None]
    c, s = np.cos(angle), np.sin(angle)
    cat = lambda a, b: np.concatenate([a, b], 1)
    return np.stack([cat(c * scale, c * scale) * QK_SCALE, cat(-s * scale, s * scale) * QK_SCALE,
                     cat(c / scale, c / scale), cat(-s / scale, s / scale)], 1).astype(np.float32)


def window_masks():
    r, c = np.arange(P)[:, None], np.arange(P)[None, :]
    return np.stack([np.full((P, P), MASKED), np.where(c >= r, 0.0, MASKED), np.where(c <= r, 0.0, MASKED)]).astype(np.float32)


def sum_spread():
    f, c, m = np.meshgrid(np.arange(KD), np.arange(2), np.arange(P), indexing="ij")
    row = 2 * (P // G_DIM) * f + 2 * (m // G_DIM) + c
    return (np.arange(P)[:, None, None, None] == row[None]).astype(np.float32)


def gated_attention_kernel(nc, x, w_qkv_t, w_out_t, wqkv, q_scale, k_scale, wo, ln_g, ln_b, w1, b1, w2, b2,
                           rope, xpos, masks, ident, spread, out):
    with ExitStack() as ctx:
        internal = lambda n, s: nc.dram_tensor(n, s, F32, kind="Internal").ap()
        xnt = ctx.enter_context(nc.sbuf_tensor("xnt", [P, KD, CHUNKS, 1 + CH], F32))
        qs_dram = internal("qs", (2 * B, 8, G_DIM, 2, L))
        ks_dram = internal("ks", (2 * B, 8, G_DIM, 2, L))
        v_dram = internal("v", (2 * B, TILES, P, P))
        o_dram = internal("o", (UNITS, P, CH))
        stored = [ctx.enter_context(nc.semaphore(f"stored{c}")) for c in range(2)]
        with ExitStack() as layers:
            wt = Weights(layers, nc, wqkv, wo, ln_g, ln_b, w1, b1, w2, b2, masks, ident)
            prepare_tokens(nc, wt, x, w_qkv_t, rope, ident, xnt, qs_dram, ks_dram, v_dram, stored)
            global_attention(nc, wt, ident, qs_dram, ks_dram, v_dram, stored, o_dram)
            local_layers(nc, wt, xpos, q_scale, k_scale, xnt)
        combine(nc, x, w_out_t, ident, spread, xnt, o_dram, out)


_INS = ['L0_attn_x', 'L0_attn_w_qkv', 'L0_attn_w_out', 'L0_ffn_wqkv', 'L0_ffn_q_scale', 'L0_ffn_k_scale', 'L0_ffn_wo', 'L0_ffn_ln_g',
        'L0_ffn_ln_b', 'L0_ffn_w1', 'L0_ffn_b1', 'L0_ffn_w2', 'L0_ffn_b2']
_TURNED = ('L0_attn_w_qkv', 'L0_attn_w_out')
_OUTS = [((4, 1024, 256), 'float32')]


def kernel(**inputs):
    import numpy as _np
    import concourse.bacc as _bacc
    from concourse import mybir as _mybir
    from concourse.bass_utils import run_bass_kernel_spmd as _run

    nc = _bacc.Bacc("TRN2", target_bir_lowering=False, num_devices=1)
    arrays, args = {}, []
    tables = {'rope': rope_table(), 'xpos': xpos_table(), 'masks': window_masks(), 'ident': _np.eye(P, dtype=_np.float32),
              'spread': sum_spread()}
    laid_out = [(n, _np.ascontiguousarray(_np.asarray(inputs[n]).T if n in _TURNED else inputs[n])) for n in _INS] + list(tables.items())
    for name, a in laid_out:
        arrays[f"in_{name}_dram"] = a
        args.append(nc.dram_tensor(f"in_{name}_dram", a.shape, _mybir.dt.from_np(a.dtype), kind="ExternalInput").ap())
    for i, (shape, dtype) in enumerate(_OUTS):
        dt = _mybir.dt.from_np(_np.dtype(dtype))
        args.append(nc.dram_tensor(f"out_{i}_dram", shape, dt, kind="ExternalOutput").ap())
    gated_attention_kernel(nc, *args)
    r = _run(nc, [arrays], core_ids=[0])
    got = tuple(r.results[0][f"out_{i}_dram"] for i in range(len(_OUTS)))
    return got[0]
```
